# Optimizing a Trainium2 kernel written in Bass

```python
import numpy as np
import jax
import jax.numpy as jnp

def _softmax(x, axis=-1):
    return jax.nn.softmax(x, axis=axis)

def _gelu(x):
    return jax.nn.gelu(x, approximate=True)

def _silu(x):
    return jax.nn.silu(x)

def _sigmoid(x):
    return jax.nn.sigmoid(x)

def _layernorm(x, axis=-1, eps=1e-05):
    m = jnp.mean(x, axis=axis, keepdims=True)
    v = jnp.var(x, axis=axis, keepdims=True)
    return (x - m) / jnp.sqrt(v + eps)

def _scatter_add(tgt, idx, src, axis=0):
    return tgt.at[idx].add(src)

def _segment_sum(src, seg, n):
    return jax.ops.segment_sum(src, seg, n)
kernel_name = 'mk_flamingo_gated_d2_seqx_r8_3512eb'

def setup_inputs(seed: int=0):
    np.random.seed(seed)
    _w = jnp.asarray

    def _rec_inputs():
        import jax
        import jax.numpy as jnp
        _rk = jax.random.key(seed)
        x = 7.22e-05 + 1 * jax.random.normal(jax.random.fold_in(_rk, 1), (16, 128, 128), jnp.float32)
        _lenS = 128 - jax.random.randint(jax.random.fold_in(_rk, 7), (16,), 0, max(1, 128 // 4) + 1, jnp.int32)
        _lenS2 = 128 - jax.random.randint(jax.random.fold_in(_rk, 8), (16,), 0, max(1, 128 // 4) + 1, jnp.int32)
        _ctx_1024P = jax.random.normal(jax.random.fold_in(_rk, 11), (16, 16, 128), jnp.float32)
        _ctx_1024c = jax.random.dirichlet(jax.random.fold_in(_rk, 511), 0.3 * jnp.ones((16,), jnp.float32), (16, 128))
        _ctx_1024t = jnp.einsum('bsk,bkd->bsd', _ctx_1024c, _ctx_1024P)
        _ctx_1024t = _ctx_1024t * jax.lax.rsqrt(jnp.mean(jnp.square(_ctx_1024t)) + 1e-12) * 0.953939
        ctx_1024 = 4.13588e-05 + 0.999923 * (_ctx_1024t + 0.3 * jax.random.normal(jax.random.fold_in(_rk, 611), (16, 128, 128), jnp.float32))
        _g = jax.random.normal(jax.random.fold_in(_rk, 9001), (2, 2), jnp.float32)
        _g = jnp.sign(_g) * jnp.maximum(jnp.abs(_g), 1.0) + (_g == 0) * 1.0
        g_xattn = _g[0]
        g_ffn = _g[1]
        return (x, ctx_1024, g_xattn, g_ffn)
    x, ctx_1024, g_xattn, g_ffn = _rec_inputs()

    def _L0_xattn_setup():
        import jax, jax.numpy as jnp
        import numpy as np
        D_MODEL = 128
        N_HEAD = 16
        N_D = D_MODEL // N_HEAD
        key = jax.random.key(seed)
        ks = jax.random.split(key, 11)
        B, S, D = (4, 256, D_MODEL)
        scale = 1.0 / np.sqrt(D)
        return {'q': jax.random.normal(ks[0], (B, S, D), jnp.float32), 'k': jax.random.normal(ks[1], (B, S, D), jnp.float32), 'v': jax.random.normal(ks[2], (B, S, D), jnp.float32), 'w_q': jax.random.normal(ks[3], (D, D), jnp.float32) * scale, 'b_q': jnp.zeros((D,), jnp.float32), 'w_k': jax.random.normal(ks[4], (D, D), jnp.float32) * scale, 'b_k': jnp.zeros((D,), jnp.float32), 'w_v': jax.random.normal(ks[5], (D, D), jnp.float32) * scale, 'b_v': jnp.zeros((D,), jnp.float32), 'w_o': jax.random.normal(ks[6], (D, D), jnp.float32) * scale, 'b_o': jnp.zeros((D,), jnp.float32)}
    _L0_xattn_all = _L0_xattn_setup()
    _L0_xattn_in = {k: v for k, v in _L0_xattn_all.items() if k in ('w_q', 'b_q', 'w_k', 'b_k', 'w_v', 'b_v', 'w_o', 'b_o')}
    del _L0_xattn_all

    def _L0_ffn_setup():
        import jax, jax.numpy as jnp
        import numpy as np
        TOP_K = 8
        CAPACITY = 64

        def _silu(x):
            return x * jax.nn.sigmoid(x)
        key = jax.random.key(seed)
        ks = jax.random.split(key, 7)
        B, S, H, E, I, Is = (2, 128, 128, 64, 64, 256)
        s = 0.05
        return {'hidden_states': jax.random.normal(ks[0], (B, S, H), jnp.float32), 'gate_w': jax.random.normal(ks[1], (H, E), jnp.float32) * s, 'shared_gate_w': jax.random.normal(ks[2], (H, 1), jnp.float32) * s, 'shared_gate_up_w': jax.random.normal(ks[3], (H, 2 * Is), jnp.float32) * s, 'shared_down_w': jax.random.normal(ks[4], (Is, H), jnp.float32) * s, 'expert_gate_up_w': jax.random.normal(ks[5], (E, H, 2 * I), jnp.float32) * s, 'expert_down_w': jax.random.normal(ks[6], (E, I, H), jnp.float32) * s}
    _L0_ffn_all = _L0_ffn_setup()
    _L0_ffn_in = {k: v for k, v in _L0_ffn_all.items() if k in ('gate_w', 'shared_gate_w', 'shared_gate_up_w', 'shared_down_w', 'expert_gate_up_w', 'expert_down_w')}
    del _L0_ffn_all

    def _L1_xattn_setup():
        import jax, jax.numpy as jnp
        import numpy as np
        D_MODEL = 128
        NUM_HEADS = 16
        HEAD_DIM = D_MODEL // NUM_HEADS

        def _split_heads(x):
            B, S, _ = x.shape
            return x.reshape(B, S, NUM_HEADS, HEAD_DIM).transpose(0, 2, 1, 3)
        key = jax.random.key(seed)
        ks = jax.random.split(key, 11)
        B, S = (2, 256)
        scale = 1.0 / np.sqrt(D_MODEL)
        inp = {'query': jax.random.normal(ks[0], (B, S, D_MODEL), jnp.float32), 'key': jax.random.normal(ks[1], (B, S, D_MODEL), jnp.float32), 'value': jax.random.normal(ks[2], (B, S, D_MODEL), jnp.float32), 'Wq': jax.random.normal(ks[3], (D_MODEL, D_MODEL), jnp.float32) * scale, 'bq': jnp.zeros((D_MODEL,), jnp.float32), 'Wk': jax.random.normal(ks[4], (D_MODEL, D_MODEL), jnp.float32) * scale, 'bk': jnp.zeros((D_MODEL,), jnp.float32), 'Wv': jax.random.normal(ks[5], (D_MODEL, D_MODEL), jnp.float32) * scale, 'bv': jnp.zeros((D_MODEL,), jnp.float32), 'Wo': jax.random.normal(ks[6], (D_MODEL, D_MODEL), jnp.float32) * scale, 'bo': jnp.zeros((D_MODEL,), jnp.float32)}
        return inp
    _L1_xattn_all = _L1_xattn_setup()
    _L1_xattn_in = {k: v for k, v in _L1_xattn_all.items() if k in ('Wq', 'bq', 'Wk', 'bk', 'Wv', 'bv', 'Wo', 'bo')}
    del _L1_xattn_all

    def _L1_ffn_setup():
        import jax, jax.numpy as jnp
        import numpy as np
        key = jax.random.key(seed)
        k1, k2, k3, k4, k5 = jax.random.split(key, 5)
        d_in, d_out, r = (128, 128, 32)
        x = jax.random.normal(k1, (8, 1024, d_in), dtype=jnp.float32)
        W = jax.random.normal(k2, (d_out, d_in), dtype=jnp.float32) * (1.0 / np.sqrt(d_in))
        b = jax.random.normal(k3, (d_out,), dtype=jnp.float32) * 0.01
        V_r = jax.random.normal(k4, (d_in, r), dtype=jnp.float32) * (1.0 / np.sqrt(d_in))
        C = jax.random.normal(k5, (d_out, r), dtype=jnp.float32) * (1.0 / np.sqrt(r))
        return {'x': x, 'W': W, 'b': b, 'V_r': V_r, 'C': C}
    _L1_ffn_all = _L1_ffn_setup()
    _L1_ffn_in = {k: v for k, v in _L1_ffn_all.items() if k in ('W', 'b', 'V_r', 'C')}
    del _L1_ffn_all
    return {'x': x, 'ctx_1024': ctx_1024, 'g_xattn': g_xattn, 'g_ffn': g_ffn, 'L0_xattn_w_q': _L0_xattn_in['w_q'], 'L0_xattn_b_q': _L0_xattn_in['b_q'], 'L0_xattn_w_k': _L0_xattn_in['w_k'], 'L0_xattn_b_k': _L0_xattn_in['b_k'], 'L0_xattn_w_v': _L0_xattn_in['w_v'], 'L0_xattn_b_v': _L0_xattn_in['b_v'], 'L0_xattn_w_o': _L0_xattn_in['w_o'], 'L0_xattn_b_o': _L0_xattn_in['b_o'], 'L0_ffn_gate_w': _L0_ffn_in['gate_w'], 'L0_ffn_shared_gate_w': _L0_ffn_in['shared_gate_w'], 'L0_ffn_shared_gate_up_w': _L0_ffn_in['shared_gate_up_w'], 'L0_ffn_shared_down_w': _L0_ffn_in['shared_down_w'], 'L0_ffn_expert_gate_up_w': _L0_ffn_in['expert_gate_up_w'], 'L0_ffn_expert_down_w': _L0_ffn_in['expert_down_w'], 'L1_xattn_Wq': _L1_xattn_in['Wq'], 'L1_xattn_bq': _L1_xattn_in['bq'], 'L1_xattn_Wk': _L1_xattn_in['Wk'], 'L1_xattn_bk': _L1_xattn_in['bk'], 'L1_xattn_Wv': _L1_xattn_in['Wv'], 'L1_xattn_bv': _L1_xattn_in['bv'], 'L1_xattn_Wo': _L1_xattn_in['Wo'], 'L1_xattn_bo': _L1_xattn_in['bo'], 'L1_ffn_W': _L1_ffn_in['W'], 'L1_ffn_b': _L1_ffn_in['b'], 'L1_ffn_V_r': _L1_ffn_in['V_r'], 'L1_ffn_C': _L1_ffn_in['C']}

def reference(x, ctx_1024, g_xattn, g_ffn, L0_xattn_w_q, L0_xattn_b_q, L0_xattn_w_k, L0_xattn_b_k, L0_xattn_w_v, L0_xattn_b_v, L0_xattn_w_o, L0_xattn_b_o, L0_ffn_gate_w, L0_ffn_shared_gate_w, L0_ffn_shared_gate_up_w, L0_ffn_shared_down_w, L0_ffn_expert_gate_up_w, L0_ffn_expert_down_w, L1_xattn_Wq, L1_xattn_bq, L1_xattn_Wk, L1_xattn_bk, L1_xattn_Wv, L1_xattn_bv, L1_xattn_Wo, L1_xattn_bo, L1_ffn_W, L1_ffn_b, L1_ffn_V_r, L1_ffn_C):
    import jax
    import jax.numpy as jnp

    def _L0_xattn_ref(q, k, v, w_q, b_q, w_k, b_k, w_v, b_v, w_o, b_o):
        import jax, jax.numpy as jnp
        import numpy as np
        D_MODEL = 128
        N_HEAD = 16
        N_D = D_MODEL // N_HEAD
        B, S, D = q.shape
        H, Dh = (N_HEAD, N_D)
        qh = (q @ w_q + b_q).reshape(B, S, H, Dh).transpose(0, 2, 1, 3)
        kh = (k @ w_k + b_k).reshape(B, S, H, Dh).transpose(0, 2, 1, 3)
        vh = (v @ w_v + b_v).reshape(B, S, H, Dh).transpose(0, 2, 1, 3)
        score = jnp.einsum('bhqd,bhkd->bhqk', qh, kh) / jnp.sqrt(jnp.float32(Dh))
        attn = jax.nn.softmax(score, axis=-1)
        out = jnp.einsum('bhqk,bhkd->bhqd', attn, vh)
        out = out.transpose(0, 2, 1, 3).reshape(B, S, D)
        return out @ w_o + b_o

    def _L0_ffn_ref(hidden_states, gate_w, shared_gate_w, shared_gate_up_w, shared_down_w, expert_gate_up_w, expert_down_w):
        import jax, jax.numpy as jnp
        import numpy as np
        TOP_K = 8
        CAPACITY = 64

        def _silu(x):
            return x * jax.nn.sigmoid(x)
        B, S, H = hidden_states.shape
        x = hidden_states.reshape(-1, H)
        T = x.shape[0]
        E = gate_w.shape[1]
        Is = shared_gate_up_w.shape[1] // 2
        I = expert_gate_up_w.shape[2] // 2
        gu = x @ shared_gate_up_w
        shared = _silu(gu[:, :Is]) * gu[:, Is:] @ shared_down_w
        shared = shared * jax.nn.sigmoid(x @ shared_gate_w)
        logits = x @ gate_w
        probs = jax.nn.softmax(logits.astype(jnp.float32), axis=-1)
        w, idx = jax.lax.top_k(probs, TOP_K)
        w = (w / jnp.sum(w, axis=-1, keepdims=True)).astype(x.dtype)
        e_flat = idx.reshape(-1)
        w_flat = w.reshape(-1)
        A = e_flat.shape[0]
        tok = jnp.arange(A) // TOP_K
        onehot = jax.nn.one_hot(e_flat, E, dtype=jnp.int32)
        pos = jnp.take_along_axis(jnp.cumsum(onehot, axis=0) - 1, e_flat[:, None], axis=1)[:, 0]
        slot = jnp.minimum(pos, CAPACITY)
        buf = jnp.zeros((E, CAPACITY + 1, H), x.dtype).at[e_flat, slot].set(x[tok])
        gu_e = jnp.einsum('ech,ehf->ecf', buf, expert_gate_up_w)
        act = _silu(gu_e[..., :I]) * gu_e[..., I:]
        out_e = jnp.einsum('eci,eih->ech', act, expert_down_w)
        y = out_e[e_flat, slot] * w_flat[:, None]
        y = jnp.where((pos < CAPACITY)[:, None], y, jnp.zeros_like(y))
        y = y.reshape(T, TOP_K, H).sum(axis=1)
        return (y + shared).reshape(B, S, H)

    def _L1_xattn_ref(query, key, value, Wq, bq, Wk, bk, Wv, bv, Wo, bo):
        import jax, jax.numpy as jnp
        import numpy as np
        D_MODEL = 128
        NUM_HEADS = 16
        HEAD_DIM = D_MODEL // NUM_HEADS

        def _split_heads(x):
            B, S, _ = x.shape
            return x.reshape(B, S, NUM_HEADS, HEAD_DIM).transpose(0, 2, 1, 3)
        q = _split_heads(query @ Wq.T + bq)
        k = _split_heads(key @ Wk.T + bk)
        v = _split_heads(value @ Wv.T + bv)
        scores = jnp.einsum('bhqd,bhkd->bhqk', q, k) / jnp.sqrt(jnp.asarray(HEAD_DIM, q.dtype))
        probs = jax.nn.softmax(scores, axis=-1)
        ctx = jnp.einsum('bhqk,bhkd->bhqd', probs, v)
        B, H, S, Dh = ctx.shape
        ctx = ctx.transpose(0, 2, 1, 3).reshape(B, S, H * Dh)
        return ctx @ Wo.T + bo

    def _L1_ffn_ref(x, W, b, V_r, C):
        import jax, jax.numpy as jnp
        import numpy as np
        base = jnp.einsum('bsd,od->bso', x, W) + b
        correction = jnp.einsum('bsr,or->bso', jnp.einsum('bsd,dr->bsr', x, V_r), C)
        return base + correction
    x = x + jnp.tanh(g_xattn[0]) * _L0_xattn_ref(_layernorm(x, axis=-1), ctx_1024, ctx_1024, L0_xattn_w_q, L0_xattn_b_q, L0_xattn_w_k, L0_xattn_b_k, L0_xattn_w_v, L0_xattn_b_v, L0_xattn_w_o, L0_xattn_b_o)
    x = x + jnp.tanh(g_ffn[0]) * _L0_ffn_ref(_layernorm(x, axis=-1), L0_ffn_gate_w, L0_ffn_shared_gate_w, L0_ffn_shared_gate_up_w, L0_ffn_shared_down_w, L0_ffn_expert_gate_up_w, L0_ffn_expert_down_w)
    x = x + jnp.tanh(g_xattn[1]) * _L1_xattn_ref(_layernorm(x, axis=-1), ctx_1024, ctx_1024, L1_xattn_Wq, L1_xattn_bq, L1_xattn_Wk, L1_xattn_bk, L1_xattn_Wv, L1_xattn_bv, L1_xattn_Wo, L1_xattn_bo)
    x = x + jnp.tanh(g_ffn[1]) * _L1_ffn_ref(_layernorm(x, axis=-1), L1_ffn_W, L1_ffn_b, L1_ffn_V_r, L1_ffn_C)
    return x

_drawn_inputs = setup_inputs


def setup_inputs(seed=0):
    import zlib

    import numpy as np

    out = dict(_drawn_inputs(seed))
    spreads = {'g_ffn': (-1.0, 0.6),
     'L0_xattn_b_q': (0.0, 0.511),
     'L0_xattn_b_k': (0.0, 2.0),
     'L0_xattn_b_v': (0.0, 0.1),
     'L0_xattn_b_o': (0.0, 0.1),
     'L1_xattn_bq': (0.0, 2.0),
     'L1_xattn_bk': (0.0, 2.0),
     'L1_xattn_bv': (0.0, 0.659),
     'L1_xattn_bo': (0.0, 0.483)}
    factors = {'L0_ffn_gate_w': 7.401,
     'L0_ffn_shared_gate_w': 39.648,
     'L0_ffn_expert_gate_up_w': 7.01,
     'L0_ffn_expert_down_w': 7.072,
     'L1_ffn_b': 54.858,
     'L0_ffn_shared_gate_up_w': 5.46,
     'L0_ffn_shared_down_w': 5.461,
     'L1_xattn_Wq': 3.305}
    for name, (base, spread) in spreads.items():
        noise = np.random.default_rng([zlib.crc32(name.encode()), seed]).standard_normal(out[name].shape)
        drawn = base * np.exp(spread * noise) if base else spread * noise
        out[name] = jnp.asarray(drawn.astype(out[name].dtype))
    for name, factor in factors.items():
        out[name] = (out[name] * factor).astype(out[name].dtype)
    return out
```

```python
from contextlib import ExitStack

import numpy as np
import concourse.bass as bass
from concourse import mybir

F32 = mybir.dt.float32
F16 = mybir.dt.float16
BF16 = mybir.dt.bfloat16
I32 = mybir.dt.int32
ALU = mybir.AluOpType
ACT = mybir.ActivationFunctionType
AXX = mybir.AxisListType.X

P = 128
NB = 16
D = 128
T = NB * P
HEADS, DH = 16, 8
G = 4
J = 4
SCALE = float(DH) ** -0.5
EXPERTS, TOPK, CAP = 64, 8, 64
FE = 64
FS = 256
SLOTS = EXPERTS * CAP
EG = 16
NG = EXPERTS // EG
DIG = 8
CH = NG * DIG
ROW = 256
EPS = 1e-5
RSQRT_SEED = float(0x5F3759DF)

C_ID, C_TRI, C_QUAD, C_KLO, C_QLO, C_SPLIT, C_OWN, C_DIG, C_TOK, C_TOK8 = 0, 128, 256, 260, 261, 262, 265, 281, 289, 305
NCONST = 321


def shape_constants():
    c = np.zeros((P, NCONST), np.float32)
    p = np.arange(P)
    c[:, C_ID:C_ID + P] = np.eye(P)
    c[:, C_TRI:C_TRI + P] = p[:, None] < p[None, :]
    for j in range(J):
        c[:, C_QUAD + j] = p // 32 == j
    c[:, C_KLO] = (p % 32) // 8 >= 2
    c[:, C_QLO] = (p // 8) % 2 == 1
    c[:, C_OWN:C_OWN + EG] = p[:, None] // DIG == np.arange(EG)[None, :]
    c[:, C_DIG:C_DIG + DIG] = np.arange(DIG)
    c[:, C_TOK:C_TOK + NB] = p[:, None] + P * np.arange(NB)[None, :] + 1
    c[:, C_TOK8:C_TOK8 + NB] = TOPK * (p[:, None] + P * np.arange(NB)[None, :])
    return c


def program(nc, x, ctx, consts, wrep, wv, wo, brep, brow, bvcol, gates, gate_w, sgu, sdown, egu, edown,
            ffn_wt, ffn_vt, ffn_ct, out):
    with ExitStack() as es:
        def sb(name, shape, dt=F32):
            return es.enter_context(nc.sbuf_tensor(name, shape, dt))

        def sem(name):
            return es.enter_context(nc.semaphore(name))

        bank = [es.enter_context(nc.psum_tensor(f"bank{i}", [P, 512], F32)) for i in range(8)]
        table = nc.dram_tensor("token_table", (T + 1, ROW), F32).ap()
        parts = nc.dram_tensor("expert_parts", (T * TOPK, D), F32).ap()

        X = sb("X", [P, NB, D])
        CON = sb("CON", [P, NCONST])
        WREP = sb("WREP", [P, 2, 2, 512])
        WV = sb("WV", [P, 2, D])
        WO = sb("WO", [P, 2, D])
        NBR = 2 * 2 * 512 + 3 * D
        BIG = sb("BIG", [P, 8192])
        BR = BIG[:, 0:NBR]
        BR_rest = BIG[:, NBR:2 * NBR]
        BR_part = BIG[:, 2 * NBR:3 * NBR].bitcast(BF16).rearrange("p (k n) -> p k n", k=2)
        B3 = sb("B3", [P, NBR], BF16)
        BVC = sb("BVC", [P, 2])
        GT = sb("GT", [P, 4])
        TH = sb("TH", [P, 4])
        ones_b = sb("ones_b", [P, P], BF16)
        negid_b = sb("negid_b", [P, P], BF16)
        tri_b = sb("tri_b", [P, P], BF16)
        ones_d = sb("ones_d", [P, G, 32])
        ident = CON[:, C_ID:C_ID + P]

        CXB = sb("CXB", [P, 2, D])
        XN = sb("XN", [P, 2, D])
        XC = sb("XC", [P, 2, 2 * D])
        LO = sb("LO", [P, 2, 512], F16)
        QS = sb("QS", [P, 1, 512], F16)
        STORE_A = sb("STORE_A", [P, 2048])
        STORE_B = sb("STORE_B", [P, 2048])
        QM = STORE_A[:, :].bitcast(F16).rearrange("p (b g j q) -> p b g j q", b=2, g=G, j=J)
        KS = sb("KS", [P, 2, G, P], F16)
        VM = sb("VM", [P, 2, G, D])
        NM = sb("NM", [P, G, J], BF16)
        E = STORE_B[:, :].rearrange("p (g n) -> p g n", g=G)
        RD = sb("RD", [P, D])
        CN = sb("CN", [P, 2, D])
        STATS = sb("STATS", [P, 2, 6])
        MV = sb("MV", [P, NB, 2])
        MV_now = sb("MV_now", [P, 2])
        RS3 = sb("RS3", [P, NB, 1])
        RS = RS3[:, :, 0]
        VE = sb("VE", [P, NB])
        NW = sb("NW", [P, 2, NB])

        TB = sb("TB", [P, NB, ROW])
        XNT = sb("XNT", [P, T])
        GW = sb("GW", [P, EXPERTS + 1])
        SGU = sb("SGU", [P, 2 * FS])
        SD = sb("SD", [P, 2, D])
        EGU = sb("EGU", [P, EXPERTS, 2 * FE])
        ED = sb("ED", [P, EXPERTS // 2, D])
        ROUTE = sb("ROUTE", [P, 4, NB, EXPERTS])
        LG = ROUTE[:, 0, :, :]
        LM = sb("LM", [P, NB, EXPERTS])
        MASK = sb("MASK", [P, NB, EXPERTS], BF16)
        POS = ROUTE[:, 1, :, :]
        KEPT = ROUTE[:, 2, :, :]
        HI_D = LM[:, :, :].bitcast(I32)
        LO_D = ROUTE[:, 3, :, :].bitcast(I32)
        TOP = sb("TOP", [P, NB, 8])
        SUMS = sb("SUMS", [P, NB])
        SG = sb("SG", [P, NB])
        HOT = BIG[:, :].bitcast(F16).rearrange("p (w n e s) -> p w n e s", w=2, n=NB, s=DIG)
        GA = BIG[:, :].rearrange("p (c r) -> p c r", r=ROW)
        IDX = sb("IDX", [P, NG, EG, DIG])
        IDF = sb("IDF", [P, CH])
        IDI = sb("IDI", [P, CH], I32)
        OWNP = sb("OWNP", [P, DIG, 2, EG])
        WD = sb("WD", [P, CH, 2])
        DST = sb("DST", [P, CH], I32)
        XG = STORE_A[:, :].rearrange("p (b s n) -> p b s n", b=2, s=DIG)
        TG = sb("TG", [P, 512])
        H1 = sb("H1", [P, 512])
        AH = sb("AH", [P, EG // 2, CAP])
        YT = sb("YT", [P, DIG, EG // 2, 2, DIG])
        YS = ROUTE[:, :, :, :].rearrange("p a n e -> p (a n e)").rearrange("p (c d) -> p c d", d=D)
        TS_ = STORE_B[:, 0:1024].rearrange("p (c n) -> p c n", c=2)
        HS = STORE_B[:, 1024:2048].rearrange("p (c n) -> p c n", c=2)
        SH = sb("SH", [P, 4, D])
        PART = YS[:, :, :].rearrange("p (b k) d -> p b (k d)", b=4)
        ysum = sb("ysum", [P, 2, D])
        ZERO = PART[:, :, :].rearrange("p a b -> p (a b)")
        WF = sb("WF", [P, D])
        FWT = sb("FWT", [P, D])
        FVC = sb("FVC", [32, 2, D])
        zrow = sb("zrow", [1, ROW])
        OT = EGU[:, 0:8, :].rearrange("p (b n) d -> p b n d", b=2)

        ld_x, ld_con, ld_w, ld_b, ld_moe, ld_ffn = (sem(n) for n in ("ld_x", "ld_con", "ld_w", "ld_b", "ld_moe", "ld_ffn"))
        cx_in = [sem("cx_in0"), sem("cx_in1")]
        const_set, dve_set, bias_mm, bias_set = sem("const_set"), sem("dve_set"), sem("bias_mm"), sem("bias_set")
        gates_done = sem("gates_done")
        max_mm, max_got, score_mm, exp_done, pv_mm = (sem(n) for n in ("max_mm", "max_got", "score_mm", "exp_done", "pv_mm"))
        xn_done, tr_mm, xc_done = sem("xn_done"), sem("tr_mm"), sem("xc_done")
        q_mm, q_low, q_split, q_masked = sem("q_mm"), sem("q_low"), sem("q_split"), sem("q_masked")
        k_mm, k_low, k_split = sem("k_mm"), sem("k_low"), sem("k_split")
        v_mm, v_done = sem("v_mm"), sem("v_done")
        recip_done, ctx_done, o_mm, x_done, stat_done, mv_done = (
            sem(n) for n in ("recip_done", "ctx_done", "o_mm", "x_done", "stat_done", "mv_done"))
        aggr_done, rs_step = sem("aggr_done"), sem("rs_step")
        zero_set, zero_st = sem("zero_set"), sem("zero_st")
        m_xn, m_tr, m_xt = sem("m_xn"), sem("m_tr"), sem("m_xt")
        m_lg, m_lgc, m_sub, m_exp, m_step, m_mask = (sem(n) for n in ("m_lg", "m_lgc", "m_sub", "m_exp", "m_step", "m_mask"))
        m_sg = sem("m_sg")
        m_pos, m_hot, m_ids, m_idx = sem("m_pos"), sem("m_hot"), sem("m_ids"), sem("m_idx")
        m_tab, m_tabw = sem("m_tab"), sem("m_tabw")
        g_in = [sem(f"g_in{g}") for g in range(NG)]
        g_tr, g_xt, g_up, g_tanh, g_h1, g_act, g_dn, g_yt, g_bk, g_ys, g_wd, g_own = (
            sem(n) for n in ("g_tr", "g_xt", "g_up", "g_tanh", "g_h1", "g_act", "g_dn", "g_yt", "g_bk", "g_ys", "g_wd", "g_own"))
        y_st = sem("y_st")
        h_mm, h_tanh, h_h1, h_act, h_dn, h_sh, h_x = (sem(n) for n in ("h_mm", "h_tanh", "h_h1", "h_act", "h_dn", "h_sh", "h_x"))
        p_in = [sem(f"p_in{i}") for i in range(4)]
        p_sum, p_x, p_st, p_mv = sem("p_sum"), sem("p_x"), sem("p_st"), sem("p_mv")
        f_w, f_wf, f_xn, f_tr, f_xt, f_mm, f_x = (sem(n) for n in ("f_w", "f_wf", "f_xn", "f_tr", "f_xt", "f_mm", "f_x"))
        f_st = [sem("f_st0"), sem("f_st1")]

        x_v = x.rearrange("(n p) d -> p n d", p=P)
        ctx_v = ctx.rearrange("(n p) d -> n p d", p=P)
        out_v = out.rearrange("(m n p) d -> m p n d", p=P, n=4)
        parts_z = parts.rearrange("(a r) d -> a (r d)", a=P)
        parts_v = parts.rearrange("(n p k) d -> n p (k d)", p=P, k=TOPK)

        def wait(eng, semaphore, value):
            if isinstance(value, int) and value <= 0:
                return
            eng.wait_ge(semaphore, value)

        def over_batches(eng, layer, step):
            def pair(i, last):
                for p in range(2):
                    step(i, p, NB * layer + 2 * i + p, last)
            pair(0, False)
            with eng.Fori(1, NB // 2 - 1) as i:
                pair(i, False)
            pair(NB // 2 - 1, True)

        block = es.enter_context(nc.Block())

        @block.sync
        def _(sp):
            sp.dma_start(X[:, :, :], x_v).then_inc(ld_x, 16)
            sp.dma_start(CON[:, :], consts).then_inc(ld_con, 16)
            sp.dma_start(GT[:, :], gates.rearrange("(a n) -> a n", a=1).to_broadcast([P, 4])).then_inc(ld_con, 16)

            def ctx_tile(i, p, B, last):
                wait(sp, tr_mm, B - 1)
                b = i * 2 + p
                sp.dma_start(CXB[:, p, :], ctx_v[b, :, :]).then_inc(cx_in[p], 16)

            sp.dma_start(WREP[:, :, :, :], wrep).then_inc(ld_w, 16)
            sp.dma_start(WV[:, :, :], wv).then_inc(ld_w, 16)
            sp.dma_start(WO[:, :, :], wo).then_inc(ld_w, 16)
            sp.dma_start(BR[:, 0:2048], brep.rearrange("(a n) -> a n", a=1).to_broadcast([P, 2048])).then_inc(ld_b, 16)
            sp.dma_start(BR[:, 2048:NBR], brow.rearrange("(a n) -> a n", a=1).to_broadcast([P, 3 * D])).then_inc(ld_b, 16)
            sp.dma_start(BVC[:, :], bvcol).then_inc(ld_b, 16)
            for p in range(2):
                ctx_tile(0, p, p, False)
            sp.dma_start(GW[:, :], gate_w).then_inc(ld_moe, 16)
            sp.dma_start(SGU[:, :], sgu).then_inc(ld_moe, 16)
            sp.dma_start(SD[:, :, :], sdown.rearrange("(c p) d -> p c d", p=P)).then_inc(ld_moe, 16)
            sp.dma_start(EGU[:, :, :], egu.rearrange("e h f -> h e f")).then_inc(ld_moe, 16)
            sp.dma_start(ED[:, :, :], edown.rearrange("(k u) i h -> (u i) k h", u=2)).then_inc(ld_moe, 16)
            sp.dma_start(FWT[:, :], ffn_wt).then_inc(ld_ffn, 16)
            sp.dma_start(FVC[:, 0, :], ffn_vt).then_inc(ld_ffn, 16)
            sp.dma_start(FVC[:, 1, :], ffn_ct).then_inc(ld_ffn, 16)
            sp.wait_ge(zero_set, 2)
            for n in range(4):
                sp.dma_start(parts_z[:, n * 4096:(n + 1) * 4096], ZERO).then_inc(zero_st, 16)
            sp.dma_start(table[0:1, :], zrow[:, :]).then_inc(zero_st, 16)
            with sp.Fori(1, NB // 2) as i:
                for p in range(2):
                    ctx_tile(i, p, i * 2 + p, False)

            sp.wait_ge(m_tab, 1)
            sp.dma_start(table[1:T + 1, :].rearrange("(n p) r -> p n r", p=P), TB[:, :, :]).then_inc(m_tabw, 16)

            for p in range(2):
                ctx_tile(0, p, NB + p, False)

            sp.wait_ge(y_st, 16 * CH)
            for n in range(NB):
                wait(sp, p_sum, n - 3)
                sp.dma_start(PART[:, n % 4, :], parts_v[n, :, :]).then_inc(p_in[n % 4], 16)
            with sp.Fori(1, NB // 2) as i:
                for p in range(2):
                    ctx_tile(i, p, i * 2 + (NB + p), False)
            for m in range(4):
                sp.wait_ge(f_x, m + 1)
                sp.dma_start(out_v[m], OT[:, m % 2, :, :]).then_inc(f_st[m % 2], 16)
            for s in f_st:
                sp.wait_ge(s, 32)

        @block.gpsimd
        def _(pool):
            pool.memset(ones_b[:, :], 1.0).then_inc(const_set, 1)
            pool.memset(ones_d[:, :, :], 0.0).then_inc(const_set, 1)
            pool.wait_ge(const_set, 2)
            for g in range(G):
                pool.memset(ones_d[:, g, g * DH:(g + 1) * DH], 1.0).then_inc(const_set, 1)
            pool.memset(VM[:, :, :, :], 0.0).then_inc(const_set, 1)
            pool.memset(B3[:, :], 0.0).then_inc(const_set, 1)
            pool.memset(ZERO, 0.0).then_inc(zero_set, 1)
            pool.memset(zrow[:, :], float(T * TOPK)).then_inc(const_set, 1)
            pool.wait_ge(const_set, 9)
            pool.memset(zrow[:, 0:D + EXPERTS], 0.0).then_inc(zero_set, 1)

            pool.wait_ge(zero_st, 80)
            pool.wait_ge(m_tabw, 16)
            for g in range(NG):
                pool.wait_ge(m_idx, 1)
                for s in range(DIG):
                    c = g * DIG + s
                    pool.indirect_dma_start(GA[:, c, :], None, table[:, :],
                                            bass.IndirectOffsetOnAxis(ap=IDI[:, c:c + 1], axis=0)).then_inc(g_in[g], 16)
            for g in range(NG):
                pool.wait_ge(g_wd, g + 1)
                for s in range(DIG):
                    c = g * DIG + s
                    pool.wait_ge(g_ys, 2 * g + s // 4 + 1)
                    pool.indirect_dma_start(parts[:, :], bass.IndirectOffsetOnAxis(ap=DST[:, c:c + 1], axis=0),
                                            YS[:, c, :], None, bounds_check=T * TOPK - 1,
                                            oob_is_err=False).then_inc(y_st, 16)

        @block.tensor
        def _(pe):
            pe.wait_ge(ld_w, 48)
            pe.wait_ge(ld_b, 48)
            for layer in range(2):
                mm = pe.matmul(bank[7][:, layer * D:(layer + 1) * D], BVC[:, layer:layer + 1].to_broadcast([P, P]),
                               WO[:, layer, :], start=True, stop=True)
            mm.then_inc(bias_mm, 1)
            pe.wait_ge(ld_ffn, 48)
            pe.wait_ge(bias_set, 2)
            pe.matmul(bank[7][:, 0:D], FVC[:, 0, :], FVC[:, 1, :], start=True, stop=True).then_inc(f_w, 1)
            pe.wait_ge(f_wf, 1)

            def transposes(layer, i, p, B):
                wait(pe, xn_done, B + 1)
                pe.wait_ge(cx_in[p], i * 16 + (NB // 2 * layer + 1) * 16)
                wait(pe, v_done, B)
                wait(pe, x_done, B - 2)
                pe.transpose(bank[7][:, 0:D], XN[:, p, :], ident)
                pe.transpose(bank[7][:, D:2 * D], CXB[:, p, :], ident).then_inc(tr_mm, 1)

            def project(layer, which, moving, last_out):
                for g in range(G):
                    pe.matmul(bank[4][:, g * P:(g + 1) * P], WREP[:, layer, which, g * P:(g + 1) * P], moving,
                              start=True, stop=False)
                    off = (layer * 2 + which) * 512 + g * P
                    mm = pe.matmul(bank[4][:, g * P:(g + 1) * P], B3[:, off:off + P], ones_b[:, :],
                                   start=False, stop=True)
                mm.then_inc(last_out, 1)

            def q_project(layer, p, B):
                wait(pe, xc_done, B + 1)
                wait(pe, k_split, B)
                project(layer, 0, XC[:, p, 0:D], q_mm)

            def k_project(layer, p, B):
                wait(pe, q_split, B + 1)
                project(layer, 1, XC[:, p, D:2 * D], k_mm)

            def v_project(layer, p, B):
                wait(pe, xc_done, B + 1)
                pe.matmul(bank[7][:, 0:D], XC[:, p, D:2 * D], WV[:, layer, :], start=True, stop=True).then_inc(v_mm, 1)

            def max_pass(p, g, B):
                if g == 0:
                    wait(pe, q_masked, B + 1)
                    wait(pe, k_split, B + 1)
                wait(pe, max_got, B * 4 + (g - 1))
                for j in range(J):
                    mm = pe.matmul(bank[g % 2][:, j * P:(j + 1) * P], QM[:, p, g, j, :], KS[:, p, g, :],
                                   start=True, stop=True)
                mm.then_inc(max_mm, 1)

            def scores(p, g, B):
                wait(pe, exp_done, B * 4 + (g - 1))
                t = bank[2 + g % 2]
                pe.matmul(t[:, :], KS[:, p, g, :], QM[:, p, g, :, :], start=True, stop=False)
                wait(pe, max_got, B * 4 + (g + 1))
                for j in range(J):
                    mm = pe.matmul(t[:, j * P:(j + 1) * P], NM[:, g, j:j + 1].to_broadcast([P, P]), negid_b[:, :],
                                   start=False, stop=(j == J - 1))
                mm.then_inc(score_mm, 1)

            def weighted(p, g, B):
                if g == 0:
                    wait(pe, ctx_done, B - 1)
                    wait(pe, v_done, B + 1)
                wait(pe, exp_done, B * 4 + (g + 1))
                acc = bank[5 + p]
                for j in range(J):
                    pe.matmul(acc[32 * j:32 * j + 32, 0:P], VM[:, p, g, 32 * j:32 * j + 32],
                              E[:, g, j * P:(j + 1) * P], start=(g == 0), stop=(g == G - 1), skip_group_check=True)
                for j in range(J):
                    mm = pe.matmul(acc[32 * j:32 * j + 32, P:2 * P], ones_d[:, g, :], E[:, g, j * P:(j + 1) * P],
                                   start=False, stop=(g == G - 1), skip_group_check=True)
                mm.then_inc(pv_mm, 1)

            def o_project(layer, p, B, newer):
                wait(pe, ctx_done, B + 1)
                if newer:
                    wait(pe, v_done, B + 3)
                off = 2048 + layer * D
                pe.matmul(bank[7][:, 0:D], CN[:, p, :], WO[:, layer, :], start=True, stop=False)
                pe.matmul(bank[7][:, 0:D], ones_b[:, :], B3[:, off:off + D], start=False, stop=True).then_inc(o_mm, 1)

            def attention(layer):
                B0 = NB * layer
                transposes(layer, 0, 0, B0)
                q_project(layer, 0, B0)
                k_project(layer, 0, B0)
                v_project(layer, 0, B0)
                transposes(layer, 0, 1, B0 + 1)
                q_project(layer, 1, B0 + 1)
                max_pass(0, 0, B0)
                max_pass(0, 1, B0)
                scores(0, 0, B0)

                def step(i, p, B, last):
                    q = 1 - p
                    end = last and p == 1
                    for g in range(G):
                        if g < 2:
                            max_pass(p, g + 2, B)
                        elif not end:
                            max_pass(q, g - 2, B + 1)
                        if g < 3:
                            scores(p, g + 1, B)
                        elif not end:
                            scores(q, 0, B + 1)
                        if g == 0 and not end:
                            k_project(layer, q, B + 1)
                            v_project(layer, q, B + 1)
                        if g == 1 and not (isinstance(i, int) and i == 0 and p == 0):
                            o_project(layer, q, B - 1, newer=not end)
                        if g == 2 and not last:
                            transposes(layer, i + 1, p, B + 2)
                        if g == 3 and not last:
                            q_project(layer, p, B + 2)
                        weighted(p, g, B)

                over_batches(pe, layer, step)
                o_project(layer, 1, B0 + NB - 1, newer=False)

            pe.wait_ge(bias_set, 3)
            attention(0)

            for m in range(4):
                pe.wait_ge(m_xn, m + 1)
                pe.wait_ge(x_done, NB)
                for n in range(4):
                    mm = pe.transpose(bank[m][:, n * P:(n + 1) * P], TB[:, 4 * m + n, 0:D], ident)
                mm.then_inc(m_tr, 1)
            pe.wait_ge(ld_moe, 80)
            for m in range(4):
                pe.wait_ge(m_xt, m + 1)
                for n in range(4):
                    t = 4 * m + n
                    mm = pe.matmul(bank[4 + m][:, n * 65:(n + 1) * 65], XNT[:, t * P:(t + 1) * P], GW[:, :],
                                   start=True, stop=True)
                mm.then_inc(m_lg, 1)

            def shared_up(m):
                for c in range(4):
                    if m > 0:
                        if c < 2:
                            pe.wait_ge(h_h1, 2 * (m - 1) + c + 1)
                        else:
                            pe.wait_ge(h_act, 2 * (m - 1) + c - 1)
                    pe.matmul(bank[c][:, :], SGU[:, c * P:(c + 1) * P], XNT[:, m * 512:(m + 1) * 512],
                              start=True, stop=True).then_inc(h_mm, 1)

            def shared_down(m):
                pe.wait_ge(h_act, 2 * m + 2)
                if m > 0:
                    pe.wait_ge(h_sh, m)
                for n in range(4):
                    for c in range(2):
                        mm = pe.matmul(bank[4][:, n * P:(n + 1) * P], HS[:, c, n * P:(n + 1) * P], SD[:, c, :],
                                       start=(c == 0), stop=(c == 1))
                mm.then_inc(h_dn, 1)

            pe.wait_ge(m_mask, 1)
            pe.wait_ge(m_lgc, 4)
            for h in range(2):
                pe.matmul(bank[6 + h][:, :], tri_b[:, :], MASK[:, 8 * h:8 * h + 8, :], start=True, stop=False)
                for t in range(8 * h + 7):
                    lo = max(8 * h, t + 1)
                    n = 8 * h + 8 - lo
                    mm = pe.matmul(bank[6 + h][:, (lo - 8 * h) * 64:512], ones_b[:, :],
                                   MASK[:, t:t + 1, :].to_broadcast([P, n, 64]), start=False, stop=(t == 8 * h + 6))
                mm.then_inc(m_pos, 1)
            pe.wait_ge(m_lgc, 4)
            for t in range(NB):
                pe.wait_ge(m_hot, t + 1)
                for g in range(NG):
                    mm = pe.matmul(bank[5][:, g * P:(g + 1) * P], HOT[:, 0, t, EG * g:EG * g + EG, :],
                                   HOT[:, 1, t, EG * g:EG * g + EG, :], start=(t == 0 and g == 0),
                                   stop=(t == NB - 1), skip_group_check=True)
            mm.then_inc(m_ids, 1)

            for m in range(4):
                shared_up(m)
                shared_down(m)

            def expert_in(g):
                pe.wait_ge(g_in[g], 16 * DIG)
                for h in range(2):
                    if g > 0:
                        pe.wait_ge(g_xt, 2 * (g - 1) + h + 1)
                    else:
                        pe.wait_ge(h_act, 8)
                    for s in range(4):
                        mm = pe.transpose(bank[h][:, s * P:(s + 1) * P], GA[:, g * DIG + 4 * h + s, 0:D], ident)
                    mm.then_inc(g_tr, 1)

            def expert_up(g):
                pe.wait_ge(g_xt, 2 * g + 2)
                if g > 0:
                    pe.wait_ge(g_act, g)
                for k in range(EG // 2):
                    for w in range(2):
                        for u in range(2):
                            e = 2 * k + u
                            mm = pe.matmul(bank[2 + w][64 * u:64 * u + 64, k * CAP:(k + 1) * CAP],
                                           EGU[:, EG * g + e, w * FE:(w + 1) * FE],
                                           XG[:, g % 2, :, e * DIG:(e + 1) * DIG], start=True, stop=True)
                mm.then_inc(g_up, 1)

            def expert_down(g):
                pe.wait_ge(g_act, g + 1)
                if g > 0:
                    pe.wait_ge(g_yt, g)
                else:
                    pe.wait_ge(h_sh, 4)
                    pe.wait_ge(m_idx, 1)
                for u in range(2):
                    o = bank[4 + u][:, :].rearrange("p (s k a) -> p s k a", s=DIG, k=EG // 2)
                    for k in range(EG // 2):
                        mm = pe.matmul(o[:, :, k, :], ED[64 * u:64 * u + 64, g * (EG // 2) + k, :],
                                       AH[64 * u:64 * u + 64, k, :].rearrange("p (s a) -> p s a", s=DIG),
                                       start=True, stop=True)
                mm.then_inc(g_dn, 1)

            def expert_back(g):
                pe.wait_ge(g_yt, g + 1)
                for h in range(2):
                    if g > 0:
                        pe.wait_ge(g_ys, 2 * (g - 1) + h + 1)
                    else:
                        pe.wait_ge(m_hot, NB)
                    for s in range(4):
                        mm = pe.transpose(bank[6 + h][:, s * P:(s + 1) * P],
                                          YT[:, 4 * h + s, :, :, :].rearrange("p k u a -> p (k u a)"), ident)
                    mm.then_inc(g_bk, 1)

            for g in range(NG):
                expert_in(g)
                expert_up(g)
                expert_down(g)
                expert_back(g)

            pe.wait_ge(g_xt, 2 * NG)
            pe.wait_ge(g_ys, 2 * NG)
            attention(1)

            for m in range(4):
                pe.wait_ge(f_xn, m + 1)
                if m >= 2:
                    pe.wait_ge(f_xt, m - 1)
                pe.wait_ge(x_done, 2 * NB)
                for n in range(4):
                    mm = pe.transpose(bank[m % 2][:, n * P:(n + 1) * P], TB[:, 4 * m + n, 0:D], ident)
                mm.then_inc(f_tr, 1)
                pe.wait_ge(f_xt, m + 1)
                if m >= 2:
                    pe.wait_ge(f_x, m - 1)
                for n in range(4):
                    t = 4 * m + n
                    pe.matmul(bank[2 + m % 2][:, n * P:(n + 1) * P], XNT[:, t * P:(t + 1) * P], WF[:, :],
                              start=True, stop=False)
                    mm = pe.matmul(bank[2 + m % 2][:, n * P:(n + 1) * P], ones_b[:, :], B3[:, 2048 + 2 * D:NBR],
                                   start=False, stop=True)
                mm.then_inc(f_mm, 1)

        @block.scalar
        def _(act):
            act.wait_ge(ld_con, 32)
            act.activation(TH[:, :], GT[:, :], ACT.Tanh).then_inc(gates_done, 1)

            def transposed(p, B):
                wait(act, tr_mm, B + 1)
                wait(act, v_mm, B - 1)
                wait(act, k_mm, B - 1)
                act.activation(XC[:, p, :], bank[7][:, 0:2 * D], ACT.Copy).then_inc(xc_done, 1)

            def q_low_part(B):
                wait(act, q_mm, B + 1)
                wait(act, q_split, B)
                act.activation(LO[:, 0, :], bank[4][:, :], ACT.Copy, scale=CON[:, C_QLO:C_QLO + 1]).then_inc(q_low, 1)

            def k_low_part(B):
                wait(act, k_mm, B + 1)
                wait(act, k_split, B)
                act.activation(LO[:, 1, :], bank[4][:, :], ACT.Copy, scale=CON[:, C_KLO:C_KLO + 1]).then_inc(k_low, 1)

            def exponentials(g, B):
                wait(act, score_mm, B * 4 + (g + 1))
                wait(act, pv_mm, B * 4 + (g - 3))
                act.activation(E[:, g, :], bank[2 + g % 2][:, :], ACT.Exp, scale=SCALE).then_inc(exp_done, 1)

            def attention(layer):
                B0 = NB * layer
                transposed(0, B0)
                q_low_part(B0)
                k_low_part(B0)
                transposed(1, B0 + 1)
                q_low_part(B0 + 1)
                exponentials(0, B0)

                def step(i, p, B, last):
                    end = last and p == 1
                    for g in range(G):
                        if g < 3:
                            exponentials(g + 1, B)
                        elif not end:
                            exponentials(0, B + 1)
                        if g == 0 and not end:
                            k_low_part(B + 1)
                        if g == 2 and not last:
                            transposed(p, B + 2)
                        if g == 3 and not last:
                            q_low_part(B + 2)

                over_batches(act, layer, step)

            attention(0)

            for m in range(4):
                act.wait_ge(m_tr, m + 1)
                act.activation(XNT[:, m * 512:(m + 1) * 512], bank[m][:, :], ACT.Copy).then_inc(m_xt, 1)
            act.wait_ge(m_sub, 1)
            act.activation(LM[:, :, :], LM[:, :, :], ACT.Exp).then_inc(m_exp, 1)
            act.activation(SG[:, :], SG[:, :], ACT.Tanh, scale=0.5).then_inc(m_exp, 1)
            for m in range(4):
                for c in range(2):
                    act.wait_ge(h_mm, 4 * m + c + 1)
                    if m > 0:
                        act.wait_ge(h_h1, 2 * (m - 1) + c + 1)
                    act.activation(TS_[:, c, :], bank[c][:, :], ACT.Tanh, scale=0.5).then_inc(h_tanh, 1)
            for g in range(NG):
                for h in range(2):
                    act.wait_ge(g_tr, 2 * g + h + 1)
                    if g >= 2:
                        act.wait_ge(g_up, g - 1)
                    act.activation(XG[:, g % 2, 4 * h:4 * h + 4, :], bank[h][:, :].rearrange("p (s n) -> p s n", s=4),
                                   ACT.Copy).then_inc(g_xt, 1)
                act.wait_ge(g_up, g + 1)
                if g > 0:
                    act.wait_ge(g_h1, g)
                act.activation(TG[:, :], bank[2][:, :], ACT.Tanh, scale=0.5).then_inc(g_tanh, 1)
                act.wait_ge(g_dn, g + 1)
                if g > 0:
                    act.wait_ge(g_bk, 2 * g)
                for u in range(2):
                    act.activation(YT[:, :, :, u, :], bank[4 + u][:, :].rearrange("p (s k a) -> p s k a", s=DIG, a=DIG),
                                   ACT.Copy).then_inc(g_own, 1)
                act.wait_ge(g_own, 2 * g + 2)
                act.nop().then_inc(g_yt, 1)
            attention(1)
            for m in range(4):
                act.wait_ge(f_tr, m + 1)
                act.activation(XNT[:, m * 512:(m + 1) * 512], bank[m % 2][:, :], ACT.Copy).then_inc(f_xt, 1)

        @block.vector
        def _(dve):
            def rsqrt_of_variances(turn):
                base = 11 * turn

                def link(ins, n):
                    ins.then_inc(rs_step, 1)
                    dve.wait_ge(rs_step, base + n)

                link(dve.tensor_scalar(VE[:, :], MV[:, :, 1], EPS, None, ALU.add), 1)
                link(dve.tensor_scalar(RS[:, :].bitcast(I32), VE[:, :].bitcast(I32), -0.5, RSQRT_SEED, ALU.mult, ALU.add), 2)
                for n in range(3):
                    link(dve.tensor_tensor(NW[:, 0, :], RS[:, :], RS[:, :], ALU.mult), 3 + 3 * n)
                    link(dve.scalar_tensor_tensor(out=NW[:, 1, :], in0=NW[:, 0, :], scalar=-0.5, in1=VE[:, :],
                                                  op0=ALU.mult, op1=ALU.mult), 4 + 3 * n)
                    ins = dve.scalar_tensor_tensor(out=RS[:, :], in0=NW[:, 1, :], scalar=1.5, in1=RS[:, :],
                                                   op0=ALU.add, op1=ALU.mult)
                    link(ins, 5 + 3 * n)

            dve.wait_ge(ld_x, 16)
            for n in range(NB):
                if n >= 2:
                    dve.wait_ge(mv_done, n - 1)
                dve.bn_stats(STATS[:, n % 2, :], X[:, n, :]).then_inc(stat_done, 1)
                dve.wait_ge(stat_done, n + 1)
                dve.bn_aggr(MV[:, n, :], STATS[:, n % 2, :]).then_inc(mv_done, 1)
            dve.wait_ge(mv_done, NB)
            rsqrt_of_variances(0)

            dve.wait_ge(ld_con, 32)
            dve.tensor_scalar(negid_b[:, :], ident, -1.0, None, ALU.mult).then_inc(dve_set, 1)
            dve.tensor_copy(tri_b[:, :], CON[:, C_TRI:C_TRI + P]).then_inc(dve_set, 1)
            dve.wait_ge(ld_b, 48)
            dve.wait_ge(bias_mm, 1)
            dve.tensor_tensor(BR[:, 2048:2048 + 2 * D], bank[7][:, 0:2 * D], BR[:, 2048:2048 + 2 * D],
                              ALU.add).then_inc(bias_set, 1)
            dve.wait_ge(bias_set, 1)
            dve.tensor_copy(BR_part[:, 0, :], BR[:, :]).then_inc(dve_set, 1)
            dve.wait_ge(dve_set, 3)
            dve.tensor_tensor(BR_rest[:, :], BR[:, :], BR_part[:, 0, :], ALU.subtract).then_inc(dve_set, 1)
            dve.wait_ge(dve_set, 4)
            dve.tensor_copy(BR_part[:, 1, :], BR_rest[:, :]).then_inc(dve_set, 1)
            dve.wait_ge(dve_set, 5)
            dve.tensor_tensor(BR[:, :], BR_rest[:, :], BR_part[:, 1, :], ALU.subtract).then_inc(dve_set, 1)
            dve.wait_ge(dve_set, 6)
            dve.wait_ge(const_set, 9)
            dve.tensor_copy(B3[0:1, :], BR_part[0:1, 0, :]).then_inc(dve_set, 1)
            dve.tensor_copy(B3[32:33, :], BR_part[32:33, 1, :]).then_inc(dve_set, 1)
            dve.tensor_copy(B3[64:65, :], BR[64:65, :]).then_inc(bias_set, 1)
            dve.wait_ge(f_w, 1)
            dve.tensor_tensor(WF[:, :], bank[7][:, 0:D], FWT[:, :], ALU.add).then_inc(f_wf, 1)
            dve.wait_ge(f_wf, 1)
            dve.wait_ge(dve_set, 8)
            dve.wait_ge(gates_done, 1)
            dve.tensor_copy(SG[:, 0:1], TH[:, 0:1]).then_inc(bias_set, 1)

            def normalised(layer, i, p, B):
                wait(dve, tr_mm, B - 1)
                b = i * 2 + p
                dve.tensor_scalar(XN[:, p, :], X[:, b, :], MV[:, b, 0:1], RS3[:, b, :],
                                  ALU.subtract, ALU.mult).then_inc(xn_done, 1)

            def maxima(g, B):
                wait(dve, max_mm, B * 4 + (g + 1))
                wait(dve, score_mm, B * 4 + (g - 3))
                dve.tensor_reduce(NM[:, g, :], bank[g % 2][:, :].rearrange("p (j k) -> p j k", j=J), AXX,
                                  ALU.max).then_inc(max_got, 1)

            def q_parts(B):
                wait(dve, q_low, B + 1)
                wait(dve, q_masked, B)
                dve.tensor_tensor(QS[:, 0, :], bank[4][:, :], LO[:, 0, :], ALU.subtract).then_inc(q_split, 1)

            def q_mask(p, B):
                wait(dve, q_split, B + 1)
                wait(dve, score_mm, B * 4 - 4)
                for j in range(J):
                    ins = dve.tensor_scalar(QM[:, p, :, j, :], QS[:, 0, :].rearrange("p (g q) -> p g q", g=G),
                                            CON[:, C_QUAD + j:C_QUAD + j + 1], None, ALU.mult)
                ins.then_inc(q_masked, 1)

            def k_parts(p, B):
                wait(dve, k_low, B + 1)
                wait(dve, score_mm, B * 4 - 4)
                dve.tensor_tensor(KS[:, p, :, :].rearrange("p g k -> p (g k)"), bank[4][:, :], LO[:, 1, :],
                                  ALU.subtract).then_inc(k_split, 1)

            def values(p, B):
                wait(dve, v_mm, B + 1)
                wait(dve, pv_mm, B * 4 - 4)
                src = bank[7][:, 0:D].rearrange("p (j g d) -> p j g d", j=J, g=G)
                for g in range(G):
                    ins = dve.tensor_copy(VM[:, p, g, :].rearrange("p (j r) -> p j r", j=J)[:, :, g * DH:(g + 1) * DH],
                                          src[:, :, g, :])
                ins.then_inc(v_done, 1)

            def normalise_context(p, B):
                wait(dve, pv_mm, B * 4 + 4)
                wait(dve, ctx_done, B)
                dve.reciprocal(RD[:, :], bank[5 + p][:, D:2 * D]).then_inc(recip_done, 1)
                wait(dve, recip_done, B + 1)
                wait(dve, o_mm, B - 1)
                dve.tensor_tensor(CN[:, p, :], bank[5 + p][:, 0:D], RD[:, :], ALU.mult).then_inc(ctx_done, 1)

            def residual(layer, i, p, B):
                wait(dve, o_mm, B + 1)
                b = i * 2 + p
                dve.scalar_tensor_tensor(out=X[:, b, :], in0=bank[7][:, 0:D], scalar=TH[:, layer:layer + 1],
                                         in1=X[:, b, :], op0=ALU.mult, op1=ALU.add).then_inc(x_done, 1)

            def before_statistics(layer, B):
                wait(dve, x_done, B + 1)
                wait(dve, mv_done, B + (NB + NB * layer - 1))

            def before_mean_variance(layer, B):
                wait(dve, stat_done, B + (NB + NB * layer + 1))
                wait(dve, mv_done, B + (NB + NB * layer))

            def statistics(layer, i, p, B):
                dve.bn_stats(STATS[:, p, :], X[:, i * 2 + p, :]).then_inc(stat_done, 1)

            def mean_variance(layer, i, p, B):
                dve.bn_aggr(MV_now[:, :], STATS[:, p, :]).then_inc(aggr_done, 1)
                wait(dve, aggr_done, B + 1)
                dve.tensor_copy(MV[:, i * 2 + p, :], MV_now[:, :]).then_inc(mv_done, 1)

            def attention(layer):
                B0 = NB * layer
                normalised(layer, 0, 0, B0)
                normalised(layer, 0, 1, B0 + 1)
                q_parts(B0)
                q_mask(0, B0)
                k_parts(0, B0)
                values(0, B0)
                maxima(0, B0)
                maxima(1, B0)
                q_parts(B0 + 1)

                def step(i, p, B, last):
                    q = 1 - p
                    end = last and p == 1
                    first = isinstance(i, int) and i == 0
                    before = i - 1 if p == 0 else i
                    for g in range(G):
                        if g == 0 and not first:
                            before_mean_variance(layer, B - 2)
                        if g == 3 and not (first and p == 0):
                            before_statistics(layer, B - 1)
                        if g < 2:
                            maxima(g + 2, B)
                        elif not end:
                            maxima(g - 2, B + 1)
                        if g == 3 and not (first and p == 0):
                            statistics(layer, before, q, B - 1)
                        if g == 0:
                            if not first:
                                mean_variance(layer, i - 1, p, B - 2)
                            if not (first and p == 0):
                                normalise_context(q, B - 1)
                            if not end:
                                q_mask(q, B + 1)
                        if g == 1:
                            if not end:
                                k_parts(q, B + 1)
                                values(q, B + 1)
                            if not last:
                                normalised(layer, i + 1, p, B + 2)
                        if g == 2 and not (first and p == 0):
                            residual(layer, before, q, B - 1)
                        if g == 3 and not last:
                            q_parts(B + 2)

                over_batches(dve, layer, step)
                n = NB // 2 - 1
                B1 = B0 + NB - 1
                normalise_context(1, B1)
                before_mean_variance(layer, B1 - 1)
                mean_variance(layer, n, 0, B1 - 1)
                residual(layer, n, 1, B1)
                before_statistics(layer, B1)
                statistics(layer, n, 1, B1)
                before_mean_variance(layer, B1)
                mean_variance(layer, n, 1, B1)
                dve.wait_ge(mv_done, NB * (2 * layer + 2))

            attention(0)

            rsqrt_of_variances(1)
            for t in range(NB):
                ins = dve.tensor_scalar(TB[:, t, 0:D], X[:, t, :], MV[:, t, 0:1], RS[:, t:t + 1], ALU.subtract, ALU.mult)
                if t % 4 == 3:
                    ins.then_inc(m_xn, 1)
            step_n = [0]

            def link(ins):
                step_n[0] += 1
                ins.then_inc(m_step, 1)
                dve.wait_ge(m_step, step_n[0])

            for m in range(4):
                dve.wait_ge(m_lg, m + 1)
                v = bank[4 + m][:, 0:260].rearrange("p (n e) -> p n e", n=4)
                dve.tensor_copy(SG[:, 4 * m:4 * m + 4], v[:, :, EXPERTS])
                dve.tensor_copy(LG[:, 4 * m:4 * m + 4, :], v[:, :, 0:EXPERTS]).then_inc(m_lgc, 1)
            dve.wait_ge(m_lgc, 4)
            for t in range(NB):
                ins = dve.max(TOP[:, t, :], LG[:, t, :])
            link(ins)
            for t in range(NB):
                ins = dve.match_replace(POS[:, t, :], TOP[:, t, :], LG[:, t, :], -3.0e38)
            dve.tensor_tensor(LM[:, :, :], LG[:, :, :], TOP[:, :, 0:1].to_broadcast([P, NB, EXPERTS]),
                              ALU.subtract).then_inc(m_sub, 1)
            dve.wait_ge(m_sub, 1)
            dve.tensor_tensor(MASK[:, :, :], POS[:, :, :], LG[:, :, :], ALU.not_equal).then_inc(m_mask, 1)
            dve.wait_ge(m_mask, 1)
            dve.wait_ge(m_exp, 2)
            link(dve.tensor_tensor(LM[:, :, :], LM[:, :, :], MASK[:, :, :], ALU.mult))
            link(dve.tensor_reduce(SUMS[:, :], LM[:, :, :], AXX, ALU.add))
            link(dve.reciprocal(SUMS[:, :], SUMS[:, :]))
            link(dve.tensor_scalar(SUMS[:, :], SUMS[:, :], 0.5, None, ALU.mult))
            link(dve.tensor_tensor(TB[:, :, D:D + EXPERTS], LM[:, :, :],
                                   SUMS[:, :].rearrange("p (n o) -> p n o", o=1).to_broadcast([P, NB, EXPERTS]), ALU.mult))
            dve.wait_ge(m_pos, 2)
            for h in range(2):
                ins = dve.tensor_copy(POS[:, 8 * h:8 * h + 8, :].rearrange("p n e -> p (n e)"), bank[6 + h][:, :])
            link(ins)
            link(dve.tensor_scalar(KEPT[:, :, :], POS[:, :, :], float(CAP), None, ALU.is_lt))
            link(dve.tensor_tensor(KEPT[:, :, :], KEPT[:, :, :], MASK[:, :, :], ALU.mult))
            link(dve.tensor_copy(HI_D[:, :, :], POS[:, :, :]))
            link(dve.tensor_scalar(LO_D[:, :, :], HI_D[:, :, :], DIG - 1, None, ALU.bitwise_and))
            link(dve.tensor_scalar(HI_D[:, :, :], HI_D[:, :, :], 3, None, ALU.logical_shift_right))
            link(dve.scalar_tensor_tensor(out=POS[:, :, :], in0=HI_D[:, :, :], scalar=1.0, in1=KEPT[:, :, :],
                                          op0=ALU.add, op1=ALU.mult))
            link(dve.tensor_scalar(POS[:, :, :], POS[:, :, :], -1.0, None, ALU.add))
            digits = CON[:, C_DIG:C_DIG + DIG].rearrange("p (o s) -> p o s", o=1).to_broadcast([P, EXPERTS, DIG])
            for t in range(NB):
                dve.tensor_tensor(HOT[:, 0, t, :, :],
                                  POS[:, t, :].rearrange("p (e o) -> p e o", o=1).to_broadcast([P, EXPERTS, DIG]),
                                  digits, ALU.is_equal)
                link(dve.tensor_tensor(HOT[:, 1, t, :, :],
                                       LO_D[:, t, :].rearrange("p (e o) -> p e o", o=1).to_broadcast([P, EXPERTS, DIG]),
                                       digits, ALU.is_equal))
                dve.tensor_scalar(HOT[:, 1, t, :, :], HOT[:, 1, t, :, :], CON[:, C_TOK + t:C_TOK + t + 1], None,
                                  ALU.mult).then_inc(m_hot, 1)
            flat = "p n e -> p (n e)"
            link(dve.tensor_tensor_scan(LG[:, :, :].rearrange(flat), KEPT[:, :, :].rearrange(flat),
                                        KEPT[:, :, :].rearrange(flat), 0.0, ALU.add, ALU.bypass))
            link(dve.tensor_copy(SUMS[:, 1:NB], LG[:, 0:NB - 1, EXPERTS - 1]))
            link(dve.memset(SUMS[:, 0:1], 0.0))
            link(dve.tensor_tensor(SUMS[:, :], CON[:, C_TOK8:C_TOK8 + NB], SUMS[:, :], ALU.subtract))
            link(dve.tensor_tensor(LG[:, :, :], LG[:, :, :], KEPT[:, :, :], ALU.subtract))
            dve.tensor_tensor(TB[:, :, D + EXPERTS:ROW], LG[:, :, :],
                              SUMS[:, :].rearrange("p (n o) -> p n o", o=1).to_broadcast([P, NB, EXPERTS]),
                              ALU.add).then_inc(m_tab, 1)
            dve.wait_ge(m_ids, 1)
            own = CON[:, C_OWN:C_OWN + EG]
            link(dve.tensor_tensor(IDX[:, :, :, :].rearrange("p g e s -> p g (e s)").rearrange("p g (e s) -> p g e s", s=DIG),
                                   bank[5][:, :].rearrange("p (g e s) -> p g e s", g=NG, s=DIG),
                                   own.rearrange("p (o e u) -> p o e u", o=1, u=1).to_broadcast([P, NG, EG, DIG]), ALU.mult))
            link(dve.tensor_reduce(IDF[:, :].rearrange("p (g s) -> p g s", g=NG),
                                   IDX[:, :, :, :].rearrange("p g e s -> p g s e"), AXX, ALU.add))
            dve.tensor_copy(IDI[:, :], IDF[:, :]).then_inc(m_idx, 1)
            link(dve.tensor_scalar(SG[:, :], SG[:, :], 0.25, 0.25, ALU.mult, ALU.add))

            for m in range(4):
                for c in range(2):
                    dve.wait_ge(h_tanh, 2 * m + c + 1)
                    dve.wait_ge(h_mm, 4 * m + 4)
                    if m > 0:
                        dve.wait_ge(h_dn, m)
                    dve.scalar_tensor_tensor(out=HS[:, c, :], in0=TS_[:, c, :], scalar=1.0, in1=bank[c][:, :],
                                             op0=ALU.add, op1=ALU.mult).then_inc(h_h1, 1)
                for c in range(2):
                    dve.wait_ge(h_h1, 2 * m + c + 1)
                    dve.tensor_tensor(HS[:, c, :], HS[:, c, :], bank[2 + c][:, :], ALU.mult).then_inc(h_act, 1)
                dve.wait_ge(h_dn, m + 1)
                if m > 0:
                    dve.wait_ge(h_x, m)
                dve.tensor_tensor(SH[:, :, :], bank[4][:, :].rearrange("p (n d) -> p n d", n=4),
                                  SG[:, 4 * m:4 * m + 4].rearrange("p (n o) -> p n o", o=1).to_broadcast([P, 4, D]),
                                  ALU.mult).then_inc(h_sh, 1)
                dve.wait_ge(h_sh, m + 1)
                dve.scalar_tensor_tensor(out=X[:, 4 * m:4 * m + 4, :], in0=SH[:, :, :], scalar=TH[:, 2:3],
                                         in1=X[:, 4 * m:4 * m + 4, :], op0=ALU.mult, op1=ALU.add).then_inc(h_x, 1)

            for g in range(NG):
                dve.wait_ge(g_in[g], 16 * DIG)
                mine = GA[:, g * DIG:(g + 1) * DIG, D:ROW].rearrange("p s (w e) -> p s w e", w=2)[:, :, :, EG * g:EG * g + EG]
                link(dve.tensor_tensor(OWNP[:, :, :, :], mine,
                                       own.rearrange("p (o u e) -> p o u e", o=1, u=1).to_broadcast([P, DIG, 2, EG]), ALU.mult))
                link(dve.tensor_reduce(WD[:, g * DIG:(g + 1) * DIG, :], OWNP[:, :, :, :], AXX, ALU.add))
                dve.tensor_copy(DST[:, g * DIG:(g + 1) * DIG], WD[:, g * DIG:(g + 1) * DIG, 1]).then_inc(g_wd, 1)
                dve.wait_ge(g_tanh, g + 1)
                dve.scalar_tensor_tensor(out=H1[:, :], in0=TG[:, :], scalar=1.0, in1=bank[2][:, :],
                                         op0=ALU.add, op1=ALU.mult).then_inc(g_h1, 1)
                dve.wait_ge(g_h1, g + 1)
                if g > 0:
                    dve.wait_ge(g_dn, g)
                dve.tensor_tensor(AH[:, :, :].rearrange("p k n -> p (k n)"), H1[:, :], bank[3][:, :],
                                  ALU.mult).then_inc(g_act, 1)
                for h in range(2):
                    dve.wait_ge(g_bk, 2 * g + h + 1)
                    c = g * DIG + 4 * h
                    dve.tensor_tensor(YS[:, c:c + 4, :], bank[6 + h][:, :].rearrange("p (s d) -> p s d", s=4),
                                      WD[:, c:c + 4, 0:1].to_broadcast([P, 4, D]), ALU.mult).then_inc(g_ys, 1)

            for n in range(NB):
                dve.wait_ge(p_in[n % 4], 16 * (n // 4 + 1))
                dve.tensor_reduce(ysum[:, n % 2, :], PART[:, n % 4, :].rearrange("p (k d) -> p d k", k=TOPK), AXX,
                                  ALU.add).then_inc(p_sum, 1)
                dve.wait_ge(p_sum, n + 1)
                dve.scalar_tensor_tensor(out=X[:, n, :], in0=ysum[:, n % 2, :], scalar=TH[:, 2:3], in1=X[:, n, :],
                                         op0=ALU.mult, op1=ALU.add).then_inc(p_x, 1)
                dve.wait_ge(p_x, n + 1)
                dve.bn_stats(STATS[:, n % 2, :], X[:, n, :]).then_inc(stat_done, 1)
                dve.wait_ge(stat_done, 2 * NB + n + 1)
                dve.bn_aggr(MV[:, n, :], STATS[:, n % 2, :]).then_inc(mv_done, 1)
            dve.wait_ge(mv_done, 3 * NB)
            rsqrt_of_variances(2)
            attention(1)

            rsqrt_of_variances(3)
            for t in range(NB):
                ins = dve.tensor_scalar(TB[:, t, 0:D], X[:, t, :], MV[:, t, 0:1], RS[:, t:t + 1], ALU.subtract, ALU.mult)
                if t % 4 == 3:
                    ins.then_inc(f_xn, 1)
            for m in range(4):
                dve.wait_ge(f_mm, m + 1)
                if m >= 2:
                    dve.wait_ge(f_st[m % 2], 16)
                dve.scalar_tensor_tensor(out=OT[:, m % 2, :, :].rearrange("p n d -> p (n d)"), in0=bank[2 + m % 2][:, :],
                                         scalar=TH[:, 3:4], in1=X[:, 4 * m:4 * m + 4, :].rearrange("p n d -> p (n d)"),
                                         op0=ALU.mult, op1=ALU.add).then_inc(f_x, 1)


def kernel(x, ctx_1024, g_xattn, g_ffn, L0_xattn_w_q, L0_xattn_b_q, L0_xattn_w_k, L0_xattn_b_k, L0_xattn_w_v,
           L0_xattn_b_v, L0_xattn_w_o, L0_xattn_b_o, L0_ffn_gate_w, L0_ffn_shared_gate_w, L0_ffn_shared_gate_up_w,
           L0_ffn_shared_down_w, L0_ffn_expert_gate_up_w, L0_ffn_expert_down_w, L1_xattn_Wq, L1_xattn_bq,
           L1_xattn_Wk, L1_xattn_bk, L1_xattn_Wv, L1_xattn_bv, L1_xattn_Wo, L1_xattn_bo, L1_ffn_W, L1_ffn_b,
           L1_ffn_V_r, L1_ffn_C):
    import concourse.bacc as bacc
    from concourse.bass_utils import run_bass_kernel_spmd

    g, j, t, d = np.meshgrid(np.arange(G), np.arange(J), np.arange(4), np.arange(DH), indexing="ij")
    cols = ((J * j + g) * DH + d + 0 * t).reshape(-1)
    a = np.asarray
    layers = [(a(L0_xattn_w_q), a(L0_xattn_w_k), a(L0_xattn_w_v), a(L0_xattn_w_o), a(L0_xattn_b_q), a(L0_xattn_b_k),
               a(L0_xattn_b_v), a(L0_xattn_b_o)),
              (a(L1_xattn_Wq).T, a(L1_xattn_Wk).T, a(L1_xattn_Wv).T, a(L1_xattn_Wo).T, a(L1_xattn_bq), a(L1_xattn_bk),
               a(L1_xattn_bv), a(L1_xattn_bo))]
    data = {
        "x": a(x).reshape(T, D),
        "ctx": a(ctx_1024).reshape(T, D),
        "consts": shape_constants(),
        "wrep": np.stack([np.stack([w[0][:, cols], w[1][:, cols]], 1) for w in layers], 1),
        "wv": np.stack([w[2] for w in layers], 1),
        "wo": np.stack([w[3] for w in layers], 1),
        "brep": np.concatenate([w[k][cols] for w in layers for k in (4, 5)]),
        "brow": np.concatenate([layers[0][7], layers[1][7], a(L1_ffn_b)]),
        "bvcol": np.stack([w[6] for w in layers], 1),
        "gates": np.concatenate([a(g_xattn), a(g_ffn)]),
        "gate_w": np.concatenate([a(L0_ffn_gate_w), a(L0_ffn_shared_gate_w)], 1),
        "sgu": a(L0_ffn_shared_gate_up_w),
        "sdown": a(L0_ffn_shared_down_w),
        "egu": a(L0_ffn_expert_gate_up_w),
        "edown": a(L0_ffn_expert_down_w),
        "ffn_wt": a(L1_ffn_W).T,
        "ffn_vt": a(L1_ffn_V_r).T,
        "ffn_ct": a(L1_ffn_C).T,
    }
    nc = bacc.Bacc("TRN2", target_bir_lowering=False, num_devices=1)
    arrays, aps = {}, {}
    for name, v in data.items():
        v = np.ascontiguousarray(v)
        arrays[f"in_{name}"] = v
        aps[name] = nc.dram_tensor(f"in_{name}", v.shape, mybir.dt.from_np(v.dtype), kind="ExternalInput").ap()
    out = nc.dram_tensor("out_0", (T, D), F32, kind="ExternalOutput").ap()
    program(nc, out=out, **aps)
    r = run_bass_kernel_spmd(nc, [arrays], core_ids=[0])
    return r.results[0]["out_0"].reshape(NB, P, D)
```

```python
from contextlib import ExitStack

import numpy as np
import concourse.bass as bass
from concourse import mybir

F32 = mybir.dt.float32
F16 = mybir.dt.float16
BF16 = mybir.dt.bfloat16
I32 = mybir.dt.int32
I16 = mybir.dt.int16
ALU = mybir.AluOpType
ACT = mybir.ActivationFunctionType
AXX = mybir.AxisListType.X

P = 128
NB = 16
D = 128
T = NB * P
HEADS, DH = 16, 8
G = 4
J = 4
SCALE = float(DH) ** -0.5
EXPERTS, TOPK, CAP = 64, 8, 64
FE = 64
FS = 256
SLOTS = EXPERTS * CAP
EG = 16
NG = EXPERTS // EG
DIG = 8
CH = NG * DIG
ROW = 256
EPS = 1e-5
RSQRT_SEED = float(0x5F3759DF)

C_ID, C_TRI, C_QUAD, C_OWN, C_DIG, C_TOK, C_TOK8 = 0, 128, 256, 260, 276, 284, 300
NCONST = 316


def shape_constants():
    c = np.zeros((P, NCONST), np.float32)
    p = np.arange(P)
    c[:, C_ID:C_ID + P] = np.eye(P)
    c[:, C_TRI:C_TRI + P] = p[:, None] < p[None, :]
    for j in range(J):
        c[:, C_QUAD + j] = p // 32 == j
    c[:, C_OWN:C_OWN + EG] = p[:, None] % EG == np.arange(EG)[None, :]
    c[:, C_DIG:C_DIG + DIG] = np.arange(DIG)
    c[:, C_TOK:C_TOK + NB] = p[:, None] + P * np.arange(NB)[None, :] + 1
    c[:, C_TOK8:C_TOK8 + NB] = TOPK * (p[:, None] + P * np.arange(NB)[None, :]) - TOPK * np.arange(NB)[None, :] - 1
    return c


def program(nc, x, ctx, consts, wqkvo, bcol, brow, gates, gate_w, sgu, sdown, egu, edown,
            ffn_wt, ffn_vt, ffn_ct, out):
    with ExitStack() as es:
        def sb(name, shape, dt=F32):
            return es.enter_context(nc.sbuf_tensor(name, shape, dt))

        def sem(name):
            return es.enter_context(nc.semaphore(name))

        bank = [es.enter_context(nc.psum_tensor(f"bank{i}", [P, 512], F32)) for i in range(8)]
        table = nc.dram_tensor("token_table", (T + 1, ROW), F32).ap()
        parts = nc.dram_tensor("expert_parts", (T * TOPK, D), F32).ap()

        X = sb("X", [P, NB, D])
        CON = sb("CON", [P, NCONST])
        W = sb("W", [P, 2, 4, D])
        BC = sb("BC", [P, 2, 3])
        NBO = 3 * D
        BIG = sb("BIG", [P, 8192])
        BR = BIG[:, 0:NBO]
        BR_rest = BIG[:, NBO:2 * NBO]
        BR_part = BIG[:, 2 * NBO:3 * NBO].bitcast(BF16).rearrange("p (k n) -> p k n", k=2)
        B3 = sb("B3", [P, NBO], BF16)
        GT = sb("GT", [P, 4])
        TH = sb("TH", [P, 4])
        ones_b = sb("ones_b", [P, P], BF16)
        negid_b = sb("negid_b", [P, P], BF16)
        tri_b = sb("tri_b", [P, P], BF16)
        off_b = sb("off_b", [P, P], BF16)
        DIGS = sb("DIGS", [P, NG, DIG, EG], I16)
        ones_d = sb("ones_d", [P, G, 32])
        ident = CON[:, C_ID:C_ID + P]

        CXB = sb("CXB", [P, 2, D])
        XN = sb("XN", [P, 2, D])
        XC = sb("XC", [P, 2, 2 * D])
        HL = sb("HL", [P, 2, 2, P], F16)
        SEL = sb("SEL", [P, 2, 2, G, P], F16)
        QS = sb("QS", [P, 512], F16)
        STORE_A = sb("STORE_A", [P, 2048])
        STORE_B = sb("STORE_B", [P, 2048])
        QM = STORE_A[:, :].bitcast(F16).rearrange("p (b g j q) -> p b g j q", b=2, g=G, j=J)
        KS = sb("KS", [P, 2, G, P], F16)
        VM = sb("VM", [P, 2, G, D])
        VM_p = VM[:, :, :, :].rearrange("p b g d -> p b (g d)")
        VM_blocks = [bass.AP(v.tensor, v.offset, [v.ap[0], [32, J], [D + DH, G], [1, DH]]) for v in (VM_p[:, 0, :], VM_p[:, 1, :])]
        NM = sb("NM", [P, G, J], BF16)
        E = STORE_B[:, :].rearrange("p (g n) -> p g n", g=G)
        RD = sb("RD", [P, D])
        CN = sb("CN", [P, 2, D])
        STATS = sb("STATS", [P, 2, 6])
        MV = sb("MV", [P, NB, 2])
        MV_now = sb("MV_now", [P, 2])
        RS3 = sb("RS3", [P, NB, 1])
        RS = RS3[:, :, 0]
        VE = sb("VE", [P, NB])
        NW = sb("NW", [P, 2, NB])

        TB = sb("TB", [P, NB, ROW])
        XNT = sb("XNT", [P, T])
        GW = sb("GW", [P, EXPERTS + 1])
        SGU = sb("SGU", [P, 2 * FS])
        SD = sb("SD", [P, 2, D])
        EGU = sb("EGU", [P, EXPERTS, 2 * FE])
        ED = sb("ED", [P, EXPERTS // 2, D])
        ROUTE = sb("ROUTE", [P, 4, NB, EXPERTS])
        LG = ROUTE[:, 0, :, :]
        LM = sb("LM", [P, NB, EXPERTS])
        MASK = sb("MASK", [P, NB, EXPERTS], BF16)
        POS = ROUTE[:, 1, :, :]
        COUNT = ROUTE[:, 2, :, :]
        SLOT3 = ROUTE[:, 3, :, :].rearrange("p n e -> p (n e)").bitcast(I16).rearrange("p (w n e) -> p w n e", w=2, n=NB)
        SLOT, HI = SLOT3[:, 0, :, :], SLOT3[:, 1, :, :]
        LOW = sb("LOW", [P, NB, EXPERTS], I16)
        TOP = sb("TOP", [P, NB, 8])
        SUMS = sb("SUMS", [P, NB])
        SG = sb("SG", [P, NB])
        HOT = BIG[:, :].bitcast(F16).rearrange("p (w n g s e) -> p w n g s e", w=2, n=NB, g=NG, s=DIG)
        GA = BIG[:, :].rearrange("p (c r) -> p c r", r=ROW)
        IDX = sb("IDX", [P, NG, DIG, EG])
        IDF = sb("IDF", [P, CH])
        IDI = sb("IDI", [P, CH], I32)
        OWNP = sb("OWNP", [P, DIG, 2, EG])
        WD = sb("WD", [P, CH, 2])
        DST = sb("DST", [P, CH], I32)
        XG = STORE_A[:, :].rearrange("p (b s n) -> p b s n", b=2, s=DIG)
        TG = sb("TG", [P, 512])
        H1 = sb("H1", [P, 512])
        AH = sb("AH", [P, EG // 2, 2, CAP])
        YT = sb("YT", [P, DIG, DIG, EG // 2, 2])
        YS = ROUTE[:, :, :, :].rearrange("p a n e -> p (a n e)").rearrange("p (c d) -> p c d", d=D)
        TS_ = STORE_B[:, 0:1024].rearrange("p (c n) -> p c n", c=2)
        HS = STORE_B[:, 1024:2048].rearrange("p (c n) -> p c n", c=2)
        SH = sb("SH", [P, 4, D])
        PART = YS[:, 0:2 * TOPK, :].rearrange("p (b k) d -> p b (k d)", b=2)
        HALF = sb("HALF", [P, 512])
        QUARTER = sb("QUARTER", [P, 256])
        YSUM = sb("YSUM", [P, 2, D])
        STATS_T = sb("STATS_T", [P, 2, 6])
        MV_T = sb("MV_T", [P, 2, 2])
        VAR_T = sb("VAR_T", [P, 2, 1])
        RS_T = sb("RS_T", [P, 2, 1])
        minus_half = sb("minus_half", [P, 1])
        ZERO = PART[:, 0, :]
        WF = sb("WF", [P, D])
        FWT = sb("FWT", [P, D])
        FVC = sb("FVC", [32, 2, D])
        zrow = sb("zrow", [1, ROW])
        OT = EGU[:, 0:8, :].rearrange("p (b n) d -> p b n d", b=2)

        ld_con, ld_w, ld_b, ld_moe, ld_ffn = (sem(n) for n in ("ld_con", "ld_w", "ld_b", "ld_moe", "ld_ffn"))
        ld_x = [sem(f"ld_x{m}") for m in range(4)]
        ld_w0, sel_zero, vm_zero, sel_set = sem("ld_w0"), sem("sel_zero"), sem("vm_zero"), sem("sel_set")
        cx_in = [sem("cx_in0"), sem("cx_in1")]
        const_set, dve_set, bias_mm, bias_set = sem("const_set"), sem("dve_set"), sem("bias_mm"), sem("bias_set")
        gates_done = sem("gates_done")
        max_mm, max_got, score_mm, exp_done, pv_mm = (sem(n) for n in ("max_mm", "max_got", "score_mm", "exp_done", "pv_mm"))
        xn_done, tr_mm, xc_done = sem("xn_done"), sem("tr_mm"), sem("xc_done")
        qk_mm, hi_done, split_done = sem("qk_mm"), sem("hi_done"), sem("split_done")
        qs_mm, q_stacked, q_masked = sem("qs_mm"), sem("q_stacked"), sem("q_masked")
        ks_mm, k_stacked = sem("ks_mm"), sem("k_stacked")
        v_mm, v_done = sem("v_mm"), sem("v_done")
        recip_done, ctx_done, o_mm, x_done, stat_done, mv_done = (
            sem(n) for n in ("recip_done", "ctx_done", "o_mm", "x_done", "stat_done", "mv_done"))
        aggr_done, rs_step = sem("aggr_done"), sem("rs_step")
        zero_set, zero_st = sem("zero_set"), sem("zero_st")
        m_xn, m_tr, m_xt = sem("m_xn"), sem("m_tr"), sem("m_xt")
        m_lg, m_lgc, m_sub, m_exp, m_step, m_mask = (sem(n) for n in ("m_lg", "m_lgc", "m_sub", "m_exp", "m_step", "m_mask"))
        m_scan, m_w, m_dest, m_raw, m_slot = sem("m_scan"), sem("m_w"), sem("m_dest"), sem("m_raw"), sem("m_slot")
        m_pos, m_hot, m_ids, m_idx = sem("m_pos"), sem("m_hot"), sem("m_ids"), sem("m_idx")
        m_tab, m_tabw = sem("m_tab"), sem("m_tabw")
        g_in = [sem(f"g_in{g}") for g in range(NG)]
        g_tr, g_xt, g_up, g_tanh, g_h1, g_act, g_dn, g_yt, g_bk, g_ys, g_wd, g_own = (
            sem(n) for n in ("g_tr", "g_xt", "g_up", "g_tanh", "g_h1", "g_act", "g_dn", "g_yt", "g_bk", "g_ys", "g_wd", "g_own"))
        y_st = sem("y_st")
        h_mm, h_tanh, h_h1, h_act, h_dn, h_sh, h_x = (sem(n) for n in ("h_mm", "h_tanh", "h_h1", "h_act", "h_dn", "h_sh", "h_x"))
        p_in = [sem("p_in0"), sem("p_in1")]
        p_step, p_sum, p_x, p_stat, p_aggr, p_var, p_rs = (
            sem(n) for n in ("p_step", "p_sum", "p_x", "p_stat", "p_aggr", "p_var", "p_rs"))
        f_w, f_wf, f_xn, f_tr, f_xt, f_mm, f_x = (sem(n) for n in ("f_w", "f_wf", "f_xn", "f_tr", "f_xt", "f_mm", "f_x"))
        f_st = [sem("f_st0"), sem("f_st1")]

        x_v = x.rearrange("(n p) d -> p n d", p=P)
        ctx_v = ctx.rearrange("(n p) d -> n p d", p=P)
        out_v = out.rearrange("(m n p) d -> m p n d", p=P, n=4)
        parts_z = parts.rearrange("(b a r) d -> b a (r d)", b=NB, a=P)
        egu_v = egu.rearrange("(b e) h f -> b h e f", b=NB)
        edown_v = edown.rearrange("(b k u) i h -> b (u i) k h", b=NB, u=2)
        parts_v = parts.rearrange("(n p k) d -> n p (k d)", p=P, k=TOPK)

        def wait(eng, semaphore, value):
            if isinstance(value, int) and value <= 0:
                return
            eng.wait_ge(semaphore, value)

        def over_batches(eng, layer, step, peeled=1):
            def pair(i, last):
                for p in range(2):
                    step(i, p, NB * layer + 2 * i + p, last)
            pair(0, False)
            with eng.Fori(1, NB // 2 - peeled) as i:
                pair(i, False)
            for i in range(NB // 2 - peeled, NB // 2):
                pair(i, i == NB // 2 - 1)

        block = es.enter_context(nc.Block())

        @block.sync
        def _(sp):
            sp.dma_start(X[:, 0:4, :], x_v[:, 0:4, :]).then_inc(ld_x[0], 16)
            sp.dma_start(CON[:, :], consts).then_inc(ld_con, 16)

            def ctx_tile(i, p, B, last):
                wait(sp, tr_mm, B - 1)
                b = i * 2 + p
                sp.dma_start(CXB[:, p, :], ctx_v[b, :, :]).then_inc(cx_in[p], 16)

            for p in range(2):
                ctx_tile(0, p, p, False)
            for m in range(1, 4):
                sp.dma_start(X[:, 4 * m:4 * m + 4, :], x_v[:, 4 * m:4 * m + 4, :]).then_inc(ld_x[m], 16)
            sp.dma_start(GW[:, :], gate_w).then_inc(ld_moe, 16)
            sp.dma_start(SGU[:, :], sgu).then_inc(ld_moe, 16)
            sp.dma_start(SD[:, :, :], sdown.rearrange("(c p) d -> p c d", p=P)).then_inc(ld_moe, 16)
            sp.wait_ge(zero_set, 2)
            sp.dma_start(table[0:1, :], zrow[:, :]).then_inc(zero_st, 16)

            def later_loads(b):
                ne, nk = EXPERTS // NB, EXPERTS // 2 // NB
                sp.dma_start(EGU[:, bass.ds(b * ne, ne), :], egu_v[b, :, :, :]).then_inc(ld_moe, 16)
                sp.dma_start(ED[:, bass.ds(b * nk, nk), :], edown_v[b, :, :, :]).then_inc(ld_moe, 16)
                sp.dma_start(parts_z[b, :, :], ZERO).then_inc(zero_st, 16)

            for b in range(2):
                later_loads(b)
            with sp.Fori(1, NB // 2) as i:
                for p in range(2):
                    ctx_tile(i, p, i * 2 + p, False)
                    later_loads(i * 2 + p)

            rows_v = table[1:T + 1, :].rearrange("(n p) r -> p n r", p=P)
            sp.wait_ge(m_xn, 4)
            sp.dma_start(rows_v[:, :, 0:D], TB[:, :, 0:D]).then_inc(m_tabw, 16)
            sp.wait_ge(m_w, 1)
            sp.wait_ge(m_dest, 1)
            sp.dma_start(rows_v[:, :, D:ROW], TB[:, :, D:ROW]).then_inc(m_tabw, 16)

            for p in range(2):
                ctx_tile(0, p, NB + p, False)

            sp.wait_ge(y_st, 16 * CH)

            def parts_tile(i, p, n):
                wait(sp, p_step, 2 * n - 3)
                sp.dma_start(PART[:, p, :], parts_v[i * 2 + p, :, :]).then_inc(p_in[p], 16)

            for p in range(2):
                parts_tile(0, p, p)
            with sp.Fori(1, NB // 2) as i:
                for p in range(2):
                    parts_tile(i, p, i * 2 + p)
                    ctx_tile(i, p, i * 2 + (NB + p), False)
            for m in range(4):
                sp.wait_ge(f_x, m + 1)
                sp.dma_start(out_v[m], OT[:, m % 2, :, :]).then_inc(f_st[m % 2], 16)
            for s in f_st:
                sp.wait_ge(s, 32)

        @block.gpsimd
        def _(pool):
            pool.memset(ones_b[:, :], 1.0).then_inc(const_set, 1)
            pool.memset(SEL[:, :, :, :, :], 0.0).then_inc(sel_zero, 1)
            pool.memset(VM[:, :, :, :], 0.0).then_inc(vm_zero, 1)
            pool.memset(ones_d[:, :, :], 0.0).then_inc(const_set, 1)
            pool.wait_ge(const_set, 2)
            for g in range(G):
                pool.memset(ones_d[:, g, g * DH:(g + 1) * DH], 1.0).then_inc(const_set, 1)
            pool.memset(B3[:, :], 0.0).then_inc(const_set, 1)
            pool.memset(zrow[:, :], float(T * TOPK)).then_inc(const_set, 1)
            pool.memset(minus_half[:, :], -0.5).then_inc(p_rs, 1)
            pool.memset(AH[:, :, :, :], 0.0).then_inc(const_set, 1)

            pool.memset(ZERO, 0.0).then_inc(zero_set, 1)
            pool.wait_ge(const_set, 9)
            pool.memset(zrow[:, 0:D + EXPERTS], 0.0).then_inc(zero_set, 1)

            pool.wait_ge(m_scan, 1)
            pool.tensor_tensor(TB[:, :, D + EXPERTS:ROW], COUNT[:, :, :],
                               CON[:, C_TOK8:C_TOK8 + NB].rearrange("p (n o) -> p n o", o=1).to_broadcast([P, NB, EXPERTS]),
                               ALU.add).then_inc(m_dest, 1)
            pool.wait_ge(zero_st, 16 * (NB + 1))
            pool.wait_ge(m_tabw, 32)
            for g in range(NG):
                pool.wait_ge(m_idx, 1)
                for s in range(DIG):
                    c = g * DIG + s
                    pool.indirect_dma_start(GA[:, c, :], None, table[:, :],
                                            bass.IndirectOffsetOnAxis(ap=IDI[:, c:c + 1], axis=0)).then_inc(g_in[g], 16)
            for g in range(NG):
                pool.wait_ge(g_wd, g + 1)
                for s in range(DIG):
                    c = g * DIG + s
                    pool.wait_ge(g_ys, 2 * g + s // 4 + 1)
                    pool.indirect_dma_start(parts[:, :], bass.IndirectOffsetOnAxis(ap=DST[:, c:c + 1], axis=0),
                                            YS[:, c, :], None, bounds_check=T * TOPK - 1,
                                            oob_is_err=False).then_inc(y_st, 16)

            def tile_sum(i, p, n):
                pool.wait_ge(p_in[p], i * 16 + 16)
                wait(pool, p_sum, n)
                pool.tensor_tensor(HALF[:, :], PART[:, p, 0:512], PART[:, p, 512:1024], ALU.add).then_inc(p_step, 1)
                pool.wait_ge(p_step, n * 2 + 1)
                pool.tensor_tensor(QUARTER[:, :], HALF[:, 0:256], HALF[:, 256:512], ALU.add).then_inc(p_step, 1)
                pool.wait_ge(p_step, n * 2 + 2)
                wait(pool, p_x, n - 1)
                pool.tensor_tensor(YSUM[:, p, :], QUARTER[:, 0:128], QUARTER[:, 128:256], ALU.add).then_inc(p_sum, 1)

            def tile_rsqrt(p, n):
                pool.wait_ge(p_var, n + 1)
                wait(pool, xn_done, n + (NB - 1))
                pool.tensor_tensor(RS_T[:, p, :], VAR_T[:, p, :], minus_half[:, :], ALU.pow).then_inc(p_rs, 1)

            for p in range(2):
                tile_sum(0, p, p)
            with pool.Fori(1, NB // 2) as i:
                for p in range(2):
                    tile_rsqrt(p, i * 2 + (p - 2))
                    tile_sum(i, p, i * 2 + p)
            for p in range(2):
                tile_rsqrt(p, NB - 2 + p)

        @block.tensor
        def _(pe):
            def output_biases():
                pe.wait_ge(ld_w, 16)
                pe.wait_ge(ld_ffn, 48)
                for layer in range(2):
                    pe.matmul(bank[6][:, layer * D:(layer + 1) * D], BC[:, layer, 2:3].to_broadcast([P, P]),
                              W[:, layer, 3, :], start=True, stop=True)
                pe.matmul(bank[6][:, 2 * D:3 * D], FVC[:, 0, :], FVC[:, 1, :], start=True, stop=True).then_inc(bias_mm, 1)

            def transposes(layer, i, p, B):
                wait(pe, xn_done, B + 1)
                pe.wait_ge(cx_in[p], i * 16 + (NB // 2 * layer + 1) * 16)
                wait(pe, split_done, B)
                wait(pe, x_done, B - 3)
                pe.transpose(bank[7][:, 0:D], XN[:, p, :], ident)
                pe.transpose(bank[7][:, D:2 * D], CXB[:, p, :], ident).then_inc(tr_mm, 1)

            def v_project(layer, p, B):
                pe.matmul(bank[7][:, 0:D], XC[:, p, D:2 * D], W[:, layer, 2, :], start=True, stop=True).then_inc(v_mm, 1)

            def qk_project(layer, p, B):
                wait(pe, xc_done, B + 1)
                for which in range(2):
                    mm = pe.matmul(bank[7][:, (1 + which) * D:(2 + which) * D], W[:, layer, which, :],
                                   XC[:, p, which * D:(which + 1) * D], start=True, stop=True)
                mm.then_inc(qk_mm, 1)

            def stack(which, done):
                for g in range(G):
                    for part in range(2):
                        mm = pe.matmul(bank[4][:, g * P:(g + 1) * P], SEL[:, which, part, g, :], HL[:, which, part, :],
                                       start=(part == 0), stop=(part == 1))
                mm.then_inc(done, 1)

            def q_stack(B):
                wait(pe, split_done, B + 1)
                wait(pe, k_stacked, B)
                stack(0, qs_mm)

            def k_stack(B):
                wait(pe, q_stacked, B + 1)
                stack(1, ks_mm)

            def max_pass(p, g, B):
                if g == 0:
                    wait(pe, q_masked, B + 1)
                    wait(pe, k_stacked, B + 1)
                wait(pe, max_got, B * 4 + (g - 1))
                for j in range(J):
                    mm = pe.matmul(bank[g % 2][:, j * P:(j + 1) * P], QM[:, p, g, j, :], KS[:, p, g, :],
                                   start=True, stop=True)
                mm.then_inc(max_mm, 1)

            def scores(p, g, B):
                wait(pe, exp_done, B * 4 + (g - 1))
                t = bank[2 + g % 2]
                pe.matmul(t[:, :], KS[:, p, g, :], QM[:, p, g, :, :], start=True, stop=False)
                wait(pe, max_got, B * 4 + (g + 1))
                for j in range(J):
                    mm = pe.matmul(t[:, j * P:(j + 1) * P], NM[:, g, j:j + 1].to_broadcast([P, P]), negid_b[:, :],
                                   start=False, stop=(j == J - 1))
                mm.then_inc(score_mm, 1)

            def weighted(p, g, B):
                if g == 0:
                    wait(pe, ctx_done, B - 1)
                    wait(pe, v_done, B + 1)
                wait(pe, exp_done, B * 4 + (g + 1))
                acc = bank[5 + p]
                for j in range(J):
                    pe.matmul(acc[32 * j:32 * j + 32, 0:P], VM[:, p, g, 32 * j:32 * j + 32],
                              E[:, g, j * P:(j + 1) * P], start=(g == 0), stop=(g == G - 1), skip_group_check=True)
                for j in range(J):
                    mm = pe.matmul(acc[32 * j:32 * j + 32, P:2 * P], ones_d[:, g, :], E[:, g, j * P:(j + 1) * P],
                                   start=False, stop=(g == G - 1), skip_group_check=True)
                mm.then_inc(pv_mm, 1)

            def o_project(layer, p, B, read, value):
                wait(pe, ctx_done, B + 1)
                wait(pe, read, value)
                off = layer * D
                pe.matmul(bank[7][:, 0:D], CN[:, p, :], W[:, layer, 3, :], start=True, stop=False)
                pe.matmul(bank[7][:, 0:D], ones_b[:, :], B3[:, off:off + D], start=False, stop=True).then_inc(o_mm, 1)

            def attention(layer):
                B0 = NB * layer
                pe.wait_ge(ld_con, 16)
                transposes(layer, 0, 0, B0)
                if layer == 0:
                    pe.wait_ge(ld_w0, 32)
                else:
                    pe.wait_ge(ld_w, 16)
                qk_project(layer, 0, B0)
                v_project(layer, 0, B0)
                transposes(layer, 0, 1, B0 + 1)
                if layer == 0:
                    pe.wait_ge(sel_set, 1)
                q_stack(B0)
                k_stack(B0)
                qk_project(layer, 1, B0 + 1)
                if layer == 0:
                    pe.wait_ge(const_set, 9)
                q_stack(B0 + 1)
                max_pass(0, 0, B0)
                max_pass(0, 1, B0)
                scores(0, 0, B0)

                def step(i, p, B, last):
                    q = 1 - p
                    end = last and p == 1
                    first = isinstance(i, int) and i == 0 and p == 0
                    for g in range(G):
                        if layer == 0 and isinstance(i, int) and B == 1 and g == 1:
                            pe.wait_ge(bias_set, 3)
                        if g < 2:
                            max_pass(p, g + 2, B)
                        elif not end:
                            max_pass(q, g - 2, B + 1)
                        if g < 3:
                            scores(p, g + 1, B)
                        elif not end:
                            scores(q, 0, B + 1)
                        if g == 3 and not first:
                            if not last:
                                o_project(layer, q, B - 1, split_done, B + 3)
                            elif p == 0:
                                o_project(layer, q, B - 1, v_done, B + 2)
                            else:
                                o_project(layer, q, B - 1, x_done, B - 1)
                        if g > 0:
                            weighted(p, g - 1, B)
                        elif not first:
                            weighted(q, G - 1, B - 1)
                        if g == 0 and not last:
                            transposes(layer, i + 1, p, B + 2)
                        if g == 0 and not end:
                            k_stack(B + 1)
                        if g == 1 and not last:
                            qk_project(layer, p, B + 2)
                        if g == 1 and not end:
                            if last:
                                wait(pe, x_done, B - 1)
                            v_project(layer, q, B + 1)
                        if g == 3 and not last:
                            q_stack(B + 2)
                        if layer == 0 and first and g == 3:
                            output_biases()

                over_batches(pe, layer, step)
                weighted(1, G - 1, B0 + NB - 1)
                o_project(layer, 1, B0 + NB - 1, x_done, B0 + NB - 1)

            attention(0)

            for m in range(4):
                pe.wait_ge(m_xn, m + 1)
                pe.wait_ge(x_done, NB)
                for n in range(4):
                    mm = pe.transpose(bank[m][:, n * P:(n + 1) * P], TB[:, 4 * m + n, 0:D], ident)
                mm.then_inc(m_tr, 1)
            pe.wait_ge(ld_moe, 16 * (3 + 2 * NB))
            for m in range(4):
                pe.wait_ge(m_xt, m + 1)
                for n in range(4):
                    t = 4 * m + n
                    mm = pe.matmul(bank[4 + m][:, n * 65:(n + 1) * 65], XNT[:, t * P:(t + 1) * P], GW[:, :],
                                   start=True, stop=True)
                mm.then_inc(m_lg, 1)

            def shared_up(m, c):
                for w in range(2):
                    pe.matmul(bank[4 * c + w][:, :], SGU[:, (2 * w + c) * P:(2 * w + c + 1) * P],
                              XNT[:, m * 512:(m + 1) * 512], start=True, stop=True).then_inc(h_mm, 1)

            def shared_down(m):
                pe.wait_ge(h_act, 2 * m + 2)
                for n in range(4):
                    for c in range(2):
                        mm = pe.matmul(bank[4][:, n * P:(n + 1) * P], HS[:, c, n * P:(n + 1) * P], SD[:, c, :],
                                       start=(c == 0), stop=(c == 1))
                mm.then_inc(h_dn, 1)

            pe.wait_ge(m_xt, 4)
            for h in range(2):
                chosen = MASK[:, 8 * h:8 * h + 8, :]
                pe.wait_ge(m_mask, 2)
                if h == 0:
                    pe.matmul(bank[h][:, :], tri_b[:, :], chosen, start=True, stop=False)
                for t in range(8 * h + 7):
                    if t == 8:
                        pe.wait_ge(m_mask, 4)
                    lo = max(8 * h, t + 1)
                    n = 8 * h + 8 - lo
                    pe.matmul(bank[h][:, (lo - 8 * h) * 64:512], ones_b[:, :],
                              MASK[:, t:t + 1, :].to_broadcast([P, n, 64]), start=(h == 1 and t == 0), stop=False)
                if h == 1:
                    pe.matmul(bank[h][:, :], tri_b[:, :], chosen, start=False, stop=False)
                pe.matmul(bank[h][:, :], off_b[:, :], chosen, start=False, stop=True).then_inc(m_pos, 1)
            pe.wait_ge(m_lgc, 4)
            for t in range(NB):
                pe.wait_ge(m_hot, t + 1)
                for g in range(NG):
                    mm = pe.matmul(bank[5][:, g * P:(g + 1) * P], HOT[:, 0, t, g, :, :],
                                   HOT[:, 1, t, g, :, :], start=(t == 0 and g == 0),
                                   stop=(t == NB - 1), skip_group_check=True)
            mm.then_inc(m_ids, 1)

            def expert_in(g):
                pe.wait_ge(g_in[g], 16 * DIG)
                for h in range(2):
                    if g == 3:
                        pe.wait_ge(g_xt, 2 * g - 1 + h)
                    elif g > 0:
                        pe.wait_ge(g_ys, 2 * (g - 1) + h + 1)
                    for s in range(4):
                        mm = pe.transpose(bank[6 + h][:, s * P:(s + 1) * P], GA[:, g * DIG + 4 * h + s, 0:D], ident)
                    mm.then_inc(g_tr, 1)

            def expert_up(g):
                pe.wait_ge(g_xt, 2 * g + 2)
                wait(pe, g_act, g)
                for k in range(EG // 2):
                    for w in range(2):
                        for u in range(2):
                            e = 2 * k + u
                            mm = pe.matmul(bank[2 + w][64 * u:64 * u + 64, k * CAP:(k + 1) * CAP],
                                           EGU[:, EG * g + e, w * FE:(w + 1) * FE],
                                           XG[:, g % 2, :, :].rearrange("p s (a e) -> p s a e", e=EG)[:, :, :, e],
                                           start=True, stop=True)
                mm.then_inc(g_up, 1)

            def expert_down(g):
                pe.wait_ge(g_act, g + 1)
                wait(pe, g_yt, g)
                for k in range(EG // 2):
                    mm = pe.matmul(bank[k // 4][:, k % 4 * P:(k % 4 + 1) * P], ED[:, g * (EG // 2) + k, :],
                                   AH[:, k, :, :], start=True, stop=True)
                mm.then_inc(g_dn, 1)

            def expert_back(g):
                pe.wait_ge(g_yt, g + 1)
                for h in range(2):
                    wait(pe, g_ys, 2 * (g - 1) + h + 1)
                    for s in range(4):
                        mm = pe.transpose(bank[6 + h][:, s * P:(s + 1) * P],
                                          YT[:, 4 * h + s, :, :, :].rearrange("p a k u -> p (a k u)"), ident)
                    mm.then_inc(g_bk, 1)

            pe.wait_ge(m_slot, 2)
            shared_up(0, 0)
            pe.wait_ge(m_idx, 1)
            shared_up(0, 1)
            pe.wait_ge(h_act, 1)
            shared_up(1, 0)
            shared_down(0)
            pe.wait_ge(h_sh, 1)
            shared_up(1, 1)
            pe.wait_ge(h_act, 3)
            shared_up(2, 0)
            shared_down(1)
            expert_in(0)
            pe.wait_ge(h_sh, 2)
            shared_up(2, 1)
            expert_up(0)
            shared_down(2)
            expert_down(0)
            expert_back(0)
            expert_in(1)
            pe.wait_ge(g_yt, 1)
            shared_up(3, 0)
            expert_up(1)
            pe.wait_ge(h_sh, 3)
            shared_up(3, 1)
            pe.wait_ge(h_act, 7)
            expert_down(1)
            shared_down(3)
            expert_back(1)
            expert_in(2)
            expert_up(2)
            expert_in(3)
            expert_down(2)
            expert_up(3)
            expert_back(2)
            expert_down(3)
            expert_back(3)

            pe.wait_ge(g_xt, 2 * NG)
            pe.wait_ge(g_ys, 2 * NG)
            attention(1)

            for m in range(4):
                pe.wait_ge(f_xn, m + 1)
                if m >= 2:
                    pe.wait_ge(f_xt, m - 1)
                pe.wait_ge(x_done, 2 * NB)
                for n in range(4):
                    mm = pe.transpose(bank[m % 2][:, n * P:(n + 1) * P], TB[:, 4 * m + n, 0:D], ident)
                mm.then_inc(f_tr, 1)
                pe.wait_ge(f_xt, m + 1)
                if m >= 2:
                    pe.wait_ge(f_x, m - 1)
                for n in range(4):
                    t = 4 * m + n
                    pe.matmul(bank[2 + m % 2][:, n * P:(n + 1) * P], XNT[:, t * P:(t + 1) * P], WF[:, :],
                              start=True, stop=False)
                    mm = pe.matmul(bank[2 + m % 2][:, n * P:(n + 1) * P], ones_b[:, :], B3[:, 2 * D:NBO],
                                   start=False, stop=True)
                mm.then_inc(f_mm, 1)

        @block.scalar
        def _(act):
            act.dma_start(W[:, 0, :, :], wqkvo[:, 0, :, :]).then_inc(ld_w0, 16)
            act.dma_start(BC[:, :, :], bcol).then_inc(ld_w0, 16)
            act.dma_start(W[:, 1, :, :], wqkvo[:, 1, :, :]).then_inc(ld_w, 16)
            act.dma_start(GT[:, :], gates.rearrange("(a n) -> a n", a=1).to_broadcast([P, 4])).then_inc(ld_b, 16)
            act.dma_start(BR[:, :], brow.rearrange("(a n) -> a n", a=1).to_broadcast([P, NBO])).then_inc(ld_b, 16)
            act.dma_start(FWT[:, :], ffn_wt).then_inc(ld_ffn, 16)
            act.dma_start(FVC[:, 0, :], ffn_vt).then_inc(ld_ffn, 16)
            act.dma_start(FVC[:, 1, :], ffn_ct).then_inc(ld_ffn, 16)
            act.wait_ge(ld_b, 32)
            act.activation(TH[:, :], GT[:, :], ACT.Tanh).then_inc(gates_done, 1)

            def transposed(p, B):
                wait(act, tr_mm, B + 1)
                wait(act, v_mm, B - 1)
                act.activation(XC[:, p, :], bank[7][:, 0:2 * D], ACT.Copy).then_inc(xc_done, 1)

            def values(p, B):
                wait(act, v_mm, B + 1)
                wait(act, pv_mm, B * 4 - 4)
                act.activation(VM_blocks[p], bank[7][:, 0:D].rearrange("p (j g d) -> p j g d", j=J, g=G),
                               ACT.Copy).then_inc(v_done, 1)

            def high_parts(layer, B):
                wait(act, qk_mm, B + 1)
                wait(act, ks_mm, B)
                act.activation(HL[:, 0, 0, :], bank[7][:, D:2 * D], ACT.Identity, bias=BC[:, layer, 0:1])
                act.activation(HL[:, 1, 0, :], bank[7][:, 2 * D:3 * D], ACT.Identity,
                               bias=BC[:, layer, 1:2]).then_inc(hi_done, 1)

            def q_stack_out(B):
                wait(act, qs_mm, B + 1)
                wait(act, q_masked, B)
                act.activation(QS[:, :], bank[4][:, :], ACT.Copy).then_inc(q_stacked, 1)

            def k_stack_out(p, B):
                wait(act, ks_mm, B + 1)
                wait(act, score_mm, B * 4 - 4)
                act.activation(KS[:, p, :, :].rearrange("p g k -> p (g k)"), bank[4][:, :],
                               ACT.Copy).then_inc(k_stacked, 1)

            def exponentials(g, B):
                wait(act, score_mm, B * 4 + (g + 1))
                wait(act, pv_mm, B * 4 + (g - 3))
                act.activation(E[:, g, :], bank[2 + g % 2][:, :], ACT.Exp, scale=SCALE).then_inc(exp_done, 1)

            def attention(layer):
                B0 = NB * layer
                transposed(0, B0)
                if layer == 0:
                    act.wait_ge(vm_zero, 1)
                    act.wait_ge(ld_w0, 32)
                values(0, B0)
                high_parts(layer, B0)
                transposed(1, B0 + 1)
                q_stack_out(B0)
                k_stack_out(0, B0)
                high_parts(layer, B0 + 1)
                exponentials(0, B0)

                def step(i, p, B, last):
                    end = last and p == 1
                    q = 1 - p
                    for g in range(G):
                        if g == 0 and not end:
                            q_stack_out(B + 1)
                        if g < 3:
                            exponentials(g + 1, B)
                        elif not end:
                            exponentials(0, B + 1)
                        if g == 0 and not last:
                            transposed(p, B + 2)
                        if g == 0 and not end:
                            k_stack_out(q, B + 1)
                        if g == 1 and not end:
                            values(q, B + 1)
                        if g == 1 and not last:
                            high_parts(layer, B + 2)

                over_batches(act, layer, step)

            attention(0)

            for m in range(4):
                act.wait_ge(m_tr, m + 1)
                act.activation(XNT[:, m * 512:(m + 1) * 512], bank[m][:, :], ACT.Copy).then_inc(m_xt, 1)
            for m in range(4):
                act.wait_ge(m_sub, m + 1)
                act.activation(LM[:, 4 * m:4 * m + 4, :], LM[:, 4 * m:4 * m + 4, :], ACT.Exp).then_inc(m_exp, 1)
            act.activation(SG[:, :], SG[:, :], ACT.Tanh, scale=0.5).then_inc(m_exp, 1)
            for t in range(NB):
                act.wait_ge(m_raw, t + 1)
                act.activation(HOT[:, 1, t, :, :, :], HOT[:, 1, t, :, :, :], ACT.Copy,
                               scale=CON[:, C_TOK + t:C_TOK + t + 1]).then_inc(m_hot, 1)

            def shared_tanh(m, c):
                act.wait_ge(h_mm, 4 * m + 2 * c + 1)
                wait(act, h_h1, 2 * (m - 1) + c + 1)
                act.activation(TS_[:, c, :], bank[4 * c][:, :], ACT.Tanh, scale=0.5).then_inc(h_tanh, 1)

            def expert_in(g):
                for h in range(2):
                    act.wait_ge(g_tr, 2 * g + h + 1)
                    wait(act, g_up, g - 1)
                    act.activation(XG[:, g % 2, 4 * h:4 * h + 4, :],
                                   bank[6 + h][:, :].rearrange("p (s n) -> p s n", s=4), ACT.Copy).then_inc(g_xt, 1)

            def expert_tanh(g):
                act.wait_ge(g_up, g + 1)
                wait(act, g_h1, g)
                act.activation(TG[:, :], bank[2][:, :], ACT.Tanh, scale=0.5).then_inc(g_tanh, 1)

            def expert_out(g):
                act.wait_ge(g_dn, g + 1)
                wait(act, g_bk, 2 * g)
                for b in range(2):
                    ins = act.activation(YT[:, :, :, :, :].rearrange("p s a k u -> p (s a) k u")[:, :, 4 * b:4 * b + 4, :],
                                         bank[b][:, :].rearrange("p (k u n) -> p n k u", k=4, u=2), ACT.Copy)
                ins.then_inc(g_yt, 1)

            for m, c in ((0, 0), (0, 1), (1, 0), (1, 1), (2, 0)):
                shared_tanh(m, c)
            expert_in(0)
            shared_tanh(2, 1)
            expert_tanh(0)
            expert_out(0)
            expert_in(1)
            shared_tanh(3, 0)
            expert_tanh(1)
            shared_tanh(3, 1)
            expert_out(1)
            expert_in(2)
            expert_tanh(2)
            expert_in(3)
            expert_out(2)
            expert_tanh(3)
            expert_out(3)
            attention(1)
            for m in range(4):
                act.wait_ge(f_tr, m + 1)
                act.activation(XNT[:, m * 512:(m + 1) * 512], bank[m % 2][:, :], ACT.Copy).then_inc(f_xt, 1)

        @block.vector
        def _(dve):
            steps_taken = [0]

            def link(ins):
                steps_taken[0] += 1
                ins.then_inc(rs_step, 1)
                dve.wait_ge(rs_step, steps_taken[0])

            def rsqrt_seed(c):
                link(dve.tensor_scalar(VE[:, c], MV[:, c, 1], EPS, None, ALU.add))
                link(dve.tensor_scalar(RS[:, c].bitcast(I32), VE[:, c].bitcast(I32), -0.5, RSQRT_SEED, ALU.mult, ALU.add))

            def newton_step(c):
                link(dve.tensor_tensor(NW[:, 0, c], RS[:, c], RS[:, c], ALU.mult))
                link(dve.scalar_tensor_tensor(out=NW[:, 1, c], in0=NW[:, 0, c], scalar=-0.5, in1=VE[:, c],
                                              op0=ALU.mult, op1=ALU.mult))
                link(dve.scalar_tensor_tensor(out=RS[:, c], in0=NW[:, 1, c], scalar=1.5, in1=RS[:, c],
                                              op0=ALU.add, op1=ALU.mult))

            def rsqrt_of_variances(lo, hi):
                rsqrt_seed(slice(lo, hi))
                for n in range(3):
                    newton_step(slice(lo, hi))

            def normalised(layer, i, p, B):
                wait(dve, tr_mm, B - 1)
                b = i * 2 + p
                if layer == 0:
                    mean, scale = MV[:, b, 0:1], RS3[:, b, :]
                else:
                    dve.wait_ge(p_rs, B + (2 - NB))
                    mean, scale = MV_T[:, p, 0:1], RS_T[:, p, :]
                dve.tensor_scalar(XN[:, p, :], X[:, b, :], mean, scale, ALU.subtract, ALU.mult).then_inc(xn_done, 1)

            def tile_add(i, p, n):
                dve.wait_ge(p_sum, n + 1)
                b = i * 2 + p
                dve.scalar_tensor_tensor(out=X[:, b, :], in0=YSUM[:, p, :], scalar=1.0, in1=X[:, b, :],
                                         op0=ALU.mult, op1=ALU.add).then_inc(p_x, 1)

            def before_tile_statistics(n):
                dve.wait_ge(p_x, n + 1)
                wait(dve, p_aggr, n - 1)

            def tile_statistics(i, p, n):
                dve.bn_stats(STATS_T[:, p, :], X[:, i * 2 + p, :]).then_inc(p_stat, 1)

            def before_tile_variance(n):
                dve.wait_ge(p_stat, n + 1)
                wait(dve, xn_done, n + (NB - 1))

            def tile_variance(p, n):
                dve.bn_aggr(MV_T[:, p, :], STATS_T[:, p, :]).then_inc(p_aggr, 1)

            def tile_variance_out(p, n):
                dve.wait_ge(p_aggr, n + 1)
                wait(dve, p_rs, n)
                dve.tensor_scalar(VAR_T[:, p, :], MV_T[:, p, 1:2], EPS, None, ALU.add).then_inc(p_var, 1)

            def input_statistics(lo, hi):
                for n in range(lo, hi + 1):
                    if n < hi:
                        if n >= 2:
                            dve.wait_ge(mv_done, n - 1)
                        dve.bn_stats(STATS[:, n % 2, :], X[:, n, :]).then_inc(stat_done, 1)
                    if n > lo:
                        dve.wait_ge(stat_done, n)
                        dve.bn_aggr(MV[:, n - 1, :], STATS[:, (n - 1) % 2, :]).then_inc(mv_done, 1)

            dve.wait_ge(ld_x[0], 16)
            input_statistics(0, 4)
            dve.wait_ge(mv_done, 4)
            rsqrt_of_variances(0, 4)
            for p in range(2):
                normalised(0, 0, p, p)
            dve.wait_ge(ld_con, 16)
            dve.tensor_scalar(negid_b[:, :], ident, -1.0, None, ALU.mult).then_inc(dve_set, 1)
            dve.tensor_copy(tri_b[:, :], CON[:, C_TRI:C_TRI + P])
            dve.tensor_scalar(off_b[:, :], ident, -float(CAP), None, ALU.mult)
            dve.tensor_copy(DIGS[:, :, :, :], CON[:, C_DIG:C_DIG + DIG].rearrange("p (g s o) -> p g s o", g=1, o=1)
                            .to_broadcast([P, NG, DIG, EG])).then_inc(dve_set, 1)
            dve.wait_ge(sel_zero, 1)
            rows = ident.rearrange("p (j g d) -> p g j d", j=J, g=G)
            for part in range(2):
                for t in range(2):
                    for which, term in ((0, 2 * t + part), (1, 2 * part + t)):
                        out_rows = SEL[:, which, part, :, :].rearrange("p g (j t d) -> p g j t d", j=J, t=4)
                        ins = dve.tensor_copy(out_rows[:, :, :, term, :], rows)
            ins.then_inc(sel_set, 1)

            def output_biases():
                dve.wait_ge(bias_mm, 1)
                dve.wait_ge(ld_b, 32)
                dve.tensor_tensor(WF[:, :], bank[6][:, 2 * D:3 * D], FWT[:, :], ALU.add).then_inc(bias_set, 1)
                dve.tensor_tensor(BR[:, 0:2 * D], bank[6][:, 0:2 * D], BR[:, 0:2 * D], ALU.add).then_inc(bias_set, 1)
                dve.wait_ge(bias_set, 2)
                dve.tensor_copy(BR_part[:, 0, :], BR[:, :]).then_inc(dve_set, 1)
                dve.wait_ge(dve_set, 3)
                dve.tensor_tensor(BR_rest[:, :], BR[:, :], BR_part[:, 0, :], ALU.subtract).then_inc(dve_set, 1)
                dve.wait_ge(dve_set, 4)
                dve.tensor_copy(BR_part[:, 1, :], BR_rest[:, :]).then_inc(dve_set, 1)
                dve.wait_ge(dve_set, 5)
                dve.tensor_tensor(BR[:, :], BR_rest[:, :], BR_part[:, 1, :], ALU.subtract).then_inc(dve_set, 1)
                dve.wait_ge(dve_set, 6)
                dve.wait_ge(const_set, 9)
                dve.tensor_copy(B3[0:1, 0:NBO], BR_part[0:1, 0, :])
                dve.tensor_copy(B3[32:33, 0:NBO], BR_part[32:33, 1, :])
                dve.tensor_copy(B3[64:65, 0:NBO], BR[64:65, :]).then_inc(bias_set, 1)

            def maxima(g, B):
                wait(dve, max_mm, B * 4 + (g + 1))
                wait(dve, score_mm, B * 4 + (g - 3))
                dve.tensor_reduce(NM[:, g, :], bank[g % 2][:, :].rearrange("p (j k) -> p j k", j=J), AXX,
                                  ALU.max).then_inc(max_got, 1)

            def low_parts(layer, B):
                wait(dve, hi_done, B + 1)
                for which in range(2):
                    ins = dve.scalar_tensor_tensor(out=HL[:, which, 1, :], in0=bank[7][:, (1 + which) * D:(2 + which) * D],
                                                   scalar=BC[:, layer, which:which + 1], in1=HL[:, which, 0, :],
                                                   op0=ALU.add, op1=ALU.subtract)
                ins.then_inc(split_done, 1)

            def q_mask(p, B):
                wait(dve, q_stacked, B + 1)
                wait(dve, score_mm, B * 4 - 4)
                for j in range(J):
                    ins = dve.tensor_scalar(QM[:, p, :, j, :], QS[:, :].rearrange("p (g q) -> p g q", g=G),
                                            CON[:, C_QUAD + j:C_QUAD + j + 1], None, ALU.mult)
                ins.then_inc(q_masked, 1)

            def reciprocals(p, B):
                wait(dve, pv_mm, B * 4 + 4)
                wait(dve, ctx_done, B)
                dve.reciprocal(RD[:, :], bank[5 + p][:, D:2 * D]).then_inc(recip_done, 1)

            def normalise_context(p, B):
                wait(dve, recip_done, B + 1)
                dve.tensor_tensor(CN[:, p, :], bank[5 + p][:, 0:D], RD[:, :], ALU.mult).then_inc(ctx_done, 1)

            def residual(layer, i, p, B):
                wait(dve, o_mm, B + 1)
                b = i * 2 + p
                dve.scalar_tensor_tensor(out=X[:, b, :], in0=bank[7][:, 0:D], scalar=TH[:, layer:layer + 1],
                                         in1=X[:, b, :], op0=ALU.mult, op1=ALU.add).then_inc(x_done, 1)

            def before_statistics(layer, B):
                wait(dve, x_done, B + 1)
                wait(dve, mv_done, B + (NB - 1))

            def before_mean_variance(layer, B):
                wait(dve, stat_done, B + (NB + 1))
                wait(dve, mv_done, B + NB)

            def statistics(layer, i, p, B):
                dve.bn_stats(STATS[:, p, :], X[:, i * 2 + p, :]).then_inc(stat_done, 1)

            def mean_variance(layer, i, p, B):
                dve.bn_aggr(MV_now[:, :], STATS[:, p, :]).then_inc(aggr_done, 1)

            def keep_mean_variance(layer, i, p, B):
                wait(dve, aggr_done, B + 1)
                dve.tensor_copy(MV[:, i * 2 + p, :], MV_now[:, :]).then_inc(mv_done, 1)

            def attention(layer):
                B0 = NB * layer
                if layer > 0:
                    for n in range(3):
                        tile_add(n // 2, n % 2, n)
                        before_tile_statistics(n)
                        tile_statistics(n // 2, n % 2, n)
                        if n == 2:
                            for p in range(2):
                                normalised(1, 0, p, B0 + p)
                        before_tile_variance(n)
                        tile_variance(n % 2, n)
                        tile_variance_out(n % 2, n)
                low_parts(layer, B0)
                q_mask(0, B0)
                low_parts(layer, B0 + 1)
                maxima(0, B0)
                maxima(1, B0)

                def step(i, p, B, last):
                    q = 1 - p
                    end = last and p == 1
                    first = isinstance(i, int) and i == 0
                    one_back = i - 1 if p == 0 else i
                    alone = first and p == 0
                    arriving = layer == 1 and not last and not (isinstance(i, int) and B + 3 >= 2 * NB)
                    ni, n = i + 1 + p, B + (3 - NB)
                    for g in range(G):
                        if g == 1 and arriving:
                            tile_add(ni, q, n)
                            before_tile_statistics(n)
                        if g == 2 and arriving:
                            before_tile_variance(n)
                        if g == 0 and not last:
                            normalised(layer, i + 1, p, B + 2)
                        if g == 0 and not first:
                            before_statistics(layer, B - 2)
                        if g == 1 and not first:
                            before_mean_variance(layer, B - 2)
                        if g < 2:
                            maxima(g + 2, B)
                        elif not end:
                            maxima(g - 2, B + 1)
                        if g == 0 and not end:
                            q_mask(q, B + 1)
                        if g == 1 and not first:
                            mean_variance(layer, i - 1, p, B - 2)
                        if g == 1 and not alone:
                            reciprocals(q, B - 1)
                        if g == 1 and not first:
                            keep_mean_variance(layer, i - 1, p, B - 2)
                        if g == 1 and not alone:
                            normalise_context(q, B - 1)
                        if g == 1 and arriving:
                            tile_statistics(ni, q, n)
                        if g == 2 and arriving:
                            tile_variance(q, n)
                        if g == 2 and not last:
                            low_parts(layer, B + 2)
                        if g == 2 and arriving:
                            tile_variance_out(q, n)
                        if g == 0 and not first:
                            statistics(layer, i - 1, p, B - 2)
                        if g == 3 and not alone:
                            residual(layer, one_back, q, B - 1)
                        if layer == 0 and alone:
                            if g < 3:
                                dve.wait_ge(ld_x[g + 1], 16)
                                input_statistics(4 * g + 4, 4 * g + 8)
                            else:
                                output_biases()
                        elif layer == 0 and first:
                            if g == 0:
                                dve.wait_ge(mv_done, NB)
                                rsqrt_seed(slice(4, NB))
                            else:
                                newton_step(slice(4, NB))

                over_batches(dve, layer, step, peeled=layer + 1)
                n = NB // 2 - 1
                B1 = B0 + NB - 1
                reciprocals(1, B1)
                normalise_context(1, B1)
                for p in range(2):
                    if p == 1:
                        residual(layer, n, p, B1 - 1 + p)
                    before_statistics(layer, B1 - 1 + p)
                    statistics(layer, n, p, B1 - 1 + p)
                    before_mean_variance(layer, B1 - 1 + p)
                    mean_variance(layer, n, p, B1 - 1 + p)
                    keep_mean_variance(layer, n, p, B1 - 1 + p)
                dve.wait_ge(mv_done, NB * (layer + 2))

            attention(0)

            rsqrt_of_variances(0, NB)
            for t in range(NB):
                ins = dve.tensor_scalar(TB[:, t, 0:D], X[:, t, :], MV[:, t, 0:1], RS[:, t:t + 1], ALU.subtract, ALU.mult)
                if t % 4 == 3:
                    ins.then_inc(m_xn, 1)
            routing_steps = [0]

            def link(ins):
                routing_steps[0] += 1
                ins.then_inc(m_step, 1)
                dve.wait_ge(m_step, routing_steps[0])

            dve.wait_ge(zero_st, 16 * (NB + 1))
            for m in range(4):
                c = slice(4 * m, 4 * m + 4)
                dve.wait_ge(m_lg, m + 1)
                v = bank[4 + m][:, 0:260].rearrange("p (n e) -> p n e", n=4)
                dve.tensor_copy(SG[:, c], v[:, :, EXPERTS])
                dve.tensor_copy(LG[:, c, :], v[:, :, 0:EXPERTS]).then_inc(m_lgc, 1)
                dve.wait_ge(m_lgc, m + 1)
                for t in range(4 * m, 4 * m + 4):
                    ins = dve.max(TOP[:, t, :], LG[:, t, :])
                link(ins)
                for t in range(4 * m, 4 * m + 4):
                    ins = dve.match_replace(POS[:, t, :], TOP[:, t, :], LG[:, t, :], -3.0e38)
                dve.tensor_tensor(LM[:, c, :], LG[:, c, :], TOP[:, c, 0:1].to_broadcast([P, 4, EXPERTS]),
                                  ALU.subtract).then_inc(m_sub, 1)
                dve.wait_ge(m_sub, m + 1)
                dve.tensor_tensor(MASK[:, c, :], POS[:, c, :], LG[:, c, :], ALU.not_equal).then_inc(m_mask, 1)
            dve.wait_ge(m_mask, 4)
            flat = "p n e -> p (n e)"
            dve.tensor_tensor_scan(COUNT[:, :, :].rearrange(flat), MASK[:, :, :].rearrange(flat),
                                   MASK[:, :, :].rearrange(flat), 0.0, ALU.add, ALU.bypass).then_inc(m_scan, 1)
            dve.wait_ge(m_exp, 4)
            link(dve.tensor_tensor(LM[:, :, :], LM[:, :, :], MASK[:, :, :], ALU.mult))
            link(dve.tensor_reduce(SUMS[:, :], LM[:, :, :], AXX, ALU.add))
            link(dve.reciprocal(SUMS[:, :], SUMS[:, :]))
            link(dve.tensor_scalar(SUMS[:, :], SUMS[:, :], TH[:, 2:3], 0.5, ALU.mult, ALU.mult))
            for h in range(2):
                c = slice(8 * h, 8 * h + 8)
                dve.wait_ge(m_pos, h + 1)
                dve.tensor_scalar(SLOT[:, c, :].rearrange(flat), bank[h][:, :], float(CAP), None,
                                  ALU.add).then_inc(m_slot, 1)
                dve.wait_ge(m_slot, h + 1)
                dve.tensor_scalar(LOW[:, c, :], SLOT[:, c, :], DIG - 1, None, ALU.bitwise_and)
                link(dve.tensor_scalar(HI[:, c, :], SLOT[:, c, :], 3, None, ALU.logical_shift_right))
                for t in range(8 * h, 8 * h + 8):
                    for w, digit in ((0, HI), (1, LOW)):
                        of_tile = digit[:, t, :].rearrange("p (g o e) -> p g o e", g=NG, o=1)
                        ins = dve.tensor_tensor(HOT[:, w, t, :, :, :], of_tile.to_broadcast([P, NG, DIG, EG]),
                                                DIGS[:, :, :, :], ALU.is_equal)
                    ins.then_inc(m_raw, 1)
                if h == 0:
                    dve.tensor_tensor(TB[:, :, D:D + EXPERTS], LM[:, :, :],
                                      SUMS[:, :].rearrange("p (n o) -> p n o", o=1).to_broadcast([P, NB, EXPERTS]),
                                      ALU.mult).then_inc(m_w, 1)
            dve.wait_ge(m_ids, 1)
            own = CON[:, C_OWN:C_OWN + EG]
            link(dve.tensor_tensor(IDX[:, :, :, :], bank[5][:, :].rearrange("p (g s e) -> p g s e", g=NG, s=DIG),
                                   own.rearrange("p (o u e) -> p o u e", o=1, u=1).to_broadcast([P, NG, DIG, EG]), ALU.mult))
            link(dve.tensor_reduce(IDF[:, :].rearrange("p (g s) -> p g s", g=NG), IDX[:, :, :, :], AXX, ALU.add))
            dve.tensor_copy(IDI[:, :], IDF[:, :]).then_inc(m_idx, 1)
            dve.wait_ge(m_exp, 5)
            link(dve.tensor_scalar(SG[:, :], SG[:, :], 0.25, 0.25, ALU.mult, ALU.add))

            def shared_hidden(m, c):
                dve.wait_ge(h_tanh, 2 * m + c + 1)
                dve.wait_ge(h_mm, 4 * m + 2 * c + 2)
                wait(dve, h_dn, m)
                dve.scalar_tensor_tensor(out=HS[:, c, :], in0=TS_[:, c, :], scalar=1.0, in1=bank[4 * c][:, :],
                                         op0=ALU.add, op1=ALU.mult).then_inc(h_h1, 1)
                dve.wait_ge(h_h1, 2 * m + c + 1)
                dve.tensor_tensor(HS[:, c, :], HS[:, c, :], bank[4 * c + 1][:, :], ALU.mult).then_inc(h_act, 1)

            def shared_out(m):
                dve.wait_ge(h_dn, m + 1)
                wait(dve, h_x, m)
                dve.tensor_tensor(SH[:, :, :], bank[4][:, :].rearrange("p (n d) -> p n d", n=4),
                                  SG[:, 4 * m:4 * m + 4].rearrange("p (n o) -> p n o", o=1).to_broadcast([P, 4, D]),
                                  ALU.mult).then_inc(h_sh, 1)
                dve.wait_ge(h_sh, m + 1)
                dve.scalar_tensor_tensor(out=X[:, 4 * m:4 * m + 4, :], in0=SH[:, :, :], scalar=TH[:, 2:3],
                                         in1=X[:, 4 * m:4 * m + 4, :], op0=ALU.mult, op1=ALU.add).then_inc(h_x, 1)

            def slot_data(g):
                dve.wait_ge(g_in[g], 16 * DIG)
                mine = GA[:, g * DIG:(g + 1) * DIG, D:ROW].rearrange("p s (w e) -> p s w e", w=2)[:, :, :, EG * g:EG * g + EG]
                link(dve.tensor_tensor(OWNP[:, :, :, :], mine,
                                       own.rearrange("p (o u e) -> p o u e", o=1, u=1).to_broadcast([P, DIG, 2, EG]), ALU.mult))
                link(dve.tensor_reduce(WD[:, g * DIG:(g + 1) * DIG, :], OWNP[:, :, :, :], AXX, ALU.add))
                dve.tensor_copy(DST[:, g * DIG:(g + 1) * DIG], WD[:, g * DIG:(g + 1) * DIG, 1]).then_inc(g_wd, 1)

            def expert_hidden(g):
                dve.wait_ge(g_tanh, g + 1)
                dve.scalar_tensor_tensor(out=H1[:, :], in0=TG[:, :], scalar=1.0, in1=bank[2][:, :],
                                         op0=ALU.add, op1=ALU.mult).then_inc(g_h1, 1)
                dve.wait_ge(g_h1, g + 1)
                wait(dve, g_dn, g)
                for u in range(2):
                    r = slice(64 * u, 64 * u + 64)
                    ins = dve.tensor_tensor(AH[r, :, u, :], H1[r, :].rearrange("p (k n) -> p k n", k=EG // 2),
                                            bank[3][r, :].rearrange("p (k n) -> p k n", k=EG // 2), ALU.mult)
                ins.then_inc(g_act, 1)

            def weighted_outputs(g):
                for h in range(2):
                    dve.wait_ge(g_bk, 2 * g + h + 1)
                    c = g * DIG + 4 * h
                    dve.tensor_tensor(YS[:, c:c + 4, :], bank[6 + h][:, :].rearrange("p (s d) -> p s d", s=4),
                                      WD[:, c:c + 4, 0:1].to_broadcast([P, 4, D]), ALU.mult).then_inc(g_ys, 1)

            shared_hidden(0, 0)
            shared_hidden(0, 1)
            shared_hidden(1, 0)
            shared_out(0)
            shared_hidden(1, 1)
            shared_out(1)
            shared_hidden(2, 0)
            slot_data(0)
            shared_hidden(2, 1)
            expert_hidden(0)
            shared_out(2)
            weighted_outputs(0)
            slot_data(1)
            shared_hidden(3, 0)
            expert_hidden(1)
            shared_hidden(3, 1)
            shared_out(3)
            weighted_outputs(1)
            slot_data(2)
            expert_hidden(2)
            slot_data(3)
            expert_hidden(3)
            weighted_outputs(2)
            weighted_outputs(3)

            attention(1)

            rsqrt_of_variances(0, NB)
            for t in range(NB):
                ins = dve.tensor_scalar(TB[:, t, 0:D], X[:, t, :], MV[:, t, 0:1], RS[:, t:t + 1], ALU.subtract, ALU.mult)
                if t % 4 == 3:
                    ins.then_inc(f_xn, 1)
            for m in range(4):
                dve.wait_ge(f_mm, m + 1)
                if m >= 2:
                    dve.wait_ge(f_st[m % 2], 16)
                dve.scalar_tensor_tensor(out=OT[:, m % 2, :, :].rearrange("p n d -> p (n d)"), in0=bank[2 + m % 2][:, :],
                                         scalar=TH[:, 3:4], in1=X[:, 4 * m:4 * m + 4, :].rearrange("p n d -> p (n d)"),
                                         op0=ALU.mult, op1=ALU.add).then_inc(f_x, 1)


def kernel(x, ctx_1024, g_xattn, g_ffn, L0_xattn_w_q, L0_xattn_b_q, L0_xattn_w_k, L0_xattn_b_k, L0_xattn_w_v,
           L0_xattn_b_v, L0_xattn_w_o, L0_xattn_b_o, L0_ffn_gate_w, L0_ffn_shared_gate_w, L0_ffn_shared_gate_up_w,
           L0_ffn_shared_down_w, L0_ffn_expert_gate_up_w, L0_ffn_expert_down_w, L1_xattn_Wq, L1_xattn_bq,
           L1_xattn_Wk, L1_xattn_bk, L1_xattn_Wv, L1_xattn_bv, L1_xattn_Wo, L1_xattn_bo, L1_ffn_W, L1_ffn_b,
           L1_ffn_V_r, L1_ffn_C):
    import concourse.bacc as bacc
    from concourse.bass_utils import run_bass_kernel_spmd

    a = np.asarray
    layers = [(a(L0_xattn_w_q), a(L0_xattn_w_k), a(L0_xattn_w_v), a(L0_xattn_w_o), a(L0_xattn_b_q), a(L0_xattn_b_k),
               a(L0_xattn_b_v), a(L0_xattn_b_o)),
              (a(L1_xattn_Wq).T, a(L1_xattn_Wk).T, a(L1_xattn_Wv).T, a(L1_xattn_Wo).T, a(L1_xattn_bq), a(L1_xattn_bk),
               a(L1_xattn_bv), a(L1_xattn_bo))]
    data = {
        "x": a(x).reshape(T, D),
        "ctx": a(ctx_1024).reshape(T, D),
        "consts": shape_constants(),
        "wqkvo": np.stack([np.stack(w[0:4], 1) for w in layers], 1),
        "bcol": np.stack([np.stack(w[4:7], 1) for w in layers], 1),
        "brow": np.concatenate([layers[0][7], layers[1][7], a(L1_ffn_b)]),
        "gates": np.concatenate([a(g_xattn), a(g_ffn)]),
        "gate_w": np.concatenate([a(L0_ffn_gate_w), a(L0_ffn_shared_gate_w)], 1),
        "sgu": a(L0_ffn_shared_gate_up_w),
        "sdown": a(L0_ffn_shared_down_w),
        "egu": a(L0_ffn_expert_gate_up_w),
        "edown": a(L0_ffn_expert_down_w),
        "ffn_wt": a(L1_ffn_W).T,
        "ffn_vt": a(L1_ffn_V_r).T,
        "ffn_ct": a(L1_ffn_C).T,
    }
    nc = bacc.Bacc("TRN2", target_bir_lowering=False, num_devices=1)
    arrays, aps = {}, {}
    for name, v in data.items():
        v = np.ascontiguousarray(v)
        arrays[f"in_{name}"] = v
        aps[name] = nc.dram_tensor(f"in_{name}", v.shape, mybir.dt.from_np(v.dtype), kind="ExternalInput").ap()
    out = nc.dram_tensor("out_0", (T, D), F32, kind="ExternalOutput").ap()
    program(nc, out=out, **aps)
    r = run_bass_kernel_spmd(nc, [arrays], core_ids=[0])
    return r.results[0]["out_0"].reshape(NB, P, D)
```

```python
from contextlib import ExitStack

import numpy as np
import concourse.bass as bass
from concourse import mybir

F32 = mybir.dt.float32
F16 = mybir.dt.float16
BF16 = mybir.dt.bfloat16
I32 = mybir.dt.int32
I16 = mybir.dt.int16
ALU = mybir.AluOpType
ACT = mybir.ActivationFunctionType
AXX = mybir.AxisListType.X

P = 128
NB = 16
D = 128
T = NB * P
HEADS, DH = 16, 8
G = 4
J = 4
SCALE = float(DH) ** -0.5
EXPERTS, TOPK, CAP = 64, 8, 64
FE = 64
FS = 256
SLOTS = EXPERTS * CAP
EG = 16
NG = EXPERTS // EG
DIG = 8
CH = NG * DIG
ROW = 256
EPS = 1e-5

C_ID, C_TRI, C_QUAD, C_OWN, C_DIG, C_TOK, C_TOK8 = 0, 128, 256, 260, 276, 284, 300
NCONST = 316


def shape_constants():
    c = np.zeros((P, NCONST), np.float32)
    p = np.arange(P)
    c[:, C_ID:C_ID + P] = np.eye(P)
    c[:, C_TRI:C_TRI + P] = p[:, None] < p[None, :]
    for j in range(J):
        c[:, C_QUAD + j] = p // 32 == j
    c[:, C_OWN:C_OWN + EG] = p[:, None] % EG == np.arange(EG)[None, :]
    c[:, C_DIG:C_DIG + DIG] = np.arange(DIG)
    c[:, C_TOK:C_TOK + NB] = p[:, None] + P * np.arange(NB)[None, :] + 1
    c[:, C_TOK8:C_TOK8 + NB] = TOPK * (p[:, None] + P * np.arange(NB)[None, :]) - TOPK * np.arange(NB)[None, :] - 1
    return c


def program(nc, x, ctx, consts, wqkvo, bcol, brow, gates, gate_w, sgu, sdown, egu, edown,
            ffn_wt, ffn_vt, ffn_ct, out):
    with ExitStack() as es:
        def sb(name, shape, dt=F32):
            return es.enter_context(nc.sbuf_tensor(name, shape, dt))

        def sem(name):
            return es.enter_context(nc.semaphore(name))

        bank = [es.enter_context(nc.psum_tensor(f"bank{i}", [P, 512], F32)) for i in range(8)]
        table = nc.dram_tensor("token_table", (T + 1, ROW), F32).ap()
        parts = nc.dram_tensor("expert_parts", (T * TOPK, D), F32).ap()

        X = sb("X", [P, NB, D])
        CON = sb("CON", [P, NCONST])
        W = sb("W", [P, 2, 4, D])
        BC = sb("BC", [P, 2, 3])
        NBO = 3 * D
        BIG = sb("BIG", [P, 8192])
        BR = BIG[:, 0:NBO]
        BR_rest = BIG[:, NBO:2 * NBO]
        BR_part = BIG[:, 2 * NBO:3 * NBO].bitcast(BF16).rearrange("p (k n) -> p k n", k=2)
        B3 = sb("B3", [P, NBO], BF16)
        GT = sb("GT", [P, 4])
        TH = sb("TH", [P, 4])
        ones_b = sb("ones_b", [P, P], BF16)
        negid_b = sb("negid_b", [P, P], BF16)
        tri_b = sb("tri_b", [P, P], BF16)
        off_b = sb("off_b", [P, P], BF16)
        DIGS = sb("DIGS", [P, NG, DIG, EG], I16)
        ones_d = sb("ones_d", [P, G, 32])
        ident = CON[:, C_ID:C_ID + P]

        CXB = sb("CXB", [P, 2, D])
        XN = sb("XN", [P, 2, D])
        XC = sb("XC", [P, 2, 2 * D])
        HL = sb("HL", [P, 2, 2, P], F16)
        SEL = sb("SEL", [P, 2, 2, G, P], F16)
        QS = sb("QS", [P, 512], F16)
        STORE_A = sb("STORE_A", [P, 2048])
        STORE_B = sb("STORE_B", [P, 2048])
        QM = STORE_A[:, :].bitcast(F16).rearrange("p (b g j q) -> p b g j q", b=2, g=G, j=J)
        KS = sb("KS", [P, 2, G, P], F16)
        VM = sb("VM", [P, 2, G, D])
        VM_p = VM[:, :, :, :].rearrange("p b g d -> p b (g d)")
        VM_blocks = [bass.AP(v.tensor, v.offset, [v.ap[0], [32, J], [D + DH, G], [1, DH]]) for v in (VM_p[:, 0, :], VM_p[:, 1, :])]
        NM = sb("NM", [P, G, J], BF16)
        E = STORE_B[:, :].rearrange("p (g n) -> p g n", g=G)
        RD = sb("RD", [P, D])
        CN = sb("CN", [P, 2, D])
        STATS = sb("STATS", [P, 2, 6])
        MV = sb("MV", [P, NB, 2])
        MV_now = sb("MV_now", [P, 2])
        RS3 = sb("RS3", [P, NB, 1])
        RS = RS3[:, :, 0]
        VE = sb("VE", [P, NB])

        TB = sb("TB", [P, NB, ROW])
        XNT = sb("XNT", [P, T])
        GW = sb("GW", [P, EXPERTS + 1])
        SGU = sb("SGU", [P, 2 * FS])
        SD = sb("SD", [P, 2, D])
        EGU = sb("EGU", [P, EXPERTS, 2 * FE])
        ED = sb("ED", [P, EXPERTS // 2, D])
        ROUTE = sb("ROUTE", [P, 4, NB, EXPERTS])
        LG = ROUTE[:, 0, :, :]
        LM = sb("LM", [P, NB, EXPERTS])
        MASK = sb("MASK", [P, NB, EXPERTS], BF16)
        POS = ROUTE[:, 1, :, :]
        COUNT = ROUTE[:, 2, :, :]
        SLOT3 = ROUTE[:, 3, :, :].rearrange("p n e -> p (n e)").bitcast(I16).rearrange("p (w n e) -> p w n e", w=2, n=NB)
        SLOT, HI = SLOT3[:, 0, :, :], SLOT3[:, 1, :, :]
        LOW = sb("LOW", [P, NB, EXPERTS], I16)
        TOP = sb("TOP", [P, NB, 8])
        SUMS = sb("SUMS", [P, NB])
        SG = sb("SG", [P, NB])
        HOT = BIG[:, :].bitcast(F16).rearrange("p (w n g s e) -> p w n g s e", w=2, n=NB, g=NG, s=DIG)
        GA = BIG[:, :].rearrange("p (c r) -> p c r", r=ROW)
        IDX = sb("IDX", [P, NG, DIG, EG])
        IDF = sb("IDF", [P, CH])
        IDI = sb("IDI", [P, CH], I32)
        OWNP = sb("OWNP", [P, DIG, 2, EG])
        WD = sb("WD", [P, CH, 2])
        DST = sb("DST", [P, CH], I32)
        XG = STORE_A[:, :].rearrange("p (b s n) -> p b s n", b=2, s=DIG)
        TG = sb("TG", [P, 512])
        H1 = sb("H1", [P, 512])
        AH = sb("AH", [P, EG // 2, 2, CAP])
        YT = sb("YT", [P, DIG, DIG, EG // 2, 2])
        YS = ROUTE[:, :, :, :].rearrange("p a n e -> p (a n e)").rearrange("p (c d) -> p c d", d=D)
        TS_ = STORE_B[:, 0:1024].rearrange("p (c n) -> p c n", c=2)
        HS = STORE_B[:, 1024:2048].rearrange("p (c n) -> p c n", c=2)
        SH = sb("SH", [P, 4, D])
        PART = YS[:, 0:2 * TOPK, :].rearrange("p (b k) d -> p b (k d)", b=2)
        HALF = H1[:, :]
        QUARTER = TG[:, 0:256]
        YSUM = sb("YSUM", [P, 2, D])
        STATS_T = sb("STATS_T", [P, 2, 6])
        MV_T = sb("MV_T", [P, 2, 2])
        VAR_T = sb("VAR_T", [P, 2, 1])
        RS_T = sb("RS_T", [P, 2, 1])
        minus_half = sb("minus_half", [P, NB])
        FIRST = sb("FIRST", [1, 1])
        NTOP = sb("NTOP", [P, NB])
        TOPX = sb("TOPX", [P, NB, TOPK])
        ZERO = PART[:, 0, :]
        WF = sb("WF", [P, D])
        FWT = sb("FWT", [P, D])
        FVC = sb("FVC", [32, 2, D])
        zrow = sb("zrow", [1, ROW])
        OT = EGU[:, 0:NB, :].rearrange("p (m n) d -> p m n d", m=4)

        ld_con, ld_w, ld_b, ld_moe, ld_ffn = (sem(n) for n in ("ld_con", "ld_w", "ld_b", "ld_moe", "ld_ffn"))
        ld_shared = sem("ld_shared")
        ld_x = [sem(f"ld_x{m}") for m in range(4)]
        ld_w0, sel_zero, vm_zero, sel_set = sem("ld_w0"), sem("sel_zero"), sem("vm_zero"), sem("sel_set")
        cx_in = [sem("cx_in0"), sem("cx_in1")]
        const_set, dve_set, bias_mm, bias_set = sem("const_set"), sem("dve_set"), sem("bias_mm"), sem("bias_set")
        gates_done = sem("gates_done")
        max_mm, max_got, score_mm, exp_done, pv_mm = (sem(n) for n in ("max_mm", "max_got", "score_mm", "exp_done", "pv_mm"))
        xn_done, tr_mm, xc_done = sem("xn_done"), sem("tr_mm"), sem("xc_done")
        qk_mm, hi_done, split_done = sem("qk_mm"), sem("hi_done"), sem("split_done")
        qs_mm, q_stacked = sem("qs_mm"), sem("q_stacked")
        q_masked, q_masked3 = sem("q_masked"), sem("q_masked3")
        ks_mm, k_stacked = sem("ks_mm"), sem("k_stacked")
        v_mm, v_done = sem("v_mm"), sem("v_done")
        recip_done, ctx_done, o_mm, x_done, stat_done, mv_done = (
            sem(n) for n in ("recip_done", "ctx_done", "o_mm", "x_done", "stat_done", "mv_done"))
        aggr_done = sem("aggr_done")
        zero_set, zero_st = sem("zero_set"), sem("zero_st")
        e_var, e_rs, e_xn, e_tr, e_xt = (sem(n) for n in ("e_var", "e_rs", "e_xn", "e_tr", "e_xt"))
        m_lg, m_lgc, m_top, m_exp, m_step, m_mask, m_less, m_inv = (
            sem(n) for n in ("m_lg", "m_lgc", "m_top", "m_exp", "m_step", "m_mask", "m_less", "m_inv"))
        m_scan, m_w, m_dest, m_raw, m_slot = sem("m_scan"), sem("m_w"), sem("m_dest"), sem("m_raw"), sem("m_slot")
        m_pos, m_hot, m_ids, m_idx = sem("m_pos"), sem("m_hot"), sem("m_ids"), sem("m_idx")
        m_tab, m_tabw = sem("m_tab"), sem("m_tabw")
        g_in = [sem(f"g_in{g}") for g in range(NG)]
        g_tr, g_xt, g_up, g_tanh, g_h1, g_act, g_dn, g_yt, g_bk, g_ys, g_wd, g_own = (
            sem(n) for n in ("g_tr", "g_xt", "g_up", "g_tanh", "g_h1", "g_act", "g_dn", "g_yt", "g_bk", "g_ys", "g_wd", "g_own"))
        y_st = sem("y_st")
        h_mm, h_tanh, h_h1, h_act, h_dn, h_sh, h_x = (sem(n) for n in ("h_mm", "h_tanh", "h_h1", "h_act", "h_dn", "h_sh", "h_x"))
        p_in = [sem("p_in0"), sem("p_in1")]
        p_first, p_step, p_sum, p_x, p_stat, p_aggr, p_var, p_rs = (
            sem(n) for n in ("p_first", "p_step", "p_sum", "p_x", "p_stat", "p_aggr", "p_var", "p_rs"))
        f_mm, f_x = sem("f_mm"), sem("f_x")
        f_st = sem("f_st")

        x_v = x.rearrange("(n p) d -> p n d", p=P)
        ctx_v = ctx.rearrange("(n p) d -> n p d", p=P)
        out_v = out.rearrange("(m n p) d -> m p n d", p=P, n=4)
        parts_z = parts.rearrange("(b a r) d -> b a (r d)", b=NB, a=P)
        egu_v = egu.rearrange("(b e) h f -> b h e f", b=NB)
        edown_v = edown.rearrange("(b k u) i h -> b (u i) k h", b=NB, u=2)
        parts_v = parts.rearrange("(n p k) d -> n p (k d)", p=P, k=TOPK)

        def wait(eng, semaphore, value):
            if isinstance(value, int) and value <= 0:
                return
            eng.wait_ge(semaphore, value)

        def over_batches(eng, layer, step, peeled=1):
            def pair(i, last):
                for p in range(2):
                    step(i, p, NB * layer + 2 * i + p, last)
            pair(0, False)
            with eng.Fori(1, NB // 2 - peeled) as i:
                pair(i, False)
            for i in range(NB // 2 - peeled, NB // 2):
                pair(i, i == NB // 2 - 1)

        block = es.enter_context(nc.Block())

        @block.sync
        def _(sp):
            sp.dma_start(X[:, 0:4, :], x_v[:, 0:4, :]).then_inc(ld_x[0], 16)
            sp.dma_start(CON[:, :], consts).then_inc(ld_con, 16)

            def ctx_tile(i, p, B, last):
                wait(sp, tr_mm, B - 1)
                b = i * 2 + p
                sp.dma_start(CXB[:, p, :], ctx_v[b, :, :]).then_inc(cx_in[p], 16)

            for p in range(2):
                ctx_tile(0, p, p, False)
            for m in range(1, 4):
                sp.dma_start(X[:, 4 * m:4 * m + 4, :], x_v[:, 4 * m:4 * m + 4, :]).then_inc(ld_x[m], 16)
            sp.dma_start(GW[:, :], gate_w).then_inc(ld_shared, 16)
            sp.dma_start(SGU[:, :], sgu).then_inc(ld_shared, 16)
            sp.dma_start(SD[:, :, :], sdown.rearrange("(c p) d -> p c d", p=P)).then_inc(ld_shared, 16)
            sp.wait_ge(zero_set, 2)
            sp.dma_start(table[0:1, :], zrow[:, :]).then_inc(zero_st, 16)

            def later_loads(b):
                ne, nk = EXPERTS // NB, EXPERTS // 2 // NB
                sp.dma_start(EGU[:, bass.ds(b * ne, ne), :], egu_v[b, :, :, :]).then_inc(ld_moe, 16)
                sp.dma_start(ED[:, bass.ds(b * nk, nk), :], edown_v[b, :, :, :]).then_inc(ld_moe, 16)
                sp.dma_start(parts_z[b, :, :], ZERO).then_inc(zero_st, 16)

            for b in range(2):
                later_loads(b)
            with sp.Fori(1, NB // 2) as i:
                for p in range(2):
                    ctx_tile(i, p, i * 2 + p, False)
                    later_loads(i * 2 + p)

            rows_v = table[1:T + 1, :].rearrange("(n p) r -> p n r", p=P)
            sp.wait_ge(e_xn, 5)
            sp.dma_start(rows_v[:, :, 0:D], TB[:, :, 0:D]).then_inc(m_tabw, 16)
            sp.wait_ge(m_w, 1)
            sp.wait_ge(m_dest, 1)
            sp.dma_start(rows_v[:, :, D:ROW], TB[:, :, D:ROW]).then_inc(m_tabw, 16)

            for p in range(2):
                ctx_tile(0, p, NB + p, False)

            sp.wait_ge(y_st, 16 * CH)

            def parts_tile(i, p, n):
                if isinstance(n, int):
                    wait(sp, p_first, n - 1)
                else:
                    wait(sp, p_step, 2 * n - 7)
                sp.dma_start(PART[:, p, :], parts_v[i * 2 + p, :, :]).then_inc(p_in[p], 16)

            for p in range(2):
                parts_tile(0, p, p)
            for p in range(2):
                parts_tile(1, p, 2 + p)
                ctx_tile(1, p, NB + 2 + p, False)
            with sp.Fori(2, NB // 2) as i:
                for p in range(2):
                    parts_tile(i, p, i * 2 + p)
                    ctx_tile(i, p, i * 2 + (NB + p), False)
            for m in range(4):
                sp.wait_ge(f_x, m + 1)
                sp.dma_start(out_v[m], OT[:, m, :, :]).then_inc(f_st, 16)
            sp.wait_ge(f_st, 64)

        @block.gpsimd
        def _(pool):
            def rsqrt_of_variances(turn, lo, hi):
                pool.wait_ge(e_var, turn)
                pool.tensor_tensor(RS[:, lo:hi], VE[:, lo:hi], minus_half[:, lo:hi], ALU.pow).then_inc(e_rs, 1)

            pool.memset(ones_b[:, :], 1.0).then_inc(const_set, 1)
            pool.memset(minus_half[:, :], -0.5).then_inc(p_rs, 1)
            pool.memset(SEL[:, :, :, :, :], 0.0).then_inc(sel_zero, 1)
            pool.memset(VM[:, :, :, :], 0.0).then_inc(vm_zero, 1)
            pool.wait_ge(p_rs, 1)
            rsqrt_of_variances(1, 0, 4)
            pool.memset(ones_d[:, :, :], 0.0).then_inc(const_set, 1)
            pool.wait_ge(const_set, 2)
            for g in range(G):
                pool.memset(ones_d[:, g, g * DH:(g + 1) * DH], 1.0).then_inc(const_set, 1)
            pool.memset(B3[:, :], 0.0).then_inc(const_set, 1)
            pool.memset(zrow[:, :], float(T * TOPK)).then_inc(const_set, 1)
            pool.memset(AH[:, :, :, :], 0.0).then_inc(const_set, 1)

            pool.memset(ZERO, 0.0).then_inc(zero_set, 1)
            pool.wait_ge(const_set, 9)
            pool.memset(zrow[:, 0:D + EXPERTS], 0.0).then_inc(zero_set, 1)

            rsqrt_of_variances(2, 4, NB)
            rsqrt_of_variances(3, 0, 12)
            rsqrt_of_variances(4, 12, NB - 1)
            rsqrt_of_variances(5, NB - 1, NB)
            pool.wait_ge(m_scan, 1)
            pool.tensor_tensor(TB[:, :, D + EXPERTS:ROW], COUNT[:, :, :],
                               CON[:, C_TOK8:C_TOK8 + NB].rearrange("p (n o) -> p n o", o=1).to_broadcast([P, NB, EXPERTS]),
                               ALU.add).then_inc(m_dest, 1)
            pool.wait_ge(m_exp, 4)
            pool.wait_ge(m_inv, 1)
            pool.tensor_tensor(TB[:, :, D:D + EXPERTS], LM[:, :, :],
                               SUMS[:, :].rearrange("p (n o) -> p n o", o=1).to_broadcast([P, NB, EXPERTS]),
                               ALU.mult).then_inc(m_w, 1)
            pool.wait_ge(zero_st, 16 * (NB + 1))
            pool.wait_ge(m_tabw, 32)
            for g in range(NG):
                pool.wait_ge(m_idx, 1)
                for s in range(DIG):
                    c = g * DIG + s
                    pool.indirect_dma_start(GA[:, c, :], None, table[:, :],
                                            bass.IndirectOffsetOnAxis(ap=IDI[:, c:c + 1], axis=0)).then_inc(g_in[g], 16)
            for g in range(NG):
                pool.wait_ge(g_wd, g + 1)
                for s in range(DIG):
                    c = g * DIG + s
                    pool.wait_ge(g_ys, 2 * g + s // 4 + 1)
                    pool.indirect_dma_start(parts[:, :], bass.IndirectOffsetOnAxis(ap=DST[:, c:c + 1], axis=0),
                                            YS[:, c, :], None, bounds_check=T * TOPK - 1,
                                            oob_is_err=False).then_inc(y_st, 16)

            def tile_sum(i, p, n):
                pool.wait_ge(p_in[p], i * 16 + 16)
                wait(pool, p_sum, n - 2)
                pool.tensor_tensor(HALF[:, :], PART[:, p, 0:512], PART[:, p, 512:1024], ALU.add).then_inc(p_step, 1)
                pool.wait_ge(p_step, n * 2 - 3)
                pool.tensor_tensor(QUARTER[:, :], HALF[:, 0:256], HALF[:, 256:512], ALU.add).then_inc(p_step, 1)
                pool.wait_ge(p_step, n * 2 - 2)
                wait(pool, p_x, n - 1)
                pool.tensor_tensor(YSUM[:, p, :], QUARTER[:, 0:128], QUARTER[:, 128:256], ALU.add).then_inc(p_sum, 1)

            def tile_rsqrt(p, n):
                pool.wait_ge(p_var, n + 1)
                wait(pool, xn_done, n + (NB - 1))
                pool.tensor_tensor(RS_T[:, p, :], VAR_T[:, p, :], minus_half[:, 0:1], ALU.pow).then_inc(p_rs, 1)

            for p in range(2):
                tile_rsqrt(p, p)
            for p in range(2):
                tile_sum(1, p, 2 + p)
            with pool.Fori(2, NB // 2) as i:
                for p in range(2):
                    tile_rsqrt(p, i * 2 + (p - 2))
                    tile_sum(i, p, i * 2 + p)
            for p in range(2):
                tile_rsqrt(p, NB - 2 + p)
            rsqrt_of_variances(6, 0, 12)
            rsqrt_of_variances(7, 12, NB - 1)
            rsqrt_of_variances(8, NB - 1, NB)

        @block.tensor
        def _(pe):
            def output_biases():
                pe.wait_ge(ld_w, 16)
                pe.wait_ge(ld_ffn, 48)
                for layer in range(2):
                    pe.matmul(bank[3][:, layer * D:(layer + 1) * D], BC[:, layer, 2:3].to_broadcast([P, P]),
                              W[:, layer, 3, :], start=True, stop=True)
                pe.matmul(bank[3][:, 2 * D:3 * D], FVC[:, 0, :], FVC[:, 1, :], start=True, stop=True).then_inc(bias_mm, 1)

            def transposes(layer, i, p, B, o=7):
                wait(pe, xn_done, B + 1)
                pe.wait_ge(cx_in[p], i * 16 + (NB // 2 * layer + 1) * 16)
                if o == 7:
                    wait(pe, split_done, B)
                    wait(pe, x_done, B - 3)
                pe.transpose(bank[o][:, 0:D], XN[:, p, :], ident)
                pe.transpose(bank[o][:, D:2 * D], CXB[:, p, :], ident).then_inc(tr_mm, 1)

            def v_project(layer, p, B, o=7):
                pe.matmul(bank[o][:, 0:D], XC[:, p, D:2 * D], W[:, layer, 2, :], start=True, stop=True).then_inc(v_mm, 1)

            def qk_project(layer, p, B, o=7):
                wait(pe, xc_done, B + 1)
                for which in range(2):
                    mm = pe.matmul(bank[o][:, (1 + which) * D:(2 + which) * D], W[:, layer, which, :],
                                   XC[:, p, which * D:(which + 1) * D], start=True, stop=True)
                mm.then_inc(qk_mm, 1)

            def stack(which, done, o=4):
                for g in range(G):
                    for part in range(2):
                        mm = pe.matmul(bank[o][:, g * P:(g + 1) * P], SEL[:, which, part, g, :], HL[:, which, part, :],
                                       start=(part == 0), stop=(part == 1))
                mm.then_inc(done, 1)

            def q_stack(B):
                wait(pe, split_done, B + 1)
                wait(pe, k_stacked, B)
                stack(0, qs_mm)

            def k_stack(B):
                wait(pe, q_stacked, B + 1)
                stack(1, ks_mm)

            def max_pass(p, g, B):
                if g == 0:
                    wait(pe, q_masked, B + 1)
                    wait(pe, q_masked3, B + 1)
                    wait(pe, k_stacked, B + 1)
                wait(pe, max_got, B * 4 + (g - 1))
                for j in range(J):
                    mm = pe.matmul(bank[g % 2][:, j * P:(j + 1) * P], QM[:, p, g, j, :], KS[:, p, g, :],
                                   start=True, stop=True)
                mm.then_inc(max_mm, 1)

            def scores(p, g, B):
                wait(pe, exp_done, B * 4 + (g - 1))
                t = bank[2 + g % 2]
                pe.matmul(t[:, :], KS[:, p, g, :], QM[:, p, g, :, :], start=True, stop=False)
                wait(pe, max_got, B * 4 + (g + 1))
                for j in range(J):
                    mm = pe.matmul(t[:, j * P:(j + 1) * P], NM[:, g, j:j + 1].to_broadcast([P, P]), negid_b[:, :],
                                   start=False, stop=(j == J - 1))
                mm.then_inc(score_mm, 1)

            def weighted(p, g, B):
                if g == 0:
                    wait(pe, ctx_done, B - 1)
                    wait(pe, v_done, B + 1)
                wait(pe, exp_done, B * 4 + (g + 1))
                acc = bank[5 + p]
                for j in range(J):
                    pe.matmul(acc[32 * j:32 * j + 32, 0:P], VM[:, p, g, 32 * j:32 * j + 32],
                              E[:, g, j * P:(j + 1) * P], start=(g == 0), stop=(g == G - 1), skip_group_check=True)
                for j in range(J):
                    mm = pe.matmul(acc[32 * j:32 * j + 32, P:2 * P], ones_d[:, g, :], E[:, g, j * P:(j + 1) * P],
                                   start=False, stop=(g == G - 1), skip_group_check=True)
                mm.then_inc(pv_mm, 1)

            def o_project(layer, p, B, read, value):
                wait(pe, ctx_done, B + 1)
                wait(pe, read, value)
                off = layer * D
                pe.matmul(bank[7][:, 0:D], CN[:, p, :], W[:, layer, 3, :], start=True, stop=False)
                pe.matmul(bank[7][:, 0:D], ones_b[:, :], B3[:, off:off + D], start=False, stop=True).then_inc(o_mm, 1)

            def transposed_tiles(layer, m):
                pe.wait_ge(e_xn, 5 * layer + m + 1)
                wait(pe, e_xt, 4 * layer + m)
                for n in range(4):
                    if 4 * m + n == NB - 1:
                        pe.wait_ge(e_xn, 5 * layer + 5)
                    mm = pe.transpose(bank[4][:, n * P:(n + 1) * P], TB[:, 4 * m + n, 0:D], ident)
                mm.then_inc(e_tr, 1)

            def logits(m):
                pe.wait_ge(ld_shared, 48)
                pe.wait_ge(e_xt, m + 1)
                for n in range(4):
                    t = 4 * m + n
                    mm = pe.matmul(bank[m][:, n * 65:(n + 1) * 65], XNT[:, t * P:(t + 1) * P], GW[:, :],
                                   start=True, stop=True)
                mm.then_inc(m_lg, 1)

            def last_products(m):
                pe.wait_ge(e_xt, 4 + m + 1)
                for n in range(4):
                    t = 4 * m + n
                    pe.matmul(bank[m][:, n * P:(n + 1) * P], XNT[:, t * P:(t + 1) * P], WF[:, :],
                              start=True, stop=False)
                    mm = pe.matmul(bank[m][:, n * P:(n + 1) * P], ones_b[:, :], B3[:, 2 * D:NBO],
                                   start=False, stop=True)
                mm.then_inc(f_mm, 1)

            next_products = (logits, last_products)

            def attention(layer):
                B0 = NB * layer
                pe.wait_ge(ld_con, 16)
                transposes(layer, 0, 0, B0)
                if layer == 0:
                    pe.wait_ge(ld_w0, 32)
                else:
                    pe.wait_ge(ld_w, 16)
                qk_project(layer, 0, B0)
                v_project(layer, 0, B0, 6)
                transposes(layer, 0, 1, B0 + 1, 5)
                if layer == 0:
                    pe.wait_ge(sel_set, 1)
                q_stack(B0)
                pe.wait_ge(xc_done, B0 + 2)
                stack(1, ks_mm, 5)
                pe.wait_ge(v_done, B0 + 1)
                qk_project(layer, 1, B0 + 1, 6)
                if layer == 0:
                    output_biases()
                    pe.wait_ge(const_set, 9)
                pe.wait_ge(q_stacked, B0 + 1)
                q_stack(B0 + 1)
                max_pass(0, 0, B0)
                max_pass(0, 1, B0)
                scores(0, 0, B0)

                def step(i, p, B, last):
                    q = 1 - p
                    end = last and p == 1
                    first = isinstance(i, int) and i == 0 and p == 0
                    for g in range(G):
                        if layer == 0 and first and g == 0:
                            pe.wait_ge(bias_set, 2)
                        if g < 2:
                            max_pass(p, g + 2, B)
                        elif not end:
                            max_pass(q, g - 2, B + 1)
                        if g < 3:
                            scores(p, g + 1, B)
                        elif not end:
                            scores(q, 0, B + 1)
                        if g == 3 and layer == 0 and isinstance(i, int) and B == 1:
                            pe.wait_ge(bias_set, 3)
                        if g == 3 and not first:
                            if not last:
                                o_project(layer, q, B - 1, split_done, B + 3)
                            elif p == 0:
                                o_project(layer, q, B - 1, v_done, B + 2)
                            else:
                                o_project(layer, q, B - 1, x_done, B - 1)
                        if g > 0:
                            weighted(p, g - 1, B)
                        elif not first:
                            weighted(q, G - 1, B - 1)
                        if g == 0 and not end:
                            k_stack(B + 1)
                        if g == 0 and not last:
                            transposes(layer, i + 1, p, B + 2)
                        if g == 1 and not last:
                            qk_project(layer, p, B + 2)
                        if g == 1 and not end:
                            if last:
                                wait(pe, x_done, B - 1)
                            v_project(layer, q, B + 1)
                        if g == 3 and not last:
                            q_stack(B + 2)
                        if end and g < 3:
                            if g == 0:
                                pe.wait_ge(k_stacked, B + 1)
                            transposed_tiles(layer, g)

                over_batches(pe, layer, step)
                weighted(1, G - 1, B0 + NB - 1)
                pe.wait_ge(max_got, 4 * (B0 + NB))
                next_products[layer](0)
                o_project(layer, 1, B0 + NB - 1, x_done, B0 + NB - 1)
                next_products[layer](1)
                pe.wait_ge(exp_done, 4 * (B0 + NB))
                next_products[layer](2)

            attention(0)

            def shared_up(m, c):
                for w in range(2):
                    pe.matmul(bank[4 * c + w][:, :], SGU[:, (2 * w + c) * P:(2 * w + c + 1) * P],
                              XNT[:, m * 512:(m + 1) * 512], start=True, stop=True).then_inc(h_mm, 1)

            def shared_down(m):
                pe.wait_ge(h_act, 2 * m + 2)
                for n in range(4):
                    for c in range(2):
                        mm = pe.matmul(bank[4][:, n * P:(n + 1) * P], HS[:, c, n * P:(n + 1) * P], SD[:, c, :],
                                       start=(c == 0), stop=(c == 1))
                mm.then_inc(h_dn, 1)

            pe.wait_ge(m_mask, 2)
            chosen = MASK[:, 0:8, :]
            pe.wait_ge(ctx_done, NB)
            pe.matmul(bank[6][:, :], tri_b[:, :], chosen, start=True, stop=False)
            for t in range(7):
                pe.matmul(bank[6][:, (t + 1) * 64:512], ones_b[:, :], MASK[:, t:t + 1, :].to_broadcast([P, 7 - t, 64]),
                          start=False, stop=False)
            pe.matmul(bank[6][:, :], off_b[:, :], chosen, start=False, stop=True).then_inc(m_pos, 1)
            transposed_tiles(0, 3)
            pe.wait_ge(x_done, NB)
            for t in range(8):
                pe.matmul(bank[7][:, :], ones_b[:, :], MASK[:, t:t + 1, :].to_broadcast([P, 8, 64]),
                          start=(t == 0), stop=False)
            logits(3)

            def token_numbers(t):
                pe.wait_ge(m_hot, t + 1)
                for g in range(NG):
                    mm = pe.matmul(bank[5][:, g * P:(g + 1) * P], HOT[:, 0, t, g, :, :],
                                   HOT[:, 1, t, g, :, :], start=(t == 0 and g == 0),
                                   stop=(t == NB - 1), skip_group_check=True)
                return mm

            for t in range(4):
                token_numbers(t)
            pe.wait_ge(m_mask, 4)
            chosen = MASK[:, 8:16, :]
            for t in range(8, 15):
                pe.matmul(bank[7][:, (t - 7) * 64:512], ones_b[:, :], MASK[:, t:t + 1, :].to_broadcast([P, 15 - t, 64]),
                          start=False, stop=False)
            pe.matmul(bank[7][:, :], tri_b[:, :], chosen, start=False, stop=False)
            pe.matmul(bank[7][:, :], off_b[:, :], chosen, start=False, stop=True).then_inc(m_pos, 1)
            for t in range(4, NB):
                mm = token_numbers(t)
            mm.then_inc(m_ids, 1)

            def expert_in(g):
                pe.wait_ge(g_in[g], 16 * DIG)
                for h in range(2):
                    if g == 1:
                        pe.wait_ge(g_xt, h + 1)
                    elif g > 1:
                        pe.wait_ge(g_ys, 2 * (g - 2) + h + 1)
                    for s in range(4):
                        mm = pe.transpose(bank[6 + h][:, s * P:(s + 1) * P], GA[:, g * DIG + 4 * h + s, 0:D], ident)
                    mm.then_inc(g_tr, 1)

            def expert_up(g):
                pe.wait_ge(g_xt, 2 * g + 2)
                wait(pe, g_act, g)
                for k in range(EG // 2):
                    for w in range(2):
                        for u in range(2):
                            e = 2 * k + u
                            mm = pe.matmul(bank[2 + w][64 * u:64 * u + 64, k * CAP:(k + 1) * CAP],
                                           EGU[:, EG * g + e, w * FE:(w + 1) * FE],
                                           XG[:, g % 2, :, :].rearrange("p s (a e) -> p s a e", e=EG)[:, :, :, e],
                                           start=True, stop=True)
                mm.then_inc(g_up, 1)

            def expert_down(g):
                pe.wait_ge(g_act, g + 1)
                wait(pe, g_yt, g)
                for k in range(EG // 2):
                    mm = pe.matmul(bank[k // 4][:, k % 4 * P:(k % 4 + 1) * P], ED[:, g * (EG // 2) + k, :],
                                   AH[:, k, :, :], start=True, stop=True)
                mm.then_inc(g_dn, 1)

            def expert_back(g):
                pe.wait_ge(g_yt, g + 1)
                pe.wait_ge(g_xt, (4, 6, 8, 8)[g])
                for h in range(2):
                    if g == 3:
                        pe.wait_ge(g_ys, 4 + h + 1)
                    for s in range(4):
                        mm = pe.transpose(bank[6 + h][:, s * P:(s + 1) * P],
                                          YT[:, 4 * h + s, :, :, :].rearrange("p a k u -> p (a k u)"), ident)
                    mm.then_inc(g_bk, 1)

            pe.wait_ge(m_lgc, 4)
            shared_up(0, 0)
            pe.wait_ge(m_idx, 1)
            shared_up(0, 1)
            pe.wait_ge(h_act, 1)
            shared_up(1, 0)
            shared_down(0)
            pe.wait_ge(h_sh, 1)
            shared_up(1, 1)
            shared_down(1)
            pe.wait_ge(m_slot, 2)
            pe.wait_ge(ld_moe, 32 * NB)
            expert_in(0)
            expert_up(0)
            expert_in(1)
            pe.wait_ge(h_act, 3)
            expert_down(0)
            expert_up(1)
            expert_back(0)
            expert_in(2)
            expert_down(1)
            expert_up(2)
            expert_back(1)
            expert_in(3)
            expert_down(2)
            expert_up(3)
            expert_back(2)
            expert_down(3)
            expert_back(3)
            pe.wait_ge(g_yt, NG)
            shared_up(2, 0)
            pe.wait_ge(h_sh, 2)
            shared_up(2, 1)
            pe.wait_ge(h_act, 5)
            shared_down(2)
            shared_up(3, 0)
            pe.wait_ge(h_sh, 3)
            shared_up(3, 1)
            shared_down(3)

            pe.wait_ge(g_xt, 2 * NG)
            pe.wait_ge(g_ys, 2 * NG)
            attention(1)

            transposed_tiles(1, 3)
            last_products(3)

        @block.scalar
        def _(act):
            act.dma_start(W[:, 0, :, :], wqkvo[:, 0, :, :]).then_inc(ld_w0, 16)
            act.dma_start(BC[:, :, :], bcol).then_inc(ld_w0, 16)
            act.wait_ge(const_set, 1)
            act.activation(FIRST[:, :], ones_b[0:1, 0:1], ACT.Tanh)
            act.dma_start(W[:, 1, :, :], wqkvo[:, 1, :, :]).then_inc(ld_w, 16)
            act.dma_start(GT[:, :], gates.rearrange("(a n) -> a n", a=1).to_broadcast([P, 4])).then_inc(ld_b, 16)
            act.dma_start(BR[:, :], brow.rearrange("(a n) -> a n", a=1).to_broadcast([P, NBO])).then_inc(ld_b, 16)
            act.dma_start(FWT[:, :], ffn_wt).then_inc(ld_ffn, 16)
            act.dma_start(FVC[:, 0, :], ffn_vt).then_inc(ld_ffn, 16)
            act.dma_start(FVC[:, 1, :], ffn_ct).then_inc(ld_ffn, 16)

            def transposed(p, B, o=7):
                wait(act, tr_mm, B + 1)
                wait(act, v_mm, B - 1)
                act.activation(XC[:, p, :], bank[o][:, 0:2 * D], ACT.Copy).then_inc(xc_done, 1)

            def values(p, B, o=7):
                wait(act, v_mm, B + 1)
                wait(act, pv_mm, B * 4 - 4)
                act.activation(VM_blocks[p], bank[o][:, 0:D].rearrange("p (j g d) -> p j g d", j=J, g=G),
                               ACT.Copy).then_inc(v_done, 1)

            def high_parts(layer, B, o=7):
                wait(act, qk_mm, B + 1)
                wait(act, ks_mm, B)
                act.activation(HL[:, 0, 0, :], bank[o][:, D:2 * D], ACT.Identity, bias=BC[:, layer, 0:1])
                act.activation(HL[:, 1, 0, :], bank[o][:, 2 * D:3 * D], ACT.Identity,
                               bias=BC[:, layer, 1:2]).then_inc(hi_done, 1)

            def q_stack_out(B):
                wait(act, qs_mm, B + 1)
                wait(act, q_masked, B)
                wait(act, q_masked3, B)
                act.activation(QS[:, :], bank[4][:, :], ACT.Copy).then_inc(q_stacked, 1)

            def q_mask3(p, B):
                wait(act, q_stacked, B + 1)
                wait(act, score_mm, B * 4 - 4)
                act.activation(QM[:, p, :, J - 1, :], QS[:, :].rearrange("p (g q) -> p g q", g=G), ACT.Copy,
                               scale=CON[:, C_QUAD + J - 1:C_QUAD + J]).then_inc(q_masked3, 1)

            def k_stack_out(p, B, o=4):
                wait(act, ks_mm, B + 1)
                wait(act, score_mm, B * 4 - 4)
                act.activation(KS[:, p, :, :].rearrange("p g k -> p (g k)"), bank[o][:, :],
                               ACT.Copy).then_inc(k_stacked, 1)

            def exponentials(g, B):
                wait(act, score_mm, B * 4 + (g + 1))
                wait(act, pv_mm, B * 4 + (g - 3))
                act.activation(E[:, g, :], bank[2 + g % 2][:, :], ACT.Exp, scale=SCALE).then_inc(exp_done, 1)

            def transposed_tiles(layer, m):
                act.wait_ge(e_tr, 4 * layer + m + 1)
                act.activation(XNT[:, m * 512:(m + 1) * 512], bank[4][:, :], ACT.Copy).then_inc(e_xt, 1)

            def logits(m):
                act.wait_ge(zero_st, 16 * (NB + 1))
                act.wait_ge(m_lg, m + 1)
                v = bank[m][:, 0:260].rearrange("p (n e) -> p n e", n=4)
                act.activation(SG[:, 4 * m:4 * m + 4], v[:, :, EXPERTS], ACT.Copy)
                act.activation(LG[:, 4 * m:4 * m + 4, :], v[:, :, 0:EXPERTS], ACT.Copy).then_inc(m_lgc, 1)

            def attention(layer):
                B0 = NB * layer
                transposed(0, B0)
                if layer == 0:
                    act.wait_ge(vm_zero, 1)
                    act.wait_ge(ld_w0, 32)
                high_parts(layer, B0)
                values(0, B0, 6)
                transposed(1, B0 + 1, 5)
                q_stack_out(B0)
                k_stack_out(0, B0, 5)
                q_mask3(0, B0)
                high_parts(layer, B0 + 1, 6)
                if layer == 0:
                    act.wait_ge(ld_b, 32)
                    act.activation(TH[:, :], GT[:, :], ACT.Tanh).then_inc(gates_done, 1)
                exponentials(0, B0)

                def step(i, p, B, last):
                    end = last and p == 1
                    q = 1 - p
                    for g in range(G):
                        if g == 0 and not end:
                            q_stack_out(B + 1)
                        if g == 1 and not end:
                            q_mask3(q, B + 1)
                        if g < 3:
                            exponentials(g + 1, B)
                        elif not end:
                            exponentials(0, B + 1)
                        if g == 0 and not end:
                            k_stack_out(q, B + 1)
                        if g == 0 and not last:
                            transposed(p, B + 2)
                        if g == 1 and not end:
                            values(q, B + 1)
                        if g == 1 and not last:
                            high_parts(layer, B + 2)
                        if end and g < 3:
                            transposed_tiles(layer, g)

                over_batches(act, layer, step)
                if layer == 0:
                    for m in range(2):
                        logits(m)

            attention(0)

            def logit_exponentials(m):
                act.wait_ge(m_top, m + 1)
                for t in range(4 * m, 4 * m + 4):
                    ins = act.activation(LM[:, t, :], LG[:, t, :], ACT.Exp, bias=NTOP[:, t:t + 1])
                ins.then_inc(m_exp, 1)

            logits(2)
            transposed_tiles(0, 3)
            for m in range(2):
                logit_exponentials(m)
            logits(3)
            act.wait_ge(m_lgc, 4)
            act.activation(SG[:, :], SG[:, :], ACT.Tanh, scale=0.5).then_inc(m_less, 1)
            for t in range(NB):
                if t == 8:
                    for m in (2, 3):
                        logit_exponentials(m)
                    act.wait_ge(m_less, 2)
                    act.activation(TOPX[:, :, :], TOPX[:, :, :], ACT.Exp).then_inc(m_less, 1)
                act.wait_ge(m_raw, t + 1)
                act.activation(HOT[:, 1, t, :, :, :], HOT[:, 1, t, :, :, :], ACT.Copy,
                               scale=CON[:, C_TOK + t:C_TOK + t + 1]).then_inc(m_hot, 1)

            def shared_tanh(m, c):
                act.wait_ge(h_mm, 4 * m + 2 * c + 1)
                wait(act, h_h1, 2 * (m - 1) + c + 1)
                act.activation(TS_[:, c, :], bank[4 * c][:, :], ACT.Tanh, scale=0.5).then_inc(h_tanh, 1)

            def expert_in(g):
                for h in range(2):
                    act.wait_ge(g_tr, 2 * g + h + 1)
                    wait(act, g_up, g - 1)
                    act.activation(XG[:, g % 2, 4 * h:4 * h + 4, :],
                                   bank[6 + h][:, :].rearrange("p (s n) -> p s n", s=4), ACT.Copy).then_inc(g_xt, 1)

            def expert_tanh(g):
                act.wait_ge(g_up, g + 1)
                wait(act, g_h1, g)
                act.activation(TG[:, :], bank[2][:, :], ACT.Tanh, scale=0.5).then_inc(g_tanh, 1)

            def expert_out(g):
                act.wait_ge(g_dn, g + 1)
                wait(act, g_bk, 2 * g)
                for b in range(2):
                    ins = act.activation(YT[:, :, :, :, :].rearrange("p s a k u -> p (s a) k u")[:, :, 4 * b:4 * b + 4, :],
                                         bank[b][:, :].rearrange("p (k u n) -> p n k u", k=4, u=2), ACT.Copy)
                ins.then_inc(g_yt, 1)

            for m, c in ((0, 0), (0, 1), (1, 0), (1, 1)):
                shared_tanh(m, c)
            expert_in(0)
            expert_tanh(0)
            expert_in(1)
            expert_out(0)
            expert_tanh(1)
            expert_in(2)
            expert_out(1)
            expert_tanh(2)
            expert_in(3)
            expert_out(2)
            expert_tanh(3)
            expert_out(3)
            shared_tanh(2, 0)
            shared_tanh(2, 1)
            shared_tanh(3, 0)
            shared_tanh(3, 1)
            attention(1)
            transposed_tiles(1, 3)

        @block.vector
        def _(dve):
            def variances(lo, hi):
                dve.tensor_scalar(VE[:, lo:hi], MV[:, lo:hi, 1], EPS, None, ALU.add).then_inc(e_var, 1)

            def normalised(layer, i, p, B):
                wait(dve, tr_mm, B - 1)
                b = i * 2 + p
                if layer == 0:
                    mean, scale = MV[:, b, 0:1], RS3[:, b, :]
                else:
                    dve.wait_ge(p_rs, B + (2 - NB))
                    mean, scale = MV_T[:, p, 0:1], RS_T[:, p, :]
                dve.tensor_scalar(XN[:, p, :], X[:, b, :], mean, scale, ALU.subtract, ALU.mult).then_inc(xn_done, 1)

            def tile_add(i, p, n):
                wait(dve, p_sum, n - 1)
                b = i * 2 + p
                dve.scalar_tensor_tensor(out=X[:, b, :], in0=YSUM[:, p, :], scalar=1.0, in1=X[:, b, :],
                                         op0=ALU.mult, op1=ALU.add).then_inc(p_x, 1)

            def before_tile_statistics(n):
                dve.wait_ge(p_x, n + 1)
                wait(dve, p_aggr, n - 1)

            def tile_statistics(i, p, n):
                dve.bn_stats(STATS_T[:, p, :], X[:, i * 2 + p, :]).then_inc(p_stat, 1)

            def before_tile_variance(n):
                dve.wait_ge(p_stat, n + 1)

            def tile_variance(p, n):
                dve.bn_aggr(MV_T[:, p, :], STATS_T[:, p, :]).then_inc(p_aggr, 1)

            def tile_variance_out(p, n):
                dve.wait_ge(p_aggr, n + 1)
                dve.tensor_scalar(VAR_T[:, p, :], MV_T[:, p, 1:2], EPS, None, ALU.add).then_inc(p_var, 1)

            def input_statistics(lo, hi):
                for n in range(lo, hi + 1):
                    if n < hi:
                        if n >= 2:
                            dve.wait_ge(mv_done, n - 1)
                        dve.bn_stats(STATS[:, n % 2, :], X[:, n, :]).then_inc(stat_done, 1)
                    if n > lo:
                        dve.wait_ge(stat_done, n)
                        dve.bn_aggr(MV[:, n - 1, :], STATS[:, (n - 1) % 2, :]).then_inc(mv_done, 1)

            dve.wait_ge(ld_x[0], 16)
            input_statistics(0, 4)
            dve.wait_ge(mv_done, 4)
            variances(0, 4)
            dve.wait_ge(e_rs, 1)
            for p in range(2):
                normalised(0, 0, p, p)
            dve.wait_ge(ld_con, 16)
            dve.tensor_scalar(negid_b[:, :], ident, -1.0, None, ALU.mult).then_inc(dve_set, 1)
            dve.tensor_copy(tri_b[:, :], CON[:, C_TRI:C_TRI + P])
            dve.tensor_scalar(off_b[:, :], ident, -float(CAP), None, ALU.mult)
            dve.tensor_copy(DIGS[:, :, :, :], CON[:, C_DIG:C_DIG + DIG].rearrange("p (g s o) -> p g s o", g=1, o=1)
                            .to_broadcast([P, NG, DIG, EG])).then_inc(dve_set, 1)
            dve.wait_ge(sel_zero, 1)
            rows = ident.rearrange("p (j g d) -> p g j d", j=J, g=G)
            for part in range(2):
                for t in range(2):
                    for which, term in ((0, 2 * t + part), (1, 2 * part + t)):
                        out_rows = SEL[:, which, part, :, :].rearrange("p g (j t d) -> p g j t d", j=J, t=4)
                        ins = dve.tensor_copy(out_rows[:, :, :, term, :], rows)
            ins.then_inc(sel_set, 1)

            def output_biases():
                dve.wait_ge(bias_mm, 1)
                dve.wait_ge(ld_b, 32)
                dve.tensor_tensor(WF[:, :], bank[3][:, 2 * D:3 * D], FWT[:, :], ALU.add).then_inc(bias_set, 1)
                dve.tensor_tensor(BR[:, 0:2 * D], bank[3][:, 0:2 * D], BR[:, 0:2 * D], ALU.add).then_inc(bias_set, 1)

            def bias_high_part():
                dve.wait_ge(bias_set, 2)
                dve.tensor_copy(BR_part[:, 0, :], BR[:, :]).then_inc(dve_set, 1)
                dve.wait_ge(dve_set, 3)
                dve.tensor_tensor(BR_rest[:, :], BR[:, :], BR_part[:, 0, :], ALU.subtract).then_inc(dve_set, 1)

            def bias_middle_part():
                dve.wait_ge(dve_set, 4)
                dve.tensor_copy(BR_part[:, 1, :], BR_rest[:, :]).then_inc(dve_set, 1)

            def bias_low_part():
                dve.wait_ge(dve_set, 5)
                dve.tensor_tensor(BR[:, :], BR_rest[:, :], BR_part[:, 1, :], ALU.subtract).then_inc(dve_set, 1)

            def bias_rows():
                dve.wait_ge(const_set, 9)
                dve.tensor_copy(B3[0:1, 0:NBO], BR_part[0:1, 0, :])
                dve.tensor_copy(B3[32:33, 0:NBO], BR_part[32:33, 1, :])
                dve.wait_ge(dve_set, 6)
                dve.tensor_copy(B3[64:65, 0:NBO], BR[64:65, :]).then_inc(bias_set, 1)

            def maxima(g, B):
                wait(dve, max_mm, B * 4 + (g + 1))
                wait(dve, score_mm, B * 4 + (g - 3))
                dve.tensor_reduce(NM[:, g, :], bank[g % 2][:, :].rearrange("p (j k) -> p j k", j=J), AXX,
                                  ALU.max).then_inc(max_got, 1)

            def low_parts(layer, B, o=7):
                wait(dve, hi_done, B + 1)
                for which in range(2):
                    ins = dve.scalar_tensor_tensor(out=HL[:, which, 1, :], in0=bank[o][:, (1 + which) * D:(2 + which) * D],
                                                   scalar=BC[:, layer, which:which + 1], in1=HL[:, which, 0, :],
                                                   op0=ALU.add, op1=ALU.subtract)
                ins.then_inc(split_done, 1)

            def q_mask(p, B):
                wait(dve, q_stacked, B + 1)
                wait(dve, score_mm, B * 4 - 4)
                for j in range(J - 1):
                    ins = dve.tensor_scalar(QM[:, p, :, j, :], QS[:, :].rearrange("p (g q) -> p g q", g=G),
                                            CON[:, C_QUAD + j:C_QUAD + j + 1], None, ALU.mult)
                ins.then_inc(q_masked, 1)

            def reciprocals(p, B):
                wait(dve, pv_mm, B * 4 + 4)
                wait(dve, ctx_done, B)
                dve.reciprocal(RD[:, :], bank[5 + p][:, D:2 * D]).then_inc(recip_done, 1)

            def normalise_context(p, B):
                wait(dve, recip_done, B + 1)
                dve.tensor_tensor(CN[:, p, :], bank[5 + p][:, 0:D], RD[:, :], ALU.mult).then_inc(ctx_done, 1)

            def residual(layer, i, p, B):
                wait(dve, o_mm, B + 1)
                b = i * 2 + p
                dve.scalar_tensor_tensor(out=X[:, b, :], in0=bank[7][:, 0:D], scalar=TH[:, layer:layer + 1],
                                         in1=X[:, b, :], op0=ALU.mult, op1=ALU.add).then_inc(x_done, 1)

            def before_statistics(layer, B):
                wait(dve, x_done, B + 1)

            def before_mean_variance(layer, B):
                wait(dve, stat_done, B + (NB + 1))
                wait(dve, mv_done, B + NB)

            def statistics(layer, i, p, B):
                dve.bn_stats(STATS[:, p, :], X[:, i * 2 + p, :]).then_inc(stat_done, 1)

            def mean_variance(layer, i, p, B):
                dve.bn_aggr(MV_now[:, :], STATS[:, p, :]).then_inc(aggr_done, 1)

            def keep_mean_variance(layer, i, p, B):
                wait(dve, aggr_done, B + 1)
                dve.tensor_copy(MV[:, i * 2 + p, :], MV_now[:, :]).then_inc(mv_done, 1)

            routing_steps = [0]

            def link(ins):
                routing_steps[0] += 1
                ins.then_inc(m_step, 1)
                dve.wait_ge(m_step, routing_steps[0])

            def next_tiles(layer, m):
                dve.wait_ge(e_rs, 3 * layer + max(m - 2, 0) + 3)
                for t in range(4 * m, 4 * m + 4) if m < 3 else range(12, NB - 1) if m == 3 else range(NB - 1, NB):
                    ins = dve.tensor_scalar(TB[:, t, 0:D], X[:, t, :], MV[:, t, 0:1], RS[:, t:t + 1],
                                            ALU.subtract, ALU.mult)
                ins.then_inc(e_xn, 1)

            def best(m):
                c = slice(4 * m, 4 * m + 4)
                dve.wait_ge(m_lgc, m + 1)
                for t in range(4 * m, 4 * m + 4):
                    ins = dve.max(TOP[:, t, :], LG[:, t, :])
                link(ins)
                for t in range(4 * m, 4 * m + 4):
                    ins = dve.match_replace(POS[:, t, :], TOP[:, t, :], LG[:, t, :], -3.0e38)
                dve.tensor_scalar(NTOP[:, c], TOP[:, c, 0], -1.0, None, ALU.mult).then_inc(m_top, 1)
                dve.wait_ge(m_top, m + 1)
                dve.tensor_tensor(MASK[:, c, :], POS[:, c, :], LG[:, c, :], ALU.not_equal).then_inc(m_mask, 1)

            def last_out(m):
                dve.wait_ge(f_mm, m + 1)
                dve.scalar_tensor_tensor(out=OT[:, m, :, :].rearrange("p n d -> p (n d)"), in0=bank[m][:, :],
                                         scalar=TH[:, 3:4], in1=X[:, 4 * m:4 * m + 4, :].rearrange("p n d -> p (n d)"),
                                         op0=ALU.mult, op1=ALU.add).then_inc(f_x, 1)

            def attention(layer):
                B0 = NB * layer
                def first_sum(n):
                    dve.wait_ge(p_in[n], 16)
                    dve.tensor_reduce(YSUM[:, n, :], PART[:, n, :].rearrange("p (k d) -> p d k", k=TOPK), AXX,
                                      ALU.add).then_inc(p_first, 1)
                    dve.wait_ge(p_first, n + 1)

                def first_tile(n):
                    tile_add(n // 2, n % 2, n)
                    before_tile_statistics(n)
                    tile_statistics(n // 2, n % 2, n)
                    before_tile_variance(n)
                    wait(dve, xn_done, n + (NB - 1))
                    tile_variance(n % 2, n)
                    tile_variance_out(n % 2, n)

                if layer > 0:
                    first_sum(0)
                    first_tile(0)
                    normalised(1, 0, 0, B0)
                    first_sum(1)
                    first_tile(1)
                    normalised(1, 0, 1, B0 + 1)
                low_parts(layer, B0)
                q_mask(0, B0)
                low_parts(layer, B0 + 1, 6)
                if layer == 0:
                    output_biases()
                    bias_high_part()
                else:
                    first_tile(2)
                maxima(0, B0)
                maxima(1, B0)

                def step(i, p, B, last):
                    q = 1 - p
                    end = last and p == 1
                    first = isinstance(i, int) and i == 0
                    one_back = i - 1 if p == 0 else i
                    alone = first and p == 0
                    arriving = layer == 1 and not last and not (isinstance(i, int) and B + 3 >= 2 * NB)
                    ni, n = i + 1 + p, B + (3 - NB)
                    for g in range(G):
                        if g == 2 and arriving and alone:
                            before_tile_statistics(n)
                        if g == 3 and arriving:
                            before_tile_variance(n)
                        if g == 0 and not last and (layer == 0 or p == 0):
                            normalised(layer, i + 1, p, B + 2)
                        if g < 2:
                            maxima(g + 2, B)
                        elif not end:
                            maxima(g - 2, B + 1)
                        if g == 0:
                            if not last and layer == 1 and p == 1:
                                normalised(layer, i + 1, p, B + 2)
                            if not first:
                                before_statistics(layer, B - 2)
                            if not end:
                                q_mask(q, B + 1)
                            if not first:
                                statistics(layer, i - 1, p, B - 2)
                        if g == 1:
                            if not first:
                                before_mean_variance(layer, B - 2)
                            if arriving:
                                tile_add(ni, q, n)
                            if not alone:
                                reciprocals(q, B - 1)
                            if not first:
                                mean_variance(layer, i - 1, p, B - 2)
                            if not alone:
                                normalise_context(q, B - 1)
                            if not first:
                                keep_mean_variance(layer, i - 1, p, B - 2)
                        if g == 2:
                            if not last:
                                low_parts(layer, B + 2)
                            if arriving:
                                tile_statistics(ni, q, n)
                        if g == 3:
                            if arriving:
                                tile_variance(q, n)
                            if not alone:
                                residual(layer, one_back, q, B - 1)
                            if arriving:
                                tile_variance_out(q, n)
                        if last and p == 0 and g == 0:
                            dve.wait_ge(mv_done, NB * (layer + 1) + 12)
                            variances(0, 12)
                        if last and p == 0 and g >= 2:
                            next_tiles(layer, g - 2)
                        if end and g == 0:
                            next_tiles(layer, 2)
                        if layer == 0 and alone:
                            if g < 3:
                                dve.wait_ge(ld_x[g + 1], 16)
                                input_statistics(4 * g + 4, 4 * g + 8)
                            else:
                                bias_middle_part()
                        elif layer == 0 and first:
                            if g == 0:
                                dve.wait_ge(mv_done, NB)
                                variances(4, NB)
                                bias_low_part()
                            elif g == 1:
                                bias_rows()
                            elif g == 3:
                                dve.wait_ge(e_rs, 2)

                over_batches(dve, layer, step, peeled=layer + 1)
                n = NB // 2 - 1
                B1 = B0 + NB - 1
                reciprocals(1, B1)
                normalise_context(1, B1)
                for p in range(2):
                    if p == 1:
                        residual(layer, n, p, B1 - 1 + p)
                    before_statistics(layer, B1 - 1 + p)
                    statistics(layer, n, p, B1 - 1 + p)
                    before_mean_variance(layer, B1 - 1 + p)
                    mean_variance(layer, n, p, B1 - 1 + p)
                    keep_mean_variance(layer, n, p, B1 - 1 + p)
                    dve.wait_ge(mv_done, NB * (layer + 2) - 1 + p)
                    if p == 0:
                        variances(12, NB - 1)
                    else:
                        variances(NB - 1, NB)
                    if p == 0 and layer == 1:
                        last_out(0)
                if layer == 0:
                    for m in range(2):
                        best(m)
                    next_tiles(layer, 3)
                    next_tiles(layer, 4)
                else:
                    for m in (3, 4):
                        next_tiles(layer, m)
                    last_out(1)

            attention(0)

            best(2)

            flat = "p n e -> p (n e)"

            def slots(h):
                c = slice(8 * h, 8 * h + 8)
                dve.wait_ge(m_pos, h + 1)
                dve.tensor_scalar(SLOT[:, c, :].rearrange(flat), bank[6 + h][:, :], float(CAP), None,
                                  ALU.add).then_inc(m_slot, 1)
                dve.wait_ge(m_slot, h + 1)
                dve.tensor_scalar(LOW[:, c, :], SLOT[:, c, :], DIG - 1, None, ALU.bitwise_and)
                link(dve.tensor_scalar(HI[:, c, :], SLOT[:, c, :], 3, None, ALU.logical_shift_right))

            def one_hots(t):
                for w, digit in ((0, HI), (1, LOW)):
                    of_tile = digit[:, t, :].rearrange("p (g o e) -> p g o e", g=NG, o=1)
                    ins = dve.tensor_tensor(HOT[:, w, t, :, :, :], of_tile.to_broadcast([P, NG, DIG, EG]),
                                            DIGS[:, :, :, :], ALU.is_equal)
                ins.then_inc(m_raw, 1)

            slots(0)
            for t in range(4):
                one_hots(t)
            best(3)
            for t in range(4, 8):
                one_hots(t)
            dve.wait_ge(m_mask, 4)
            dve.tensor_tensor_scan(COUNT[:, :, :].rearrange(flat), MASK[:, :, :].rearrange(flat),
                                   MASK[:, :, :].rearrange(flat), 0.0, ALU.add, ALU.bypass).then_inc(m_scan, 1)
            dve.wait_ge(m_less, 1)
            dve.tensor_tensor(TOPX[:, :, :], TOP[:, :, :], TOP[:, :, 0:1].to_broadcast([P, NB, TOPK]),
                              ALU.subtract).then_inc(m_less, 1)
            slots(1)
            for t in range(8, NB):
                one_hots(t)
                if t == 9:
                    dve.wait_ge(m_less, 3)
                    link(dve.tensor_reduce(SUMS[:, :], TOPX[:, :, :], AXX, ALU.add))
                    link(dve.reciprocal(SUMS[:, :], SUMS[:, :]))
                    dve.tensor_scalar(SUMS[:, :], SUMS[:, :], TH[:, 2:3], 0.5, ALU.mult, ALU.mult).then_inc(m_inv, 1)
            dve.wait_ge(m_ids, 1)
            own = CON[:, C_OWN:C_OWN + EG]
            link(dve.tensor_tensor(IDX[:, :, :, :], bank[5][:, :].rearrange("p (g s e) -> p g s e", g=NG, s=DIG),
                                   own.rearrange("p (o u e) -> p o u e", o=1, u=1).to_broadcast([P, NG, DIG, EG]), ALU.mult))
            link(dve.tensor_reduce(IDF[:, :].rearrange("p (g s) -> p g s", g=NG), IDX[:, :, :, :], AXX, ALU.add))
            dve.tensor_copy(IDI[:, :], IDF[:, :]).then_inc(m_idx, 1)
            link(dve.tensor_scalar(SG[:, :], SG[:, :], 0.25, 0.25, ALU.mult, ALU.add))

            def shared_hidden(m, c):
                dve.wait_ge(h_tanh, 2 * m + c + 1)
                dve.wait_ge(h_mm, 4 * m + 2 * c + 2)
                wait(dve, h_dn, m)
                dve.scalar_tensor_tensor(out=HS[:, c, :], in0=TS_[:, c, :], scalar=1.0, in1=bank[4 * c][:, :],
                                         op0=ALU.add, op1=ALU.mult).then_inc(h_h1, 1)
                dve.wait_ge(h_h1, 2 * m + c + 1)
                dve.tensor_tensor(HS[:, c, :], HS[:, c, :], bank[4 * c + 1][:, :], ALU.mult).then_inc(h_act, 1)

            def shared_out(m):
                dve.wait_ge(h_dn, m + 1)
                wait(dve, h_x, m)
                dve.tensor_tensor(SH[:, :, :], bank[4][:, :].rearrange("p (n d) -> p n d", n=4),
                                  SG[:, 4 * m:4 * m + 4].rearrange("p (n o) -> p n o", o=1).to_broadcast([P, 4, D]),
                                  ALU.mult).then_inc(h_sh, 1)
                dve.wait_ge(h_sh, m + 1)
                dve.scalar_tensor_tensor(out=X[:, 4 * m:4 * m + 4, :], in0=SH[:, :, :], scalar=TH[:, 2:3],
                                         in1=X[:, 4 * m:4 * m + 4, :], op0=ALU.mult, op1=ALU.add).then_inc(h_x, 1)

            def slot_data(g):
                dve.wait_ge(g_in[g], 16 * DIG)
                mine = GA[:, g * DIG:(g + 1) * DIG, D:ROW].rearrange("p s (w e) -> p s w e", w=2)[:, :, :, EG * g:EG * g + EG]
                link(dve.tensor_tensor(OWNP[:, :, :, :], mine,
                                       own.rearrange("p (o u e) -> p o u e", o=1, u=1).to_broadcast([P, DIG, 2, EG]), ALU.mult))
                link(dve.tensor_reduce(WD[:, g * DIG:(g + 1) * DIG, :], OWNP[:, :, :, :], AXX, ALU.add))
                dve.tensor_copy(DST[:, g * DIG:(g + 1) * DIG], WD[:, g * DIG:(g + 1) * DIG, 1]).then_inc(g_wd, 1)

            def expert_hidden(g):
                dve.wait_ge(g_tanh, g + 1)
                dve.scalar_tensor_tensor(out=H1[:, :], in0=TG[:, :], scalar=1.0, in1=bank[2][:, :],
                                         op0=ALU.add, op1=ALU.mult).then_inc(g_h1, 1)
                dve.wait_ge(g_h1, g + 1)
                wait(dve, g_dn, g)
                for u in range(2):
                    r = slice(64 * u, 64 * u + 64)
                    ins = dve.tensor_tensor(AH[r, :, u, :], H1[r, :].rearrange("p (k n) -> p k n", k=EG // 2),
                                            bank[3][r, :].rearrange("p (k n) -> p k n", k=EG // 2), ALU.mult)
                ins.then_inc(g_act, 1)

            def weighted_outputs(g):
                for h in range(2):
                    dve.wait_ge(g_bk, 2 * g + h + 1)
                    c = g * DIG + 4 * h
                    dve.tensor_tensor(YS[:, c:c + 4, :], bank[6 + h][:, :].rearrange("p (s d) -> p s d", s=4),
                                      WD[:, c:c + 4, 0:1].to_broadcast([P, 4, D]), ALU.mult).then_inc(g_ys, 1)

            shared_hidden(0, 0)
            shared_hidden(0, 1)
            shared_hidden(1, 0)
            shared_out(0)
            shared_hidden(1, 1)
            shared_out(1)
            slot_data(0)
            expert_hidden(0)
            slot_data(1)
            expert_hidden(1)
            weighted_outputs(0)
            slot_data(2)
            expert_hidden(2)
            weighted_outputs(1)
            slot_data(3)
            expert_hidden(3)
            weighted_outputs(2)
            weighted_outputs(3)
            shared_hidden(2, 0)
            shared_hidden(2, 1)
            shared_out(2)
            shared_hidden(3, 0)
            shared_hidden(3, 1)
            shared_out(3)
            attention(1)

            last_out(2)
            last_out(3)


def kernel(x, ctx_1024, g_xattn, g_ffn, L0_xattn_w_q, L0_xattn_b_q, L0_xattn_w_k, L0_xattn_b_k, L0_xattn_w_v,
           L0_xattn_b_v, L0_xattn_w_o, L0_xattn_b_o, L0_ffn_gate_w, L0_ffn_shared_gate_w, L0_ffn_shared_gate_up_w,
           L0_ffn_shared_down_w, L0_ffn_expert_gate_up_w, L0_ffn_expert_down_w, L1_xattn_Wq, L1_xattn_bq,
           L1_xattn_Wk, L1_xattn_bk, L1_xattn_Wv, L1_xattn_bv, L1_xattn_Wo, L1_xattn_bo, L1_ffn_W, L1_ffn_b,
           L1_ffn_V_r, L1_ffn_C):
    import concourse.bacc as bacc
    from concourse.bass_utils import run_bass_kernel_spmd

    a = np.asarray
    layers = [(a(L0_xattn_w_q), a(L0_xattn_w_k), a(L0_xattn_w_v), a(L0_xattn_w_o), a(L0_xattn_b_q), a(L0_xattn_b_k),
               a(L0_xattn_b_v), a(L0_xattn_b_o)),
              (a(L1_xattn_Wq).T, a(L1_xattn_Wk).T, a(L1_xattn_Wv).T, a(L1_xattn_Wo).T, a(L1_xattn_bq), a(L1_xattn_bk),
               a(L1_xattn_bv), a(L1_xattn_bo))]
    data = {
        "x": a(x).reshape(T, D),
        "ctx": a(ctx_1024).reshape(T, D),
        "consts": shape_constants(),
        "wqkvo": np.stack([np.stack(w[0:4], 1) for w in layers], 1),
        "bcol": np.stack([np.stack(w[4:7], 1) for w in layers], 1),
        "brow": np.concatenate([layers[0][7], layers[1][7], a(L1_ffn_b)]),
        "gates": np.concatenate([a(g_xattn), a(g_ffn)]),
        "gate_w": np.concatenate([a(L0_ffn_gate_w), a(L0_ffn_shared_gate_w)], 1),
        "sgu": a(L0_ffn_shared_gate_up_w),
        "sdown": a(L0_ffn_shared_down_w),
        "egu": a(L0_ffn_expert_gate_up_w),
        "edown": a(L0_ffn_expert_down_w),
        "ffn_wt": a(L1_ffn_W).T,
        "ffn_vt": a(L1_ffn_V_r).T,
        "ffn_ct": a(L1_ffn_C).T,
    }
    nc = bacc.Bacc("TRN2", target_bir_lowering=False, num_devices=1)
    arrays, aps = {}, {}
    for name, v in data.items():
        v = np.ascontiguousarray(v)
        arrays[f"in_{name}"] = v
        aps[name] = nc.dram_tensor(f"in_{name}", v.shape, mybir.dt.from_np(v.dtype), kind="ExternalInput").ap()
    out = nc.dram_tensor("out_0", (T, D), F32, kind="ExternalOutput").ap()
    program(nc, out=out, **aps)
    r = run_bass_kernel_spmd(nc, [arrays], core_ids=[0])
    return r.results[0]["out_0"].reshape(NB, P, D)
```
